# Optimizing a Trainium2 kernel written in Bass

```python
import numpy as np
import jax
import jax.numpy as jnp

def _softmax(x, axis=-1):
    return jax.nn.softmax(x, axis=axis)

def _gelu(x):
    return jax.nn.gelu(x, approximate=True)

def _silu(x):
    return jax.nn.silu(x)

def _sigmoid(x):
    return jax.nn.sigmoid(x)

def _layernorm(x, axis=-1, eps=1e-05):
    m = jnp.mean(x, axis=axis, keepdims=True)
    v = jnp.var(x, axis=axis, keepdims=True)
    return (x - m) / jnp.sqrt(v + eps)

def _scatter_add(tgt, idx, src, axis=0):
    return tgt.at[idx].add(src)

def _segment_sum(src, seg, n):
    return jax.ops.segment_sum(src, seg, n)
kernel_name = 'mk_decoder_preln_d1_seqx_r4_a7534c'

def setup_inputs(seed: int=0):
    np.random.seed(seed)
    _w = jnp.asarray

    def _rec_inputs():
        import jax
        import jax.numpy as jnp
        _rk = jax.random.key(seed)
        x = -0.0002928 + 1 * jax.random.normal(jax.random.fold_in(_rk, 1), (16, 256, 512), jnp.float32)
        _lenS = 256 - jax.random.randint(jax.random.fold_in(_rk, 7), (16,), 0, max(1, 256 // 4) + 1, jnp.int32)
        _lenS2 = 256 - jax.random.randint(jax.random.fold_in(_rk, 8), (16,), 0, max(1, 256 // 4) + 1, jnp.int32)
        _ctx_2048P = jax.random.normal(jax.random.fold_in(_rk, 11), (16, 16, 512), jnp.float32)
        _ctx_2048c = jax.random.dirichlet(jax.random.fold_in(_rk, 511), 0.3 * jnp.ones((16,), jnp.float32), (16, 256))
        _ctx_2048t = jnp.einsum('bsk,bkd->bsd', _ctx_2048c, _ctx_2048P)
        _ctx_2048t = _ctx_2048t * jax.lax.rsqrt(jnp.mean(jnp.square(_ctx_2048t)) + 1e-12) * 0.953939
        ctx_2048 = -1.39393e-06 + 0.999914 * (_ctx_2048t + 0.3 * jax.random.normal(jax.random.fold_in(_rk, 611), (16, 256, 512), jnp.float32))
        _validS = jnp.arange(256)[None, :] < _lenS[:, None]
        _validS2 = jnp.arange(256)[None, :] < _lenS2[:, None]
        _causal = jnp.tril(jnp.ones((256, 256), dtype=bool))
        mask_Bx1x2048_fk1 = jnp.where(jnp.ones((16, 1, 512), dtype=bool), 1.0, 0.0).astype(jnp.float32)
        return (x, ctx_2048, mask_Bx1x2048_fk1)
    x, ctx_2048, mask_Bx1x2048_fk1 = _rec_inputs()

    def _L0_attn_setup():
        import jax, jax.numpy as jnp
        import numpy as np
        B, SQ, HIDDEN = (2, 512, 512)
        HEADS, GROUPS, KVC = (16, 4, 128)
        HPG = HEADS // GROUPS
        LAYER_INDEX = 1
        SCALE = KVC ** (-0.5)
        key = jax.random.key(seed)
        k1, k2, k3, k4 = jax.random.split(key, 4)
        return {'x': jax.random.normal(k1, (B, SQ, HIDDEN), jnp.float32), 'w_q': jax.random.normal(k2, (HIDDEN, HEADS * KVC), jnp.float32) * 0.02, 'w_kv': jax.random.normal(k3, (HIDDEN, 2 * GROUPS * KVC), jnp.float32) * 0.02, 'w_dense': jax.random.normal(k4, (HEADS * KVC, HIDDEN), jnp.float32) * 0.02}
    _L0_attn_all = _L0_attn_setup()
    _L0_attn_in = {k: v for k, v in _L0_attn_all.items() if k in ('w_q', 'w_kv', 'w_dense')}
    del _L0_attn_all

    def _L0_xattn_setup():
        import math
        import jax, jax.numpy as jnp
        import numpy as np
        SIZE = 256
        HEADS = 16
        HEAD_DIM = SIZE // HEADS
        B, T, S = (2, 512, 512)
        NEG = 1000000.0
        key = jax.random.key(seed)
        ks = jax.random.split(key, 10)
        target = jax.random.normal(ks[0], (B, SIZE, T), dtype=jnp.float32)
        source = jax.random.normal(ks[1], (B, SIZE, S), dtype=jnp.float32)
        target_mask = (jax.random.uniform(ks[2], (B, 1, T)) > 0.1).astype(jnp.float32)
        source_mask = (jax.random.uniform(ks[3], (B, 1, S)) > 0.1).astype(jnp.float32)
        scale = 1.0 / math.sqrt(SIZE)
        Wq = jax.random.normal(ks[4], (SIZE, SIZE), dtype=jnp.float32) * scale
        Wk = jax.random.normal(ks[5], (SIZE, SIZE), dtype=jnp.float32) * scale
        Wv = jax.random.normal(ks[6], (SIZE, SIZE), dtype=jnp.float32) * scale
        bq = jax.random.normal(ks[7], (SIZE,), dtype=jnp.float32) * 0.01
        bk = jax.random.normal(ks[8], (SIZE,), dtype=jnp.float32) * 0.01
        bv = jax.random.normal(ks[9], (SIZE,), dtype=jnp.float32) * 0.01
        return {'target': target, 'source': source, 'target_mask': target_mask, 'source_mask': source_mask, 'Wq': Wq, 'bq': bq, 'Wk': Wk, 'bk': bk, 'Wv': Wv, 'bv': bv}
    _L0_xattn_all = _L0_xattn_setup()
    _L0_xattn_in = {k: v for k, v in _L0_xattn_all.items() if k in ('Wq', 'bq', 'Wk', 'bk', 'Wv', 'bv')}
    del _L0_xattn_all

    def _L0_ffn_setup():
        import jax, jax.numpy as jnp
        import numpy as np
        B, S, H = (2, 512, 512)
        FFN = 256
        E = 8
        TOP_K = 2
        key = jax.random.key(seed)
        ks = jax.random.split(key, 5)
        scale = 0.02
        hidden_states = jax.random.normal(ks[0], (B, S, H), dtype=jnp.float32)
        Wg = jax.random.normal(ks[1], (E, H), dtype=jnp.float32) * scale
        W1 = jax.random.normal(ks[2], (E, FFN, H), dtype=jnp.float32) * scale
        W3 = jax.random.normal(ks[3], (E, FFN, H), dtype=jnp.float32) * scale
        W2 = jax.random.normal(ks[4], (E, H, FFN), dtype=jnp.float32) * scale
        bias = jnp.zeros((E,), dtype=jnp.float32)
        return {'hidden_states': hidden_states, 'Wg': Wg, 'W1': W1, 'W2': W2, 'W3': W3, 'bias': bias}
    _L0_ffn_all = _L0_ffn_setup()
    _L0_ffn_in = {k: v for k, v in _L0_ffn_all.items() if k in ('Wg', 'W1', 'W2', 'W3', 'bias')}
    del _L0_ffn_all
    return {'x': x, 'ctx_2048': ctx_2048, 'mask_Bx1x2048_fk1': mask_Bx1x2048_fk1, 'L0_attn_w_q': _L0_attn_in['w_q'], 'L0_attn_w_kv': _L0_attn_in['w_kv'], 'L0_attn_w_dense': _L0_attn_in['w_dense'], 'L0_xattn_Wq': _L0_xattn_in['Wq'], 'L0_xattn_bq': _L0_xattn_in['bq'], 'L0_xattn_Wk': _L0_xattn_in['Wk'], 'L0_xattn_bk': _L0_xattn_in['bk'], 'L0_xattn_Wv': _L0_xattn_in['Wv'], 'L0_xattn_bv': _L0_xattn_in['bv'], 'L0_ffn_Wg': _L0_ffn_in['Wg'], 'L0_ffn_W1': _L0_ffn_in['W1'], 'L0_ffn_W2': _L0_ffn_in['W2'], 'L0_ffn_W3': _L0_ffn_in['W3'], 'L0_ffn_bias': _L0_ffn_in['bias']}

def reference(x, ctx_2048, mask_Bx1x2048_fk1, L0_attn_w_q, L0_attn_w_kv, L0_attn_w_dense, L0_xattn_Wq, L0_xattn_bq, L0_xattn_Wk, L0_xattn_bk, L0_xattn_Wv, L0_xattn_bv, L0_ffn_Wg, L0_ffn_W1, L0_ffn_W2, L0_ffn_W3, L0_ffn_bias):
    import jax
    import jax.numpy as jnp

    def _L0_attn_ref(x, w_q, w_kv, w_dense):
        import jax, jax.numpy as jnp
        import numpy as np
        B, SQ, HIDDEN = (2, 512, 512)
        HEADS, GROUPS, KVC = (16, 4, 128)
        HPG = HEADS // GROUPS
        LAYER_INDEX = 1
        SCALE = KVC ** (-0.5)
        b, sq, _ = x.shape
        sk = sq
        q = jnp.einsum('bsh,he->bse', x, w_q).reshape(b, sq, GROUPS, HPG, KVC)
        kv = jnp.einsum('bsh,he->bse', x, w_kv)
        k, v = jnp.split(kv, 2, axis=-1)
        k = k.reshape(b, sk, GROUPS, KVC)
        v = v.reshape(b, sk, GROUPS, KVC)
        scores = jnp.einsum('bqgpd,bkgd->bgqpk', q, k) * (SCALE / LAYER_INDEX)
        scores = scores.astype(jnp.float32) * LAYER_INDEX
        causal = jnp.arange(sq)[:, None] >= jnp.arange(sk)[None, :]
        scores = jnp.where(causal[None, None, :, None, :], scores, -jnp.inf)
        probs = jax.nn.softmax(scores, axis=-1).astype(x.dtype)
        ctx = jnp.einsum('bgqpk,bkgd->bqgpd', probs, v).reshape(b, sq, HEADS * KVC)
        return jnp.einsum('bse,eh->bsh', ctx, w_dense)

    def _L0_xattn_ref(target, source, target_mask, source_mask, Wq, bq, Wk, bk, Wv, bv):
        import math
        import jax, jax.numpy as jnp
        import numpy as np
        SIZE = 256
        HEADS = 16
        HEAD_DIM = SIZE // HEADS
        B, T, S = (2, 512, 512)
        NEG = 1000000.0
        b, _, t = target.shape
        s = source.shape[-1]
        q = jnp.einsum('oc,bct->bot', Wq, target) + bq[None, :, None]
        k = jnp.einsum('oc,bcs->bos', Wk, source) + bk[None, :, None]
        v = jnp.einsum('oc,bcs->bos', Wv, source) + bv[None, :, None]
        q = q.reshape(b, HEADS, HEAD_DIM, t)
        k = k.reshape(b, HEADS, HEAD_DIM, s)
        v = v.reshape(b, HEADS, HEAD_DIM, s)
        dot = jnp.einsum('bhdt,bhds->bhts', q, k) / math.sqrt(HEAD_DIM)
        mask = target_mask[:, :, :, None] * source_mask[:, :, None, :]
        dot = mask * dot - (1.0 - mask) * NEG
        amap = jax.nn.softmax(dot, axis=-1) * mask
        out = jnp.einsum('bhts,bhds->bhdt', amap, v)
        return out.reshape(b, HEADS * HEAD_DIM, t)

    def _L0_ffn_ref(hidden_states, Wg, W1, W2, W3, bias):
        import jax, jax.numpy as jnp
        import numpy as np
        B, S, H = (2, 512, 512)
        FFN = 256
        E = 8
        TOP_K = 2
        bsz, seq_len, hidden_dim = hidden_states.shape
        x = hidden_states.reshape(-1, hidden_dim)
        router_logits = x @ Wg.T
        routing_weights = jax.nn.sigmoid(router_logits.astype(jnp.float32))
        scores = routing_weights + bias
        _, top_k_index = jax.lax.top_k(scores, TOP_K)
        top_k_weights = jnp.take_along_axis(routing_weights, top_k_index, axis=1)
        top_k_weights = top_k_weights / top_k_weights.sum(axis=-1, keepdims=True)
        top_k_weights = top_k_weights.astype(x.dtype)
        one_hot = jax.nn.one_hot(top_k_index, Wg.shape[0], dtype=x.dtype)
        expert_w = jnp.einsum('tk,tke->te', top_k_weights, one_hot)
        h1 = jnp.einsum('th,efh->tef', x, W1)
        h3 = jnp.einsum('th,efh->tef', x, W3)
        g = jax.nn.silu(h1) * h3 * expert_w[:, :, None]
        out = jnp.einsum('tef,ehf->th', g, W2)
        return out.reshape(bsz, seq_len, hidden_dim)
    x = x + _L0_attn_ref(_layernorm(x, axis=-1), L0_attn_w_q, L0_attn_w_kv, L0_attn_w_dense)
    x = x + _L0_xattn_ref(_layernorm(x, axis=-1), ctx_2048, mask_Bx1x2048_fk1, mask_Bx1x2048_fk1, L0_xattn_Wq, L0_xattn_bq, L0_xattn_Wk, L0_xattn_bk, L0_xattn_Wv, L0_xattn_bv)
    x = x + _L0_ffn_ref(_layernorm(x, axis=-1), L0_ffn_Wg, L0_ffn_W1, L0_ffn_W2, L0_ffn_W3, L0_ffn_bias)
    return x

_drawn_inputs = setup_inputs


def setup_inputs(seed=0):
    import zlib

    import numpy as np

    out = dict(_drawn_inputs(seed))
    spreads = {'L0_ffn_bias': (0.0, 0.668)}
    factors = {'L0_attn_w_q': 8.0,
     'L0_xattn_bv': 5.805,
     'L0_ffn_Wg': 6.481,
     'L0_ffn_W1': 4.689,
     'L0_ffn_W2': 4.584,
     'L0_ffn_W3': 4.587}
    for name, (base, spread) in spreads.items():
        noise = np.random.default_rng([zlib.crc32(name.encode()), seed]).standard_normal(out[name].shape)
        drawn = base * np.exp(spread * noise) if base else spread * noise
        out[name] = jnp.asarray(drawn.astype(out[name].dtype))
    for name, factor in factors.items():
        out[name] = (out[name] * factor).astype(out[name].dtype)
    return out
```

```python
from contextlib import ExitStack

import concourse.bass as bass
from concourse import mybir

F32 = mybir.dt.float32
F32R = mybir.dt.float32r
BF16 = mybir.dt.bfloat16
ACT = mybir.ActivationFunctionType
ALU = mybir.AluOpType
AX = mybir.AxisListType

P = 128
BANK = 512
LN_EPS = 1e-5


def wait_alone(eng, sem, value, past):
    if not isinstance(value, int):
        value = eng.to_reg(value)
    eng.wait_ge(*past)
    eng.wait_ge(sem, value)


def attention_phase(nc, x_rows, w_q, w_kv, w_dense, x1_rows, TOKENS, HIDDEN, SEQ, HEADS, GROUPS):
    D = P
    HALVES = 2
    G = GROUPS // HALVES
    HPG = HEADS // GROUPS
    NH = G * HPG
    TB = BANK // P
    KT = HIDDEN // P
    PAIRS = TOKENS // BANK
    UNITS = 2 * NH
    SCALE = float(D) ** -0.5
    FILLS = 16
    assert SEQ == 2 * P and FILLS == KT + G + TB // 2 + NH
    QW, KVW = NH * D, 2 * G * D
    NEG = -1.0e30

    with ExitStack() as ctx:
        def sb(name, shape, dt=F32):
            return ctx.enter_context(nc.sbuf_tensor(name, shape, dt))

        def psum(name, shape):
            return ctx.enter_context(nc.psum_tensor(name, shape, F32))

        def sem(name):
            return ctx.enter_context(nc.semaphore("a_" + name))

        wq = [sb(f"wq_{s}", [P, KT, QW], F32R) for s in "hl"]
        wkv = [sb(f"wkv_{s}", [P, KT, KVW], F32R) for s in "hl"]
        wd = [sb(f"wd_{s}", [P, NH, HIDDEN], F32R) for s in "hl"]
        x_in = sb("x_in", [P, TB, HIDDEN])
        acc = sb("acc", [P, TB, HIDDEN])
        xn = sb("xn", [P, TB, HIDDEN])
        xT = [sb(f"xT_{s}", [P, KT, BANK], F32R) for s in "hl"]
        kT = [sb(f"kT_{s}", [P, G, BANK], F32R) for s in "hl"]
        v = [sb(f"v_{s}", [P, TB, G * D], F32R) for s in "hl"]
        qT = [sb(f"qT_{s}", [P, 2, BANK], F32R) for s in "hl"]
        probs = sb("probs", [P, 2, 3 * P])
        pT = [sb(f"pT_{s}", [P, 2, 3 * P], F32R) for s in "hl"]
        cT = [sb(f"cT_{s}", [P, G, HPG, BANK], F32R) for s in "hl"]
        ident = sb("ident", [P, P])
        ident_b = sb("ident_b", [P, P], BF16)
        causal = sb("causal", [P, P], BF16)
        stats = sb("stats", [P, TB, 6])
        mv = sb("mv", [P, TB, 2])
        veps = sb("veps", [P, TB])
        rstd = sb("rstd", [P, TB])
        minus_half = sb("minus_half", [P, TB])
        negmax = sb("negmax", [P, 2, 2])
        rowsum = sb("rowsum", [P, 2, 2])
        rinv = sb("rinv", [P, 2, 2])

        ps_proj = [psum(f"ps_proj{i}", [P, BANK]) for i in range(2)]
        ps_s = [psum(f"ps_s{i}", [P, BANK]) for i in range(2)]
        ps_pT = [psum(f"ps_pT{i}", [P, BANK]) for i in range(2)]
        ps_c = psum("ps_c", [P, BANK])
        ps_d = psum("ps_d", [P, BANK])

        consts = sem("consts")
        w_loaded = [sem("w_loaded0"), sem("w_loaded1")]
        w_high = sem("w_high")
        w_low = sem("w_low")
        x_loaded = sem("x_loaded")
        acc_loaded = sem("acc_loaded")
        stored = sem("stored")
        stats_done = sem("stats_done")
        aggr_done = sem("aggr_done")
        veps_done = sem("veps_done")
        rstd_done = sem("rstd_done")
        xn_done = sem("xn_done")
        proj_filled = sem("proj_filled")
        proj_high = sem("proj_high")
        proj_low = sem("proj_low")
        s_filled = sem("s_filled")
        max_done = sem("max_done")
        exp_done = sem("exp_done")
        rinv_done = sem("rinv_done")
        probs_done = sem("probs_done")
        pT_filled = sem("pT_filled")
        pT_high = sem("pT_high")
        pT_low = sem("pT_low")
        c_filled = sem("c_filled")
        c_high = sem("c_high")
        c_low = sem("c_low")
        d_filled = sem("d_filled")
        d_added = sem("d_added")

        def tokens(rows, pair):
            return rows[pair].rearrange("(n p) h -> p n h", p=P)

        CH = TB * HIDDEN

        def chunks(half):
            out = []
            for kt0 in range(0, KT, CH // QW):
                out.append(([w[:, kt0:kt0 + CH // QW, :] for w in wq],
                            w_q[kt0 * P:(kt0 + CH // QW) * P, half * QW:(half + 1) * QW]
                            .rearrange("(k p) e -> p k e", p=P)))
            for part in range(2):
                out.append(([w[:, :, part * G * D:(part + 1) * G * D] for w in wkv],
                            w_kv[:, (part * GROUPS + half * G) * D:(part * GROUPS + half * G + G) * D]
                            .rearrange("(k p) e -> p k e", p=P)))
            for h0 in range(0, NH, TB):
                r0 = (half * NH + h0) * D
                out.append(([w[:, h0:h0 + TB, :] for w in wd],
                            w_dense[r0:r0 + TB * D, :].rearrange("(k p) e -> p k e", p=P)))
            return out

        NCH = len(chunks(0))
        stage = [x_in, xn]

        def staged(n, like):
            flat = stage[n % 2][:, :, :].rearrange("p n h -> p (n h)")
            k, e = like.shape[1], like.shape[2]
            return flat[:, 0:k * e].rearrange("p (k e) -> p k e", k=k)

        def pairs(eng, half, body):
            with eng.Fori(half * PAIRS, (half + 1) * PAIRS - 1) as t:
                body(t, False)
            body((half + 1) * PAIRS - 1, True)

        with nc.Block() as block:
            @block.sync
            def _(sp):
                sp.sem_inc(stored, 16)
                for half in range(HALVES):
                    x_base = half * PAIRS
                    for n, ((high, _low), src) in enumerate(chunks(half)):
                        N = half * NCH + n
                        if n >= 2:
                            sp.wait_ge(w_low, N - 1)
                        elif half:
                            sp.wait_ge(proj_low, FILLS * PAIRS)
                            sp.wait_ge(xn_done, half * PAIRS)
                        sp.dma_start(staged(n, high), src).then_inc(w_loaded[n % 2], 16)
                    sp.wait_ge(w_low, (half + 1) * NCH)
                    sp.dma_start(x_in[:], tokens(x_rows, 0)).then_inc(x_loaded, 16)

                    def body(t, last):
                        if not last:
                            wait_alone(sp, xn_done, t + 1, (consts, 6))
                            sp.dma_start(x_in[:], tokens(x_rows, t + 1 - x_base)).then_inc(x_loaded, 16)
                        wait_alone(sp, stored, 16 * (t + 1), (consts, 6))
                        rows = x_rows if half == 0 else x1_rows
                        sp.dma_start(acc[:], tokens(rows, t - x_base)).then_inc(acc_loaded, 16)
                        wait_alone(sp, d_added, G * TB * (t + 1) + 1, (consts, 6))
                        sp.dma_start(tokens(x1_rows, t - x_base), acc[:]).then_inc(stored, 16)

                    pairs(sp, half, body)
                sp.wait_ge(stored, 16 * (HALVES * PAIRS + 1))

            @block.gpsimd
            def _(pool):
                nc.gpsimd.memset(ident[:], 0.0).then_inc(consts, 1)
                nc.gpsimd.memset(causal[:], 0.0).then_inc(consts, 1)
                nc.gpsimd.memset(minus_half[:], -0.5).then_inc(consts, 1)
                pool.wait_ge(consts, 3)
                nc.gpsimd.affine_select(out=ident[:], in_=ident[:], compare_op=ALU.not_equal, fill=1.0, base=0,
                                        pattern=[[-1, P]], channel_multiplier=1).then_inc(consts, 1)
                nc.gpsimd.affine_select(out=causal[:], in_=causal[:], compare_op=ALU.is_ge, fill=NEG, base=0,
                                        pattern=[[-1, P]], channel_multiplier=1).then_inc(consts, 1)
                pool.wait_ge(consts, 5)
                nc.gpsimd.tensor_copy(ident_b[:], ident[:]).then_inc(consts, 1)

                def norm_scale(t):
                    wait_alone(pool, aggr_done, TB * (t + 1), (consts, 6))
                    nc.gpsimd.tensor_scalar(veps[:], mv[:, :, 1], LN_EPS, None, ALU.add).then_inc(veps_done, 1)
                    pool.wait_ge(veps_done, t + 1)
                    nc.gpsimd.tensor_tensor(veps[:], veps[:], minus_half[:], ALU.pow).then_inc(rstd_done, 1)

                for half in range(HALVES):
                    norm_scale(half * PAIRS)

                    def body(t, last):
                        for u in range(UNITS):
                            U = UNITS * t + u
                            s = u % 2
                            wait_alone(pool, rinv_done, U + 1, (consts, 6))
                            nc.gpsimd.tensor_scalar(probs[:, s, 0:P], probs[:, s, 0:P], rinv[:, s, 0:1], None, ALU.mult)
                            nc.gpsimd.tensor_scalar(probs[:, s, P:3 * P], probs[:, s, P:3 * P], rinv[:, s, 1:2], None,
                                                    ALU.mult).then_inc(probs_done, 1)
                            if u == 4 and not last:
                                norm_scale(t + 1)

                    pairs(pool, half, body)

            @block.scalar
            def _(act):
                def prologue(t):
                    for j in range(KT):
                        act.wait_ge(proj_filled, FILLS * t + j + 1)
                        nc.scalar.activation(xT[0][:, j, :], ps_proj[j % 2][:], ACT.Copy).then_inc(proj_high, 1)
                    for g in range(G):
                        act.wait_ge(proj_filled, FILLS * t + KT + g + 1)
                        nc.scalar.activation(kT[0][:, g, :], ps_proj[g % 2][:], ACT.Copy).then_inc(proj_high, 1)

                def values(t):
                    for n in range(2):
                        act.wait_ge(proj_filled, FILLS * t + KT + G + n + 1)
                        nc.scalar.activation(v[0][:, 2 * n:2 * n + 2, :], ps_proj[n % 2][:], ACT.Copy).then_inc(proj_high, 1)

                def query(t, m):
                    act.wait_ge(proj_filled, FILLS * t + 8 + m + 1)
                    nc.scalar.activation(qT[0][:, m % 2, :], ps_proj[m % 2][:], ACT.Copy, scale=SCALE).then_inc(proj_high, 1)

                def probs_transposed(t, u):
                    act.wait_ge(pT_filled, UNITS * t + u + 1)
                    nc.scalar.activation(pT[0][:, u % 2, :], ps_pT[u % 2][:, 0:3 * P], ACT.Copy).then_inc(pT_high, 1)

                def context(t, n):
                    act.wait_ge(c_filled, NH * t + n + 1)
                    nc.scalar.activation(cT[0][:, n // HPG, n % HPG, :], ps_c[:], ACT.Copy).then_inc(c_high, 1)

                for half in range(HALVES):
                    for n, ((high, _low), _src) in enumerate(chunks(half)):
                        N = half * NCH + n
                        if half and n == NCH - NH // TB:
                            act.wait_ge(d_filled, G * TB * PAIRS)
                        act.wait_ge(w_loaded[n % 2], 16 * (half * ((NCH + 1 - n % 2) // 2) + n // 2 + 1))
                        nc.scalar.activation(high, staged(n, high), ACT.Copy).then_inc(w_high, 1)
                    prologue(half * PAIRS)
                    values(half * PAIRS)

                    def body(t, last):
                        query(t, 0)
                        for u in range(UNITS):
                            U = UNITS * t + u
                            s = u % 2
                            if u >= 1:
                                probs_transposed(t, u - 1)
                            act.wait_ge(max_done, U + 1)
                            nc.scalar.activation(probs[:, s, 0:P], ps_s[s][:, 0:P], ACT.Exp, bias=negmax[:, s, 0:1],
                                                 accum_out=rowsum[:, s, 0:1])
                            nc.scalar.activation(probs[:, s, P:3 * P], ps_s[s][:, P:3 * P], ACT.Exp,
                                                 bias=negmax[:, s, 1:2], accum_out=rowsum[:, s, 1:2]).then_inc(exp_done, 1)
                            if u % 2 == 0 and u // 2 + 1 < NH:
                                query(t, u // 2 + 1)
                            if u % 2 == 1 and u >= 3:
                                context(t, (u - 3) // 2)
                        if not last:
                            for j in range(KT):
                                act.wait_ge(proj_filled, FILLS * (t + 1) + j + 1)
                                nc.scalar.activation(xT[0][:, j, :], ps_proj[j % 2][:], ACT.Copy).then_inc(proj_high, 1)
                        probs_transposed(t, UNITS - 1)
                        if not last:
                            for g in range(G):
                                act.wait_ge(proj_filled, FILLS * (t + 1) + KT + g + 1)
                                nc.scalar.activation(kT[0][:, g, :], ps_proj[g % 2][:], ACT.Copy).then_inc(proj_high, 1)
                        context(t, NH - 1)
                        if not last:
                            values(t + 1)

                    pairs(act, half, body)

            @block.vector
            def _(dve):
                def low(dst, ps, h):
                    return nc.vector.tensor_tensor(dst, ps, h.bitcast(F32), ALU.subtract)

                def normalise(t):
                    dve.wait_ge(x_loaded, 16 * (t + 1))
                    for n in range(TB):
                        nc.vector.bn_stats(stats[:, n, :], x_in[:, n, :]).then_inc(stats_done, 1)
                    wait_alone(dve, stats_done, TB * (t + 1), (consts, 6))
                    for n in range(TB):
                        nc.vector.bn_aggr(mv[:, n, :], stats[:, n, :]).then_inc(aggr_done, 1)

                def apply_norm(t):
                    dve.wait_ge(rstd_done, t + 1)
                    for n in range(TB):
                        ins = nc.vector.tensor_scalar(xn[:, n, :], x_in[:, n, :], mv[:, n, 0:1], veps[:, n:n + 1],
                                                      ALU.subtract, ALU.mult)
                    ins.then_inc(xn_done, 1)

                def xT_low(t):
                    for j in range(KT):
                        dve.wait_ge(proj_high, FILLS * t + j + 1)
                        low(xT[1][:, j, :], ps_proj[j % 2][:], xT[0][:, j, :]).then_inc(proj_low, 1)

                def k_low(t):
                    for g in range(G):
                        dve.wait_ge(proj_high, FILLS * t + KT + g + 1)
                        low(kT[1][:, g, :], ps_proj[g % 2][:], kT[0][:, g, :]).then_inc(proj_low, 1)

                def v_low(t, n):
                    dve.wait_ge(proj_high, FILLS * t + KT + G + n + 1)
                    src = v[0][:, 2 * n:2 * n + 2, :].rearrange("p a b -> p (a b)")
                    dst = v[1][:, 2 * n:2 * n + 2, :].rearrange("p a b -> p (a b)")
                    low(dst, ps_proj[n % 2][:], src).then_inc(proj_low, 1)

                def q_low(t, m):
                    dve.wait_ge(proj_high, FILLS * t + 8 + m + 1)
                    nc.vector.scalar_tensor_tensor(qT[1][:, m % 2, :], ps_proj[m % 2][:], SCALE,
                                                   qT[0][:, m % 2, :].bitcast(F32), ALU.mult,
                                                   ALU.subtract).then_inc(proj_low, 1)

                def pT_low_part(t, u):
                    dve.wait_ge(pT_high, UNITS * t + u + 1)
                    low(pT[1][:, u % 2, :], ps_pT[u % 2][:, 0:3 * P], pT[0][:, u % 2, :]).then_inc(pT_low, 1)

                def c_low_part(t, n):
                    dve.wait_ge(c_high, NH * t + n + 1)
                    low(cT[1][:, n // HPG, n % HPG, :], ps_c[:], cT[0][:, n // HPG, n % HPG, :]).then_inc(c_low, 1)

                def add_dense(t, g, n):
                    if g == 0 and n == 0:
                        dve.wait_ge(acc_loaded, 16 * (t + 1))
                    dve.wait_ge(d_filled, TB * (G * t + g) + n + 1)
                    nc.vector.tensor_tensor(acc[:, n, :], ps_d[:], acc[:, n, :], ALU.add).then_inc(d_added, 1)

                dve.sem_inc(c_low, 1)
                dve.sem_inc(d_added, 1)
                for half in range(HALVES):
                    for n, ((high, lowp), _src) in enumerate(chunks(half)):
                        dve.wait_ge(w_high, half * NCH + n + 1)
                        nc.vector.tensor_tensor(lowp, staged(n, high), high.bitcast(F32), ALU.subtract).then_inc(w_low, 1)
                    t0 = half * PAIRS
                    normalise(t0)
                    apply_norm(t0)
                    xT_low(t0)
                    k_low(t0)
                    for n in range(2):
                        v_low(t0, n)

                    def body(t, last):
                        q_low(t, 0)
                        for u in range(UNITS):
                            U = UNITS * t + u
                            s = u % 2
                            dve.wait_ge(s_filled, U + 1)
                            nc.vector.tensor_reduce(negmax[:, s, 0:1], ps_s[s][:, 0:P], AX.X, ALU.max, negate=True)
                            nc.vector.tensor_reduce(negmax[:, s, 1:2], ps_s[s][:, P:3 * P], AX.X, ALU.max,
                                                    negate=True).then_inc(max_done, 1)
                            if u >= 1:
                                pT_low_part(t, u - 1)
                            dve.wait_ge(exp_done, U + 1)
                            nc.vector.reciprocal(rinv[:, s, :], rowsum[:, s, :]).then_inc(rinv_done, 1)
                            if u % 2 == 0 and u // 2 + 1 < NH:
                                q_low(t, u // 2 + 1)
                            if u % 2 == 1 and u >= 3:
                                c_low_part(t, (u - 3) // 2)
                            if UNITS - 5 <= u < UNITS - 1:
                                add_dense(t, 0, u - (UNITS - 5))
                            if u == 3 and not last:
                                normalise(t + 1)
                            if u == 6 and not last:
                                apply_norm(t + 1)
                        if not last:
                            xT_low(t + 1)
                        pT_low_part(t, UNITS - 1)
                        if not last:
                            k_low(t + 1)
                        c_low_part(t, NH - 1)
                        if not last:
                            v_low(t + 1, 0)
                        add_dense(t, 1, 0)
                        if not last:
                            v_low(t + 1, 1)
                        for n in range(1, TB):
                            add_dense(t, 1, n)

                    pairs(dve, half, body)

            @block.tensor
            def _(pe):
                def product3(out, w, w_at, m, m_at, first=True, last=True):
                    for a, b, st, en in ((0, 0, first, False), (0, 1, False, False), (1, 0, False, last)):
                        ins = nc.tensor.matmul(out, w[a][w_at], m[b][m_at], start=st, stop=en)
                    return ins

                def bank_free(F):
                    if isinstance(F, int) and F < 2:
                        return
                    pe.wait_ge(proj_low, F - 1)

                def xT_fill(t):
                    pe.wait_ge(xn_done, t + 1)
                    for j in range(KT):
                        bank_free(FILLS * t + j)
                        for n in range(TB):
                            ins = nc.tensor.transpose(ps_proj[j % 2][:, n * P:(n + 1) * P], xn[:, n, j * P:(j + 1) * P], ident[:])
                        ins.then_inc(proj_filled, 1)

                def k_fill(t):
                    pe.wait_ge(proj_low, FILLS * t + KT)
                    for g in range(G):
                        bank_free(FILLS * t + KT + g)
                        for kt in range(KT):
                            ins = product3(ps_proj[g % 2][:], wkv, (slice(None), kt, slice(g * D, (g + 1) * D)),
                                           xT, (slice(None), kt, slice(None)), kt == 0, kt == KT - 1)
                        ins.then_inc(proj_filled, 1)

                def v_fill(t, n):
                    bank_free(FILLS * t + KT + G + n)
                    for i in range(2):
                        blk = 2 * n + i
                        for kt in range(KT):
                            ins = product3(ps_proj[n % 2][:, i * G * D:(i + 1) * G * D],
                                           xT, (slice(None), kt, slice(blk * P, (blk + 1) * P)),
                                           wkv, (slice(None), kt, slice(G * D, 2 * G * D)), kt == 0, kt == KT - 1)
                    ins.then_inc(proj_filled, 1)

                def q_fill(t, m, part):
                    if part == 0:
                        bank_free(FILLS * t + 8 + m)
                    for kt in range(part * KT // 2, (part + 1) * KT // 2):
                        ins = product3(ps_proj[m % 2][:], wq, (slice(None), kt, slice(m * D, (m + 1) * D)),
                                       xT, (slice(None), kt, slice(None)), kt == 0, kt == KT - 1)
                    if part == 1:
                        ins.then_inc(proj_filled, 1)

                def scores(t, u):
                    m, b = u // 2, u % 2
                    g, s = m // HPG, u % 2
                    if b == 0:
                        pe.wait_ge(proj_low, FILLS * t + 8 + m + 1)
                    for qb in range(2):
                        c0, n = qb * P, (qb + 1) * P
                        q0 = b * SEQ + qb * P
                        product3(ps_s[s][:, c0:c0 + n], qT, (slice(None), m % 2, slice(q0, q0 + P)),
                                 kT, (slice(None), g, slice(b * SEQ, b * SEQ + n)), True, False)
                        ins = nc.tensor.matmul(ps_s[s][:, c0 + n - P:c0 + n], ident_b[:], causal[:], start=False, stop=True)
                    ins.then_inc(s_filled, 1)

                def transposes(t, u):
                    s = u % 2
                    pe.wait_ge(probs_done, UNITS * t + u + 1)
                    for j in range(3):
                        ins = nc.tensor.transpose(ps_pT[s][:, j * P:(j + 1) * P], probs[:, s, j * P:(j + 1) * P], ident[:])
                    ins.then_inc(pT_filled, 1)

                def values_product(t, u):
                    m, b = u // 2, u % 2
                    g, s = m // HPG, u % 2
                    pe.wait_ge(pT_low, UNITS * t + u + 1)
                    if b == 0:
                        pe.wait_ge(c_low, NH * t + m + 1)
                    vs = slice(g * D, (g + 1) * D)
                    product3(ps_c[:, b * SEQ:(b + 1) * SEQ], v, (slice(None), 2 * b, vs),
                             pT, (slice(None), s, slice(0, 2 * P)), True, False)
                    ins = product3(ps_c[:, b * SEQ + P:(b + 1) * SEQ], v, (slice(None), 2 * b + 1, vs),
                                   pT, (slice(None), s, slice(2 * P, 3 * P)), False, True)
                    if b == 1:
                        ins.then_inc(c_filled, 1)

                def dense(t, g, n):
                    if n == 0:
                        pe.wait_ge(c_low, NH * t + (g + 1) * HPG + 1)
                    pe.wait_ge(d_added, TB * (G * t + g) + n + 1)
                    for j in range(HPG):
                        ins = product3(ps_d[:], cT, (slice(None), g, j, slice(n * P, (n + 1) * P)),
                                       wd, (slice(None), g * HPG + j, slice(None)), j == 0, j == HPG - 1)
                    ins.then_inc(d_filled, 1)

                pe.wait_ge(consts, 6)
                for half in range(HALVES):
                    t0 = half * PAIRS
                    xT_fill(t0)
                    pe.wait_ge(w_low, (half + 1) * NCH)
                    k_fill(t0)
                    for n in range(2):
                        v_fill(t0, n)

                    def body(t, last):
                        for part in range(2):
                            q_fill(t, 0, part)
                        q_fill(t, 1, 0)
                        for u in range(UNITS):
                            scores(t, u)
                            if u % 2 == 0 and u // 2 + 1 < NH:
                                q_fill(t, u // 2 + 1, 1)
                            if u % 2 == 1 and u // 2 + 2 < NH:
                                q_fill(t, u // 2 + 2, 0)
                            if u >= 1:
                                transposes(t, u - 1)
                            if u >= 2:
                                values_product(t, u - 2)
                            if UNITS - 5 <= u < UNITS - 1:
                                dense(t, 0, u - (UNITS - 5))
                        if not last:
                            xT_fill(t + 1)
                        values_product(t, UNITS - 2)
                        transposes(t, UNITS - 1)
                        if not last:
                            k_fill(t + 1)
                        values_product(t, UNITS - 1)
                        if not last:
                            v_fill(t + 1, 0)
                        dense(t, 1, 0)
                        if not last:
                            v_fill(t + 1, 1)
                        for n in range(1, TB):
                            dense(t, 1, n)

                    pairs(pe, half, body)


def cross_attention_phase(nc, x1_seq, context_seq, mask, mask_cols, w_qT, b_q, w_kT, b_k, w_vT, b_v, aux_dram, rinv_dram, x2_seq):
    B, C, T = x1_seq.shape
    DH = 16
    HQ = 4
    QUADS = C // (DH * HQ)
    CT = C // P
    TBL = T // P
    AUX, AUXROWS = 3 * DH, 6
    MAXROW = 96
    NEG4 = -4.0e6
    AUX_STEPS = 11
    TC = T // 32
    FILLS = 10
    PRO = 7
    assert T == BANK and DH == 16 and QUADS == 4 and CT == 2

    with ExitStack() as ctx:
        def sb(name, shape, dt=F32):
            return ctx.enter_context(nc.sbuf_tensor("b_" + name, shape, dt))

        def psum(name, shape):
            return ctx.enter_context(nc.psum_tensor("b_" + name, shape, F32))

        def sem(name):
            return ctx.enter_context(nc.semaphore("b_" + name))

        stack = sb("stack", [P, QUADS, 2, HQ, T], F32R)
        probs = sb("probs", [P, 2, HQ, T])
        v_stack = sb("v_stack", [P, TBL, C // DH, 32])
        v_raw = sb("v_raw", [P, TBL, C])
        w = {n: [sb(f"w{n}_{s}", [P, CT, C], F32R) for s in "hl"] for n in "qkv"}
        w_stage = sb("w_stage", [P, 3, CT, C])
        bias = {n: sb(f"bias_{n}", [P, CT]) for n in "qk"}
        bias_v = sb("bias_v", [P, C])
        x_in = sb("x_in", [P, CT, T])
        c_in = sb("c_in", [P, CT, T])
        xn = sb("xn", [P, CT, T])
        xs = [sb(f"x_{s}", [P, CT, T], F32R) for s in "hl"]
        cs = [sb(f"c_{s}", [P, CT, T], F32R) for s in "hl"]
        raw = {n: sb(f"raw_{n}", [P, T]) for n in "qk"}
        tile = {n: [[sb(f"{n}{half}_{s}", [P, T], F32R) for s in "hl"] for half in range(2)] for n in "qk"}
        mask_b = sb("mask_b", [P, T])
        mask_col = sb("mask_col", [P, TBL])
        mask_r = sb("mask_r", [P, TC])
        mask_rows, one_minus, neg_row = (probs[0:B, 0, i, :] for i in range(3))
        stats = sb("stats", [P, CT, 6])
        mv = sb("mv", [P, CT, 2])
        rstd = sb("rstd", [P, CT])
        minus_half = sb("minus_half", [P, CT])
        ident = sb("ident", [P, P])
        negmax = sb("negmax", [P, TBL, HQ])
        nm_split = sb("nm_split", [P, TBL, 2, HQ])
        nm_rows = sb("nm_rows", [2 * HQ, T])
        o_sb = sb("o_sb", [P, QUADS, T])
        sums = sb("sums", [P, TC])
        rsum = sb("rsum", [P, TC])
        r_out = sb("r_out", [P, TC])
        out_tiles = sb("out_tiles", [P, 3, QUADS, T])
        r_b, x_res, y = (out_tiles[:, i, :, :] for i in range(3))
        aux = out_tiles[0:B].rearrange("b i q t -> b (i q t)").rearrange("b (r s t) -> b r s t", r=AUXROWS, s=2)
        assert 3 * QUADS == 2 * AUXROWS

        ps_e = [psum(f"ps_e{i}", [P, 2, BANK]) for i in range(2)]
        ps_m = [psum(f"ps_m{i}", [P, BANK]) for i in range(2)]
        ps_o = psum("ps_o", [P, BANK])
        ps_p = psum("ps_p", [P, BANK])

        consts = sem("consts")
        w_loaded = sem("w_loaded")
        w_high = sem("w_high")
        w_low = sem("w_low")
        mrow_loaded = sem("mrow_loaded")
        aux_step = sem("aux_step")
        aux_stored = sem("aux_stored")
        xc_loaded = sem("xc_loaded")
        mask_b_loaded = sem("mask_b_loaded")
        mask_col_loaded = sem("mask_col_loaded")
        mask_r_loaded = sem("mask_r_loaded")
        stats_done = sem("stats_done")
        aggr_done = sem("aggr_done")
        veps_done = sem("veps_done")
        rstd_done = sem("rstd_done")
        xn_done = sem("xn_done")
        xs_high = sem("xs_high")
        xs_low = sem("xs_low")
        cs_high = sem("cs_high")
        cs_low = sem("cs_low")
        proj_filled = sem("proj_filled")
        raw_done = sem("raw_done")
        tile_high = sem("tile_high")
        tile_low = sem("tile_low")
        v_done = sem("v_done")
        vbias_done = sem("vbias_done")
        stacked = [sem(f"stacked{q}") for q in range(QUADS)]
        m_filled = sem("m_filled")
        m_reduced = sem("m_reduced")
        nm_high = sem("nm_high")
        nm_low = sem("nm_low")
        nm_rows_done = sem("nm_rows_done")
        nm_stacked = sem("nm_stacked")
        e_filled = sem("e_filled")
        e_done = sem("e_done")
        o_filled = sem("o_filled")
        o_out = sem("o_out")
        sums_loaded = sem("sums_loaded")
        r_step = sem("r_step")
        r_done = sem("r_done")
        r_stored = sem("r_stored")
        r_loaded = [sem(f"r_loaded{q}") for q in range(QUADS)]
        o_scaled = sem("o_scaled")
        y_done = sem("y_done")
        xres_clear = sem("xres_clear")
        xres_loaded = sem("xres_loaded")
        y_stored = sem("y_stored")

        ORDER = ["m1", "k0", "q0", "m2", "v0", "v1", "m3", "q1", "k1", "m0"]
        LAST_ORDER = ["m1", "m2", "m3"]
        PRO_ORDER = ["k0", "q0", "v0", "v1", "q1", "k1", "m0"]
        assert len(ORDER) == FILLS and len(PRO_ORDER) == PRO

        def fill_no(where, name):
            if where is None:
                return PRO_ORDER.index(name)
            b, last = where
            return FILLS * b + PRO + (LAST_ORDER if last else ORDER).index(name)

        TILES = ["k0", "q0", "q1", "k1"]

        def tile_no(b, name):
            return 4 * b + TILES.index(name)

        def loop(eng, body):
            body(0, True, False)
            with eng.Fori(1, B - 2) as b:
                body(b, False, False)
            body(B - 2, False, False)
            body(B - 1, False, True)

        def static(b):
            return isinstance(b, int)

        with nc.Block() as block:
            @block.sync
            def _(sp):
                for n, t in enumerate((w_qT, w_kT, w_vT)):
                    sp.dma_start(w_stage[:, n, :, :], t.rearrange("(k p) o -> p k o", p=P)).then_inc(w_loaded, 16)
                sp.dma_start(bias["q"][:], b_q).then_inc(w_loaded, 16)
                sp.dma_start(bias["k"][:], b_k).then_inc(w_loaded, 16)
                sp.dma_start(bias_v[:], b_v.to_broadcast([P, C])).then_inc(w_loaded, 16)
                sp.dma_start(mask_rows, mask).then_inc(mrow_loaded, 16)

                def load_xc(b):
                    sp.dma_start(x_in[:], x1_seq[b].rearrange("(k p) t -> p k t", p=P)).then_inc(xc_loaded, 16)
                    sp.dma_start(c_in[:], context_seq[b].rearrange("(k p) t -> p k t", p=P)).then_inc(xc_loaded, 16)

                def load_mask_b(b):
                    sp.dma_start(mask_b[:], mask[b].rearrange("(o t) -> o t", o=1).to_broadcast([P, T])).then_inc(mask_b_loaded, 16)

                def load_mask_col(b):
                    sp.dma_start(mask_col[:], mask_cols[b]).then_inc(mask_col_loaded, 16)

                def load_mask_r(b):
                    sp.dma_start(mask_r[:], mask[b].rearrange("(o c t) -> o c t", o=1, c=32)
                                 .to_broadcast([HQ, 32, TC])).then_inc(mask_r_loaded, 16)

                def stack_quad(b, q):
                    half, p0 = q // 2, (q % 2) * HQ * DH
                    for side, name, part, row in ((0, "q", 0, 0), (0, "q", 0, DH), (0, "q", 1, 2 * DH),
                                                  (1, "k", 0, 0), (1, "k", 1, DH), (1, "k", 0, 2 * DH)):
                        sp.dma_start(stack[row:row + DH, q, side, :, :].bitcast(F32),
                                     tile[name][half][part][p0:p0 + HQ * DH, :].bitcast(F32)).then_inc(stacked[q], 16)
                    for side in range(2):
                        sp.dma_start(stack[AUX:AUX + AUXROWS, q, side, :, :].bitcast(F32),
                                     aux_dram[b][:, side:side + 1, :].to_broadcast([AUXROWS, HQ, T])).then_inc(stacked[q], 16)

                def stack_negmax(b, q):
                    wait_alone(sp, nm_rows_done, QUADS * b + q + 1, (consts, 7))
                    sp.dma_start(stack[MAXROW:MAXROW + 2, q, 0, :, :].bitcast(F32), nm_rows[:]).then_inc(nm_stacked, 16)

                def sums_out(g, q):
                    wait_alone(sp, o_out, g + 1, (consts, 7))
                    sp.dma_start(sums[:], o_sb[DH::32, q, :]).then_inc(sums_loaded, 16)

                def reciprocals(g, q):
                    wait_alone(sp, r_done, g + 1, (consts, 7))
                    sp.dma_start(rinv_dram[q].rearrange("(p c) -> p c", p=P), r_out[:]).then_inc(r_stored, 16)
                    wait_alone(sp, r_stored, 16 * (g + 1), (consts, 7))
                    sp.dma_start(r_b[:, q, :], rinv_dram[q].rearrange("(j o t) -> j o t", j=HQ, o=1)
                                 .to_broadcast([HQ, 32, T])).then_inc(r_loaded[q], 16)

                def rows(seq, b, j):
                    return seq[b].rearrange("(q j d) t -> j d q t", q=QUADS, j=HQ)[j]

                def load_res(b):
                    for j in range(HQ):
                        sp.dma_start(x_res[32 * j:32 * j + DH, :, :], rows(x1_seq, b, j)).then_inc(xres_loaded, 16)

                def store_y(b):
                    for j in range(HQ):
                        sp.dma_start(rows(x2_seq, b, j), y[32 * j:32 * j + DH, :, :]).then_inc(y_stored, 16)

                load_xc(0)
                load_mask_b(0)
                load_mask_col(0)
                load_mask_r(0)
                sp.wait_ge(aux_step, AUX_STEPS)
                sp.dma_start(aux_dram.rearrange("b r s t -> b (r s t)"),
                             aux.rearrange("b r s t -> b (r s t)")).then_inc(aux_stored, 16)
                sp.wait_ge(aux_stored, 16)
                sp.wait_ge(xres_clear, 1)
                load_res(0)
                sp.wait_ge(consts, 5)
                sp.wait_ge(tile_low, tile_no(0, "q0") + 1)
                stack_quad(0, 0)
                stack_quad(0, 1)
                sp.wait_ge(xs_low, 1)
                sp.wait_ge(cs_low, 1)
                load_xc(1)
                sp.wait_ge(tile_low, tile_no(0, "k1") + 1)
                load_mask_b(1)
                stack_quad(0, 2)
                stack_negmax(0, 0)

                def body(b, first, last):
                    g = QUADS * b
                    if not first:
                        wait_alone(sp, e_filled, 8 * g, (consts, 7))
                    stack_quad(b, 3)
                    stack_negmax(b, 1)
                    if not first:
                        sums_out(g - 1, 3)
                        reciprocals(g - 1, 3)
                        load_mask_r(b)
                    stack_negmax(b, 2)
                    if not last:
                        wait_alone(sp, v_done, QUADS * (b + 1), (consts, 7))
                        load_mask_col(b + 1)
                    sums_out(g, 0)
                    if not first:
                        wait_alone(sp, y_done, g, (consts, 7))
                        store_y(b - 1)
                        load_res(b)
                    if not last:
                        wait_alone(sp, xs_low, b + 2, (consts, 7))
                        wait_alone(sp, cs_low, b + 2, (consts, 7))
                        if not (static(b) and b + 2 >= B):
                            load_xc(b + 2)
                        wait_alone(sp, tile_low, tile_no(b + 1, "q0") + 1, (consts, 7))
                        wait_alone(sp, e_filled, 8 * (g + 1), (consts, 7))
                        stack_quad(b + 1, 0)
                    reciprocals(g, 0)
                    if not last:
                        wait_alone(sp, e_filled, 8 * (g + 2), (consts, 7))
                        stack_quad(b + 1, 1)
                    stack_negmax(b, 3)
                    sums_out(g + 1, 1)
                    reciprocals(g + 1, 1)
                    if not last:
                        wait_alone(sp, tile_low, tile_no(b + 1, "k1") + 1, (consts, 7))
                        if not (static(b) and b + 2 >= B):
                            load_mask_b(b + 2)
                        wait_alone(sp, e_filled, 8 * (g + 3), (consts, 7))
                        stack_quad(b + 1, 2)
                        stack_negmax(b + 1, 0)
                    sums_out(g + 2, 2)
                    reciprocals(g + 2, 2)

                loop(sp, body)
                sums_out(QUADS * B - 1, 3)
                reciprocals(QUADS * B - 1, 3)
                sp.wait_ge(y_done, QUADS * B)
                store_y(B - 1)
                sp.wait_ge(y_stored, 16 * HQ * B)

            @block.gpsimd
            def _(pool):
                nc.gpsimd.memset(ident[:], 0.0).then_inc(consts, 1)
                nc.gpsimd.memset(minus_half[:], -0.5).then_inc(consts, 1)
                nc.gpsimd.memset(stack[:].rearrange("p a b c t -> p (a b c t)").bitcast(F32), 0.0).then_inc(consts, 1)
                pool.wait_ge(consts, 3)
                nc.gpsimd.affine_select(out=ident[:], in_=ident[:], compare_op=ALU.not_equal, fill=1.0, base=0,
                                        pattern=[[-1, P]], channel_multiplier=1).then_inc(consts, 1)
                pool.wait_ge(consts, 4)
                nc.gpsimd.memset(stack[MAXROW:MAXROW + 2, :, 1, :, :].bitcast(F32), 1.0).then_inc(consts, 1)
                pool.wait_ge(consts, 5)
                nc.gpsimd.memset(v_stack[:], 0.0).then_inc(consts, 1)
                pool.wait_ge(consts, 6)
                nc.gpsimd.memset(v_stack[:, :, :, DH:DH + 1], 1.0).then_inc(consts, 1)
                pool.wait_ge(aux_stored, 16)
                nc.gpsimd.memset(x_res, 0.0).then_inc(xres_clear, 1)

                def norm_scale(b):
                    wait_alone(pool, aggr_done, CT * (b + 1), (consts, 7))
                    nc.gpsimd.tensor_scalar(rstd[:], mv[:, :, 1], LN_EPS, None, ALU.add).then_inc(veps_done, 1)
                    pool.wait_ge(veps_done, b + 1)
                    nc.gpsimd.tensor_tensor(rstd[:], rstd[:], minus_half[:], ALU.pow).then_inc(rstd_done, 1)

                def low(dst, full, high, high_sem, n, out_sem):
                    pool.wait_ge(high_sem, n)
                    nc.gpsimd.tensor_tensor(dst, full, high.bitcast(F32), ALU.subtract).then_inc(out_sem, 1)

                def context_low(b):
                    low(cs[1][:], c_in[:], cs[0][:], cs_high, b + 1, cs_low)

                def x_low(b):
                    low(xs[1][:], xn[:], xs[0][:], xs_high, b + 1, xs_low)

                def tile_low_part(b, name):
                    n, half = name[0], int(name[1])
                    if not (static(b) and b == 0):
                        pool.wait_ge(stacked[2 * half + 1], 16 * 8 * b)
                    low(tile[n][half][1][:], raw[n][:], tile[n][half][0][:], tile_high, tile_no(b, name) + 1, tile_low)

                def values(b, q):
                    if q == 0:
                        wait_alone(pool, vbias_done, 2 * (b + 1), (consts, 7))
                        wait_alone(pool, mask_col_loaded, 16 * (b + 1), (consts, 7))
                    if not (static(b) and b == 0):
                        wait_alone(pool, o_filled, QUADS * (b - 1) + q + 1, (consts, 7))
                    for k in range(TBL):
                        ins = nc.gpsimd.tensor_scalar(
                            v_stack[:, k, HQ * q:HQ * q + HQ, 0:DH],
                            v_raw[:, k, HQ * DH * q:HQ * DH * (q + 1)].rearrange("p (h d) -> p h d", h=HQ),
                            mask_col[:, k:k + 1], None, ALU.mult)
                    ins.then_inc(v_done, 1)

                def residual(b, g, q):
                    pool.wait_ge(r_loaded[q], 16 * (b + 1))
                    nc.gpsimd.tensor_tensor(r_b[:, q, :], o_sb[:, q, :], r_b[:, q, :], ALU.mult).then_inc(o_scaled, 1)
                    if q == 0:
                        pool.wait_ge(xres_loaded, 16 * HQ * (b + 1))
                        if not (static(b) and b == 0):
                            pool.wait_ge(y_stored, 16 * HQ * b)
                    pool.wait_ge(o_scaled, g + 2)
                    nc.gpsimd.tensor_tensor(y[:, q, :], r_b[:, q, :], x_res[:, q, :], ALU.add).then_inc(y_done, 1)

                pool.wait_ge(consts, 7)
                pool.sem_inc(o_scaled, 1)
                norm_scale(0)
                context_low(0)
                x_low(0)
                for name in TILES:
                    tile_low_part(0, name)
                for q in range(3):
                    values(0, q)

                def body(b, first, last):
                    g = QUADS * b
                    if not last:
                        norm_scale(b + 1)
                        context_low(b + 1)
                    values(b, 3)
                    if not last:
                        x_low(b + 1)
                        tile_low_part(b + 1, "k0")
                    if not first:
                        residual(b - 1, g - 1, 3)
                    if not last:
                        tile_low_part(b + 1, "q0")
                    if not last:
                        values(b + 1, 0)
                    residual(b, g, 0)
                    if not last:
                        values(b + 1, 1)
                        tile_low_part(b + 1, "q1")
                        tile_low_part(b + 1, "k1")
                    residual(b, g + 1, 1)
                    if not last:
                        values(b + 1, 2)
                    residual(b, g + 2, 2)

                loop(pool, body)
                residual(B - 1, QUADS * B - 1, 3)

            @block.scalar
            def _(act):
                for n, name in enumerate("qkv"):
                    if n == 0:
                        act.wait_ge(w_loaded, 16 * 6)
                    nc.scalar.activation(w[name][0][:], w_stage[:, n, :, :], ACT.Copy).then_inc(w_high, 1)

                def context_high(b):
                    act.wait_ge(xc_loaded, 32 * (b + 1))
                    if not (static(b) and b == 0):
                        act.wait_ge(tile_high, 4 * b)
                    nc.scalar.activation(cs[0][:], c_in[:], ACT.Copy).then_inc(cs_high, 1)

                def x_high(b):
                    act.wait_ge(xn_done, b + 1)
                    nc.scalar.activation(xs[0][:], xn[:], ACT.Copy).then_inc(xs_high, 1)

                def tile_high_part(b, name):
                    n, half = name[0], int(name[1])
                    act.wait_ge(raw_done, tile_no(b, name) + 1)
                    if not (static(b) and b == 0):
                        act.wait_ge(stacked[2 * half + 1], 16 * 8 * b)
                    nc.scalar.activation(tile[n][half][0][:], raw[n][:], ACT.Copy).then_inc(tile_high, 1)

                def negmax_rows(where, b, q):
                    g = QUADS * b + q
                    act.wait_ge(proj_filled, fill_no(where, f"m{q}") + 1)
                    act.wait_ge(nm_stacked, 16 * g)
                    nc.scalar.activation(nm_rows[:], ps_p[0:2 * HQ, :], ACT.Copy).then_inc(nm_rows_done, 1)

                def exps(g, k):
                    for p in range(2):
                        act.wait_ge(e_filled, 8 * g + 2 * k + p + 1)
                        nc.scalar.activation(probs[:, k % 2, 2 * p:2 * p + 2, :], ps_e[p][:], ACT.Exp,
                                             scale=0.25).then_inc(e_done, 1)

                def output(g, q):
                    act.wait_ge(o_filled, g + 1)
                    if not (static(g) and g < QUADS):
                        act.wait_ge(o_scaled, g - QUADS + 2)
                    nc.scalar.activation(o_sb[:, q, :], ps_o[:], ACT.Copy).then_inc(o_out, 1)

                context_high(0)
                x_high(0)
                for name in TILES:
                    tile_high_part(0, name)
                negmax_rows(None, 0, 0)

                def body(b, first, last):
                    g = QUADS * b
                    where = (b, last)
                    exps(g, 0)
                    if not first:
                        output(g - 1, 3)
                    negmax_rows(where, b, 1)
                    if not last:
                        context_high(b + 1)
                    exps(g, 1)
                    if not last:
                        x_high(b + 1)
                    exps(g, 2)
                    exps(g, 3)
                    if not last:
                        tile_high_part(b + 1, "k0")
                    exps(g + 1, 0)
                    output(g, 0)
                    if not last:
                        tile_high_part(b + 1, "q0")
                    negmax_rows(where, b, 2)
                    for k in (1, 2, 3):
                        exps(g + 1, k)
                    exps(g + 2, 0)
                    output(g + 1, 1)
                    negmax_rows(where, b, 3)
                    exps(g + 2, 1)
                    if not last:
                        tile_high_part(b + 1, "q1")
                    exps(g + 2, 2)
                    if not last:
                        tile_high_part(b + 1, "k1")
                    exps(g + 2, 3)
                    exps(g + 3, 0)
                    output(g + 2, 2)
                    if not last:
                        negmax_rows(where, b + 1, 0)
                    for k in (1, 2, 3):
                        exps(g + 3, k)

                loop(act, body)
                output(QUADS * B - 1, 3)

            @block.vector
            def _(dve):
                dve.wait_ge(w_loaded, 16 * 6)
                for n, name in enumerate("qkv"):
                    dve.wait_ge(w_high, n + 1)
                    nc.vector.tensor_tensor(w[name][1][:], w_stage[:, n, :, :], w[name][0][:].bitcast(F32),
                                            ALU.subtract).then_inc(w_low, 1)

                steps = [0]

                def aux_op(ins):
                    steps[0] += 1
                    ins.then_inc(aux_step, 1)
                    dve.wait_ge(aux_step, steps[0])

                def split_rows(full, side, highs, lows):
                    aux_op(nc.vector.tensor_copy(aux[:, highs[0], side, :].bitcast(F32R), full))
                    aux_op(nc.vector.tensor_tensor(aux[:, lows[0], side, :].bitcast(F32R), full,
                                                   aux[:, highs[0], side, :], ALU.subtract))
                    for r in highs[1:]:
                        nc.vector.tensor_copy(aux[:, r, side, :], aux[:, highs[0], side, :])

                dve.wait_ge(mrow_loaded, 16)
                aux_op(nc.vector.tensor_scalar(one_minus, mask_rows, -1.0, 1.0, ALU.mult, ALU.add))
                split_rows(one_minus, 0, (0, 2), (1,))
                split_rows(mask_rows, 0, (3, 5), (4,))
                aux_op(nc.vector.memset(neg_row, NEG4))
                split_rows(neg_row, 1, (0, 1), (2,))
                aux_op(nc.vector.tensor_scalar(one_minus, one_minus, NEG4, None, ALU.mult))
                aux_op(nc.vector.tensor_copy(aux[:, 3, 1, :].bitcast(F32R), one_minus))
                nc.vector.tensor_copy(aux[:, 4, 1, :], aux[:, 3, 1, :])
                nc.vector.tensor_tensor(aux[:, 5, 1, :].bitcast(F32R), one_minus, aux[:, 3, 1, :],
                                        ALU.subtract).then_inc(aux_step, 1)
                assert steps[0] + 1 == AUX_STEPS

                def normalise(b):
                    dve.wait_ge(xc_loaded, 32 * (b + 1))
                    for k in range(CT):
                        nc.vector.bn_stats(stats[:, k, :], x_in[:, k, :]).then_inc(stats_done, 1)
                    wait_alone(dve, stats_done, CT * (b + 1), (consts, 7))
                    for k in range(CT):
                        nc.vector.bn_aggr(mv[:, k, :], stats[:, k, :]).then_inc(aggr_done, 1)

                def apply_norm(b):
                    dve.wait_ge(rstd_done, b + 1)
                    for k in range(CT):
                        ins = nc.vector.tensor_scalar(xn[:, k, :], x_in[:, k, :], mv[:, k, 0:1], rstd[:, k:k + 1],
                                                      ALU.subtract, ALU.mult)
                    ins.then_inc(xn_done, 1)

                def raw_tile(where, b, name):
                    n, half = name[0], int(name[1])
                    dve.wait_ge(proj_filled, fill_no(where, name) + 1)
                    if name in ("k0", "q0"):
                        if name == "k0":
                            dve.wait_ge(mask_b_loaded, 16 * (b + 1))
                        if not (static(b) and b == 0):
                            dve.wait_ge(tile_low, 4 * b)
                    else:
                        dve.wait_ge(tile_low, tile_no(b, n + "0") + 1)
                    nc.vector.scalar_tensor_tensor(raw[n][:], ps_p[:], bias[n][:, half:half + 1], mask_b[:], ALU.add,
                                                   ALU.mult).then_inc(raw_done, 1)

                def raw_values(where, b, i):
                    dve.wait_ge(proj_filled, fill_no(where, f"v{i}") + 1)
                    if i == 0 and not (static(b) and b == 0):
                        dve.wait_ge(v_done, QUADS * b)
                    for k in range(2):
                        ins = nc.vector.tensor_tensor(v_raw[:, 2 * i + k, :], ps_p[:, k * C:(k + 1) * C], bias_v[:], ALU.add)
                    ins.then_inc(vbias_done, 1)

                def maxima(g, k0, k1):
                    for k in range(k0, k1):
                        if k == 0 and not (static(g) and g == 0):
                            dve.wait_ge(nm_low, g)
                        dve.wait_ge(m_filled, 16 * g + k + 1)
                        nc.vector.tensor_reduce(negmax[:, k // HQ, k % HQ:k % HQ + 1], ps_m[k % 2][:], AX.X, ALU.max,
                                                negate=True).then_inc(m_reduced, 1)

                def split_maxima(g):
                    dve.wait_ge(m_reduced, 16 * (g + 1))
                    nc.vector.tensor_copy(nm_split[:, :, 0, :].bitcast(F32R), negmax[:]).then_inc(nm_high, 1)
                    dve.wait_ge(nm_high, g + 1)
                    nc.vector.tensor_tensor(nm_split[:, :, 1, :].bitcast(F32R), negmax[:], nm_split[:, :, 0, :],
                                            ALU.subtract).then_inc(nm_low, 1)

                def reciprocal(g):
                    dve.wait_ge(sums_loaded, 16 * (g + 1))
                    nc.vector.reciprocal(rsum[:], sums[:]).then_inc(r_step, 1)
                    dve.wait_ge(r_step, g + 1)

                def masked_reciprocal(g, b, q):
                    reciprocal(g)
                    if q == 0:
                        dve.wait_ge(mask_r_loaded, 16 * (b + 1))
                    if not (static(g) and g == 0):
                        dve.wait_ge(r_stored, 16 * g)
                    nc.vector.tensor_tensor(r_out[:], rsum[:], mask_r[:], ALU.mult).then_inc(r_done, 1)

                normalise(0)
                apply_norm(0)
                for name in ("k0", "q0"):
                    raw_tile(None, 0, name)
                raw_values(None, 0, 0)
                raw_values(None, 0, 1)
                for name in ("q1", "k1"):
                    raw_tile(None, 0, name)
                for g in range(2):
                    maxima(g, 0, 16)
                    split_maxima(g)

                def body(b, first, last):
                    g = QUADS * b
                    where = (b, last)
                    nxt = b + 1
                    maxima(g + 2, 0, 4)
                    if not last:
                        normalise(nxt)
                    maxima(g + 2, 4, 8)
                    if not last:
                        apply_norm(nxt)
                    maxima(g + 2, 8, 12)
                    if not first:
                        masked_reciprocal(g - 1, b - 1, 3)
                    maxima(g + 2, 12, 16)
                    split_maxima(g + 2)
                    if not last:
                        raw_tile(where, nxt, "k0")
                        raw_tile(where, nxt, "q0")
                    maxima(g + 3, 0, 8)
                    if not last:
                        raw_values(where, nxt, 0)
                    maxima(g + 3, 8, 12)
                    masked_reciprocal(g, b, 0)
                    if not last:
                        raw_values(where, nxt, 1)
                    maxima(g + 3, 12, 16)
                    split_maxima(g + 3)
                    if not last:
                        maxima(g + 4, 0, 4)
                        raw_tile(where, nxt, "q1")
                        maxima(g + 4, 4, 8)
                        raw_tile(where, nxt, "k1")
                        maxima(g + 4, 8, 12)
                    masked_reciprocal(g + 1, b, 1)
                    if not last:
                        maxima(g + 4, 12, 16)
                        split_maxima(g + 4)
                        maxima(g + 5, 0, 12)
                    masked_reciprocal(g + 2, b, 2)
                    if not last:
                        maxima(g + 5, 12, 16)
                        split_maxima(g + 5)

                loop(dve, body)
                masked_reciprocal(QUADS * B - 1, B - 1, 3)

            @block.tensor
            def _(pe):
                ROWS = {"max": MAXROW, "exp": MAXROW + 2}

                def bank(where, b, name):
                    order = PRO_ORDER if where is None else (LAST_ORDER if where[1] else ORDER)
                    i = order.index(name)
                    if where is None and i == 0:
                        return
                    if i == 0:
                        pe.wait_ge(nm_rows_done, QUADS * b + 1)
                        return
                    before = order[i - 1]
                    if before[0] == "m":
                        cur = b if (where is not None and name[0] == "m" and name != "m0") else b - 1
                        pe.wait_ge(nm_rows_done, QUADS * cur + int(before[1]) + 1)
                    else:
                        nxt = b if name[0] != "m" or name == "m0" else b + 1
                        if before[0] == "v":
                            pe.wait_ge(vbias_done, 2 * nxt + int(before[1]) + 1)
                        else:
                            pe.wait_ge(raw_done, tile_no(nxt, before) + 1)

                def products(out, pairs):
                    n = len(pairs)
                    for i, (s, m) in enumerate(pairs):
                        for k, (a, c) in enumerate(((0, 0), (0, 1), (1, 0))):
                            ins = nc.tensor.matmul(out, s(a), m(c), start=(i == 0 and k == 0), stop=(i == n - 1 and k == 2))
                    return ins

                def project(where, b, name):
                    n, half = name[0], int(name[1])
                    src = xs if n == "q" else cs
                    pe.wait_ge(xs_low if n == "q" else cs_low, b + 1)
                    bank(where, b, name)
                    products(ps_p[:], [(lambda a, k=k: w[n][a][:, k, half * P:(half + 1) * P],
                                        lambda c, k=k: src[c][:, k, :]) for k in range(CT)]).then_inc(proj_filled, 1)

                def project_values(where, b, i):
                    bank(where, b, f"v{i}")
                    for j in range(2):
                        blk = 2 * i + j
                        ins = products(ps_p[:, j * C:(j + 1) * C],
                                       [(lambda a, k=k: cs[a][:, k, blk * P:(blk + 1) * P],
                                         lambda c, k=k: w["v"][c][:, k, :]) for k in range(CT)])
                    ins.then_inc(proj_filled, 1)

                def negmax_transpose(where, b, q):
                    g = QUADS * b + q
                    pe.wait_ge(nm_low, g + 1)
                    bank(where, b, f"m{q}")
                    for k in range(TBL):
                        ins = nc.tensor.transpose(ps_p[0:2 * HQ, k * P:(k + 1) * P],
                                                  nm_split[:, k, :, :].rearrange("p s h -> p (s h)"), ident[:])
                    ins.then_inc(proj_filled, 1)

                def max_scores(b, g, q, k0, k1):
                    for k in range(k0, k1):
                        blk, h = k // HQ, k % HQ
                        if k == 0:
                            pe.wait_ge(stacked[q], 16 * 8 * (b + 1))
                        if not (static(g) and 16 * g + k < 2):
                            pe.wait_ge(m_reduced, 16 * g + k - 1)
                        nc.tensor.matmul(ps_m[k % 2][:], stack[0:MAXROW, q, 0, h, blk * P:(blk + 1) * P],
                                         stack[0:MAXROW, q, 1, h, :], start=True, stop=True).then_inc(m_filled, 1)

                def exp_scores(g, q, k, first):
                    if k == 0:
                        pe.wait_ge(nm_stacked, 16 * (g + 1))
                    for p in range(2):
                        if not (static(g) and 8 * g + 2 * k + p < 2):
                            pe.wait_ge(e_done, 8 * g + 2 * k + p - 1)
                        for i in range(2):
                            h = 2 * p + i
                            ins = nc.tensor.matmul(ps_e[p][:, i, :], stack[0:MAXROW + 2, q, 1, h, k * P:(k + 1) * P],
                                                   stack[0:MAXROW + 2, q, 0, h, :], start=True, stop=True)
                        ins.then_inc(e_filled, 1)

                def values_product(g, q, k):
                    pe.wait_ge(e_done, 8 * g + 2 * k + 2)
                    if k == 0:
                        pe.wait_ge(v_done, g + 1)
                        pe.wait_ge(o_out, g)
                    for h in range(HQ):
                        ins = nc.tensor.matmul(ps_o[32 * h:32 * h + 32, :], v_stack[:, k, HQ * q + h, :],
                                               probs[:, k % 2, h, :], start=(k == 0), stop=(k == TBL - 1))
                    if k == TBL - 1:
                        ins.then_inc(o_filled, 1)

                pe.wait_ge(consts, 7)
                pe.wait_ge(w_low, 3)
                project(None, 0, "k0")
                project(None, 0, "q0")
                project_values(None, 0, 0)
                project_values(None, 0, 1)
                project(None, 0, "q1")
                project(None, 0, "k1")
                max_scores(0, 0, 0, 0, 16)
                negmax_transpose(None, 0, 0)
                max_scores(0, 1, 1, 0, 16)

                def body(b, first, last):
                    g = QUADS * b
                    where = (b, last)
                    beside = [(b, 2), (b, 3), (b + 1, 0), (b + 1, 1)]
                    after = {(0, 3): "k0", (1, 0): "q0", (1, 1): "v0", (1, 2): "v1", (2, 1): "q1", (2, 2): "k1"}
                    for q in range(QUADS):
                        mb, mq = beside[q]
                        for k in range(TBL):
                            exp_scores(g + q, q, k, first)
                            name = after.get((q, k))
                            if name and not last:
                                if name[0] == "v":
                                    project_values(where, b + 1, int(name[1]))
                                else:
                                    project(where, b + 1, name)
                            if not (last and q >= 2):
                                max_scores(mb, g + q + 2, mq, 4 * k, 4 * k + 4)
                            if k > 0:
                                values_product(g + q, q, k - 1)
                            elif q > 0:
                                values_product(g + q - 1, q - 1, TBL - 1)
                            elif not first:
                                values_product(g - 1, QUADS - 1, TBL - 1)
                            if k == 0 and q < 3:
                                negmax_transpose(where, b, q + 1)
                            if k == 0 and q == 3 and not last:
                                negmax_transpose(where, b + 1, 0)

                loop(pe, body)
                values_product(QUADS * B - 1, QUADS - 1, TBL - 1)


def experts_phase(nc, x2_rows, w_gT, w_13T, w_2T, bias, out_rows):
    GROUPS, GT, HID = x2_rows.shape
    E = w_gT.shape[1]
    FF = w_2T.shape[1]
    HALVES = 2
    GH = GROUPS // HALVES
    TB = GT // P
    NB = GH * TB
    KT = HID // P
    FT = FF // P
    assert GT == BANK and 2 * FF == BANK and HID == BANK
    UNITS = 2 * GH
    PAIRS = E // 2

    with ExitStack() as ctx:
        def sb(name, shape, dt=F32):
            return ctx.enter_context(nc.sbuf_tensor("c_" + name, shape, dt))

        def psum(name, shape):
            return ctx.enter_context(nc.psum_tensor("c_" + name, shape, F32))

        def sem(name):
            return ctx.enter_context(nc.semaphore("c_" + name))

        acc = sb("acc", [P, NB, HID])
        xT = [sb(f"xT_{s}", [P, KT, GH * GT], F32R) for s in "hl"]
        xn = sb("xn", [P, TB, HID])
        w13 = [[sb(f"w13_{i}{s}", [P, KT, 2 * FF], F32R) for s in "hl"] for i in range(2)]
        w2 = [[sb(f"w2_{i}{s}", [P, FT, HID], F32R) for s in "hl"] for i in range(2)]
        raw13 = sb("raw13", [P, KT, 2 * FF])
        raw2 = sb("raw2", [P, FT, HID])
        wg_raw = sb("wg_raw", [P, KT, E])
        wg = [sb(f"wg_{s}", [P, KT, E], F32R) for s in "hl"]
        bias_b = sb("bias_b", [P, E])
        gate = sb("gate", [P, 2, GT])
        g_full = sb("g_full", [P, 2, GT])
        gT = [sb(f"gT_{s}", [P, 2, FT, GT], F32R) for s in "hl"]
        ident = sb("ident", [P, P])
        minus_half = sb("minus_half", [P, TB])
        stats = sb("stats", [P, TB, 6])
        mv = sb("mv", [P, TB, 2])
        rstd = sb("rstd", [P, TB])
        ez = sb("ez", [P, NB, E])
        sig = sb("sig", [P, NB, E])
        score = sb("score", [P, NB, E])
        rank = sb("rank", [P, NB, E])
        cmp = sb("cmp", [P, NB, E])
        total = sb("total", [P, NB])
        inv = sb("inv", [P, NB])
        weight = sb("weight", [P, NB, E])
        w_now = sb("w_now", [P, 2, NB])

        ps_h = [psum(f"ps_h{i}", [P, BANK]) for i in range(4)]
        ps_y = [psum(f"ps_y{i}", [P, BANK]) for i in range(2)]
        ps_r = psum("ps_r", [P, NB, E])

        consts = sem("consts")
        small_loaded = sem("small_loaded")
        wg_high = sem("wg_high")
        wg_low = sem("wg_low")
        acc_loaded = [sem(f"acc_loaded{g}") for g in range(GH)]
        stored = sem("stored")
        w13_loaded = sem("w13_loaded")
        w2_loaded = sem("w2_loaded")
        w13_high = sem("w13_high")
        w13_low = sem("w13_low")
        w2_high = sem("w2_high")
        w2_low = sem("w2_low")
        stats_done = sem("stats_done")
        aggr_done = sem("aggr_done")
        veps_done = sem("veps_done")
        rstd_done = sem("rstd_done")
        xn_done = sem("xn_done")
        xT_filled = sem("xT_filled")
        xT_high = sem("xT_high")
        xT_low = sem("xT_low")
        logits_done = sem("logits_done")
        ez_done = sem("ez_done")
        route = sem("route")
        w_now_done = sem("w_now_done")
        h_filled = sem("h_filled")
        gate_done = sem("gate_done")
        g_done = sem("g_done")
        g_high = sem("g_high")
        g_low = sem("g_low")
        y_filled = sem("y_filled")
        y_added = sem("y_added")

        def group_rows(rows, g):
            return rows[g].rearrange("(n p) h -> p n h", p=P)

        def pairs(eng, half, body):
            with eng.Fori(half * PAIRS, (half + 1) * PAIRS) as t:
                body(t)

        with nc.Block() as block:
            @block.sync
            def _(sp):
                sp.dma_start(wg_raw[:], w_gT.rearrange("(k p) e -> p k e", p=P)).then_inc(small_loaded, 16)
                sp.dma_start(bias_b[:], bias.to_broadcast([P, E])).then_inc(small_loaded, 16)
                for half in range(HALVES):
                    for g in range(GH):
                        if half:
                            sp.wait_ge(stored, 16 * GH)
                        sp.dma_start(acc[:, g * TB:(g + 1) * TB, :], group_rows(x2_rows, half * GH + g)).then_inc(acc_loaded[g], 16)

                    def body(t):
                        for s in range(2):
                            n = 2 * t + s
                            e = n - half * E
                            wait_alone(sp, w13_low, n + 1, (consts, 3))
                            sp.dma_start(raw13[:], w_13T[e].rearrange("(k p) f -> p k f", p=P)).then_inc(w13_loaded, 16)
                            wait_alone(sp, w2_low, n + 1, (consts, 3))
                            sp.dma_start(raw2[:], w_2T[e].rearrange("(k p) h -> p k h", p=P)).then_inc(w2_loaded, 16)

                    pairs(sp, half, body)
                    sp.wait_ge(y_added, UNITS * TB * PAIRS * (half + 1) + 1)
                    for g in range(GH):
                        sp.dma_start(group_rows(out_rows, half * GH + g), acc[:, g * TB:(g + 1) * TB, :]).then_inc(stored, 16)
                sp.wait_ge(stored, 16 * GROUPS)

            @block.gpsimd
            def _(pool):
                nc.gpsimd.memset(ident[:], 0.0).then_inc(consts, 1)
                nc.gpsimd.memset(minus_half[:], -0.5).then_inc(consts, 1)
                pool.wait_ge(consts, 2)
                nc.gpsimd.affine_select(out=ident[:], in_=ident[:], compare_op=ALU.not_equal, fill=1.0, base=0,
                                        pattern=[[-1, P]], channel_multiplier=1).then_inc(consts, 1)
                for half in range(HALVES):
                    for g in range(GH):
                        G = half * GH + g
                        pool.wait_ge(aggr_done, TB * (G + 1))
                        nc.gpsimd.tensor_scalar(rstd[:], mv[:, :, 1], LN_EPS, None, ALU.add).then_inc(veps_done, 1)
                        pool.wait_ge(veps_done, G + 1)
                        nc.gpsimd.tensor_tensor(rstd[:], rstd[:], minus_half[:], ALU.pow).then_inc(rstd_done, 1)

            @block.scalar
            def _(act):
                def weights(t, s):
                    n = 2 * t + s
                    act.wait_ge(w13_loaded, 16 * (n + 1))
                    nc.scalar.activation(w13[s][0][:], raw13[:], ACT.Copy).then_inc(w13_high, 1)
                    act.wait_ge(w2_loaded, 16 * (n + 1))
                    nc.scalar.activation(w2[s][0][:], raw2[:], ACT.Copy).then_inc(w2_high, 1)

                act.wait_ge(small_loaded, 32)
                nc.scalar.activation(wg[0][:], wg_raw[:], ACT.Copy).then_inc(wg_high, 1)
                for half in range(HALVES):
                    for g in range(GH):
                        for j in range(KT):
                            act.wait_ge(xT_filled, KT * (half * GH + g) + j + 1)
                            nc.scalar.activation(xT[0][:, j, g * GT:(g + 1) * GT], ps_h[j][:], ACT.Copy).then_inc(xT_high, 1)
                    act.wait_ge(logits_done, NB * (half + 1))
                    nc.scalar.activation(ez[:], ps_r[:], ACT.Exp, scale=-1.0).then_inc(ez_done, 1)

                    def body(t):
                        weights(t, 0)
                        for u in range(UNITS):
                            U = UNITS * t + u
                            for f in range(FT):
                                act.wait_ge(h_filled, FT * U + f + 1)
                                nc.scalar.activation(gate[:, f, :], ps_h[2 * f][:], ACT.Silu).then_inc(gate_done, 1)
                                act.wait_ge(g_done, FT * U + f + 1)
                                nc.scalar.activation(gT[0][:, u % 2, f, :], g_full[:, f, :], ACT.Copy).then_inc(g_high, 1)
                            if u == 0:
                                weights(t, 1)

                    pairs(act, half, body)

            @block.vector
            def _(dve):
                steps = [0]

                def then(ins):
                    steps[0] += 1
                    ins.then_inc(route, 1)
                    dve.wait_ge(route, steps[0])

                def weights(t, s):
                    n = 2 * t + s
                    dve.wait_ge(w13_high, n + 1)
                    nc.vector.tensor_tensor(w13[s][1][:], raw13[:], w13[s][0][:].bitcast(F32), ALU.subtract).then_inc(w13_low, 1)
                    dve.wait_ge(w2_high, n + 1)
                    nc.vector.tensor_tensor(w2[s][1][:], raw2[:], w2[s][0][:].bitcast(F32), ALU.subtract).then_inc(w2_low, 1)

                for counted_from_one in (w13_low, w2_low, y_added):
                    dve.sem_inc(counted_from_one, 1)
                dve.wait_ge(wg_high, 1)
                nc.vector.tensor_tensor(wg[1][:], wg_raw[:], wg[0][:].bitcast(F32), ALU.subtract).then_inc(wg_low, 1)
                for half in range(HALVES):
                    for g in range(GH):
                        G = half * GH + g
                        dve.wait_ge(acc_loaded[g], 16 * (half + 1))
                        for n in range(TB):
                            nc.vector.bn_stats(stats[:, n, :], acc[:, g * TB + n, :]).then_inc(stats_done, 1)
                        dve.wait_ge(stats_done, TB * (G + 1))
                        if G:
                            dve.wait_ge(xn_done, G)
                        for n in range(TB):
                            nc.vector.bn_aggr(mv[:, n, :], stats[:, n, :]).then_inc(aggr_done, 1)
                        dve.wait_ge(rstd_done, G + 1)
                        if G:
                            dve.wait_ge(xT_filled, KT * G)
                        for n in range(TB):
                            ins = nc.vector.tensor_scalar(xn[:, n, :], acc[:, g * TB + n, :], mv[:, n, 0:1],
                                                          rstd[:, n:n + 1], ALU.subtract, ALU.mult)
                        ins.then_inc(xn_done, 1)
                        for j in range(KT):
                            dve.wait_ge(xT_high, KT * G + j + 1)
                            cols = slice(g * GT, (g + 1) * GT)
                            nc.vector.tensor_tensor(xT[1][:, j, cols], ps_h[j][:], xT[0][:, j, cols].bitcast(F32),
                                                    ALU.subtract).then_inc(xT_low, 1)

                    dve.wait_ge(ez_done, half + 1)
                    then(nc.vector.tensor_scalar(ez[:], ez[:], 1.0, None, ALU.add))
                    then(nc.vector.reciprocal(sig[:], ez[:]))
                    then(nc.vector.tensor_tensor(score[:], sig[:], bias_b[:, None, :].to_broadcast([P, NB, E]), ALU.add))
                    then(nc.vector.memset(rank[:], 0.0))
                    for e in range(E):
                        mine = score[:, :, e:e + 1]
                        then(nc.vector.tensor_tensor(cmp[:], mine.to_broadcast([P, NB, E]), score[:], ALU.is_gt))
                        then(nc.vector.tensor_tensor(rank[:], rank[:], cmp[:], ALU.add))
                        if e < E - 1:
                            then(nc.vector.tensor_tensor(cmp[:, :, e + 1:], mine.to_broadcast([P, NB, E - 1 - e]),
                                                         score[:, :, e + 1:], ALU.is_equal))
                            then(nc.vector.tensor_tensor(rank[:, :, e + 1:], rank[:, :, e + 1:], cmp[:, :, e + 1:], ALU.add))
                    then(nc.vector.tensor_scalar(cmp[:], rank[:], 1.5, None, ALU.is_lt))
                    then(nc.vector.tensor_tensor(sig[:], sig[:], cmp[:], ALU.mult))
                    then(nc.vector.tensor_reduce(total[:], sig[:], AX.X, ALU.add))
                    then(nc.vector.reciprocal(inv[:], total[:]))
                    then(nc.vector.tensor_tensor(weight[:], sig[:], inv[:, :, None].to_broadcast([P, NB, E]), ALU.mult))

                    def body(t):
                        def add(u):
                            U = UNITS * t + u
                            e = 2 * t + u // GH - half * E
                            g = u % GH
                            for n in range(TB):
                                dve.wait_ge(y_filled, TB * U + n + 1)
                                blk = g * TB + n
                                nc.vector.scalar_tensor_tensor(acc[:, blk, :], ps_y[n % 2][:], w_now[:, u // GH, blk:blk + 1],
                                                               acc[:, blk, :], ALU.mult, ALU.add).then_inc(y_added, 1)

                        weights(t, 0)
                        dve.wait_ge(y_added, TB * UNITS * t + 1)
                        for s in range(2):
                            ins = nc.vector.tensor_copy(w_now[:, s, :], weight[:, :, bass.ds(2 * t + s - half * E, 1)]
                                                        .rearrange("p n o -> p (n o)"))
                        ins.then_inc(w_now_done, 1)
                        dve.wait_ge(w_now_done, t + 1)
                        for u in range(UNITS):
                            U = UNITS * t + u
                            for f in range(FT):
                                dve.wait_ge(gate_done, FT * U + f + 1)
                                if u:
                                    dve.wait_ge(g_low, FT * (U - 1) + f + 1)
                                nc.vector.tensor_tensor(g_full[:, f, :], ps_h[2 * f + 1][:], gate[:, f, :],
                                                        ALU.mult).then_inc(g_done, 1)
                            for f in range(FT):
                                dve.wait_ge(g_high, FT * U + f + 1)
                                nc.vector.tensor_tensor(gT[1][:, u % 2, f, :], g_full[:, f, :],
                                                        gT[0][:, u % 2, f, :].bitcast(F32), ALU.subtract).then_inc(g_low, 1)
                            if u:
                                add(u - 1)
                            if u == 0:
                                weights(t, 1)
                        add(UNITS - 1)

                    pairs(dve, half, body)

            @block.tensor
            def _(pe):
                PASSES = ((0, 0), (0, 1), (1, 0))
                pe.wait_ge(consts, 3)
                pe.wait_ge(wg_low, 1)
                for half in range(HALVES):
                    for g in range(GH):
                        G = half * GH + g
                        pe.wait_ge(xn_done, G + 1)
                        for j in range(KT):
                            if G:
                                pe.wait_ge(xT_low, KT * (G - 1) + j + 1)
                            if half and g == 0 and j == 0:
                                pe.wait_ge(g_done, FT * UNITS * PAIRS * half)
                            for n in range(TB):
                                ins = nc.tensor.transpose(ps_h[j][:, n * P:(n + 1) * P], xn[:, n, j * P:(j + 1) * P], ident[:])
                            ins.then_inc(xT_filled, 1)
                    pe.wait_ge(xT_low, KT * GH * (half + 1))
                    if half:
                        pe.wait_ge(ez_done, half)
                    for b in range(NB):
                        for j in range(KT):
                            for i, (a, c) in enumerate(PASSES):
                                ins = nc.tensor.matmul(ps_r[:, b, :], xT[a][:, j, b * P:(b + 1) * P], wg[c][:, j, :],
                                                       start=(j == 0 and i == 0), stop=(j == KT - 1 and i == 2))
                        ins.then_inc(logits_done, 1)

                    def body(t):
                        def up(u):
                            s, g = u // GH, u % GH
                            U = UNITS * t + u
                            if g == 0:
                                pe.wait_ge(w13_low, 2 * t + s + 2)
                            for f in range(FT):
                                if not (u == 0):
                                    pe.wait_ge(g_done, FT * (U - 1) + f + 1)
                                for which in range(2):
                                    c0 = which * FF + f * P
                                    for j in range(KT):
                                        for i, (a, c) in enumerate(PASSES):
                                            ins = nc.tensor.matmul(ps_h[2 * f + which][:], w13[s][a][:, j, c0:c0 + P],
                                                                   xT[c][:, j, g * GT:(g + 1) * GT],
                                                                   start=(j == 0 and i == 0), stop=(j == KT - 1 and i == 2))
                                ins.then_inc(h_filled, 1)

                        def down(u):
                            s = u // GH
                            U = UNITS * t + u
                            if u % GH == 0:
                                pe.wait_ge(w2_low, 2 * t + s + 2)
                            pe.wait_ge(g_low, FT * (U + 1))
                            for n in range(TB):
                                if n < 2 and u == 0:
                                    pe.wait_ge(y_added, TB * U + 1)
                                else:
                                    pe.wait_ge(y_added, TB * U + n)
                                for f in range(FT):
                                    for i, (a, c) in enumerate(PASSES):
                                        ins = nc.tensor.matmul(ps_y[n % 2][:], gT[a][:, u % 2, f, n * P:(n + 1) * P],
                                                               w2[s][c][:, f, :], start=(f == 0 and i == 0),
                                                               stop=(f == FT - 1 and i == 2))
                                ins.then_inc(y_filled, 1)

                        for u in range(UNITS):
                            up(u)
                            if u:
                                down(u - 1)
                        down(UNITS - 1)

                    pairs(pe, half, body)


def decoder_layer(nc, x, context, mask, mask_cols, a_wq, a_wkv, a_wd, x_wq, x_bq, x_wk, x_bk, x_wv, x_bv,
                  f_wg, f_w13, f_w2, f_bias, out):
    B, S, H = x.shape
    GROUPS = 4
    HEADS = a_wq.shape[1] // P
    x1 = nc.dram_tensor("x1", [B, S, H], F32, kind="Internal").ap()
    x2 = nc.dram_tensor("x2", [B, S, H], F32, kind="Internal").ap()
    aux = nc.dram_tensor("mask_rows_split", [B, 6, 2, H], F32, kind="Internal").ap()
    rinv = nc.dram_tensor("row_sum_inverses", [4, 4 * H], F32, kind="Internal").ap()

    def by_512(t):
        return t.rearrange("(g b) s h -> g (b s) h", b=BANK // S)

    attention_phase(nc, by_512(x), a_wq, a_wkv, a_wd, by_512(x1), B * S, H, S, HEADS, GROUPS)
    cross_attention_phase(nc, x1, context, mask, mask_cols, x_wq, x_bq, x_wk, x_bk, x_wv, x_bv, aux, rinv, x2)
    experts_phase(nc, by_512(x2), f_wg, f_w13, f_w2, f_bias, by_512(out))


def kernel(**inputs):
    import numpy as np
    import concourse.bacc as bacc
    from concourse.bass_utils import run_bass_kernel_spmd

    a = {name: np.asarray(value) for name, value in inputs.items()}
    B, S, H = a["x"].shape
    C = a["L0_xattn_Wq"].shape[0]
    mask = a["mask_Bx1x2048_fk1"].reshape(B, H)

    def by_quads(w):
        return w.reshape(4, 4, 16, -1).transpose(0, 2, 1, 3).reshape(C, -1)

    laid = {
        "x": a["x"],
        "context": a["ctx_2048"],
        "mask": mask,
        "mask_cols": mask.reshape(B, H // 128, 128).transpose(0, 2, 1),
        "a_wq": a["L0_attn_w_q"],
        "a_wkv": a["L0_attn_w_kv"],
        "a_wd": a["L0_attn_w_dense"],
        "x_wq": by_quads(a["L0_xattn_Wq"]).T,
        "x_bq": by_quads(a["L0_xattn_bq"]).reshape(C // 128, 128).T,
        "x_wk": by_quads(a["L0_xattn_Wk"]).T,
        "x_bk": by_quads(a["L0_xattn_bk"]).reshape(C // 128, 128).T,
        "x_wv": a["L0_xattn_Wv"].T,
        "x_bv": a["L0_xattn_bv"].reshape(1, C),
        "f_wg": a["L0_ffn_Wg"].T,
        "f_w13": np.concatenate([a["L0_ffn_W1"], a["L0_ffn_W3"]], axis=1).transpose(0, 2, 1),
        "f_w2": a["L0_ffn_W2"].transpose(0, 2, 1),
        "f_bias": a["L0_ffn_bias"].reshape(1, -1),
    }
    nc = bacc.Bacc("TRN2", target_bir_lowering=False, num_devices=1)
    arrays = {f"in_{name}": np.ascontiguousarray(value) for name, value in laid.items()}
    args = [nc.dram_tensor(f"in_{name}", list(arrays[f"in_{name}"].shape), F32, kind="ExternalInput").ap() for name in laid]
    out = nc.dram_tensor("out", [B, S, H], F32, kind="ExternalOutput").ap()
    decoder_layer(nc, *args, out)
    r = run_bass_kernel_spmd(nc, [arrays], core_ids=[0])
    return r.results[0]["out"]
```

```python
from contextlib import ExitStack

import concourse.bass as bass
from concourse import mybir

F32 = mybir.dt.float32
F32R = mybir.dt.float32r
BF16 = mybir.dt.bfloat16
I32 = mybir.dt.int32
ACT = mybir.ActivationFunctionType
ALU = mybir.AluOpType
AX = mybir.AxisListType

P = 128
BANK = 512
LN_EPS = 1e-5


def wait_alone(eng, sem, value, past):
    if not isinstance(value, int):
        value = eng.to_reg(value)
    eng.wait_ge(*past)
    eng.wait_ge(sem, value)


def attention_phase(nc, x_rows, w_q, w_kv, w_dense, x1_rows, TOKENS, HIDDEN, SEQ, HEADS, GROUPS):
    D = P
    HALVES = 2
    G = GROUPS // HALVES
    HPG = HEADS // GROUPS
    NH = G * HPG
    TB = BANK // P
    KT = HIDDEN // P
    PAIRS = TOKENS // BANK
    UNITS = 2 * NH
    SCALE = float(D) ** -0.5
    FILLS = 16
    assert SEQ == 2 * P and FILLS == KT + G + TB // 2 + NH
    QW, KVW = NH * D, 2 * G * D
    NEG = -1.0e30

    with ExitStack() as ctx:
        def sb(name, shape, dt=F32):
            return ctx.enter_context(nc.sbuf_tensor(name, shape, dt))

        def psum(name, shape):
            return ctx.enter_context(nc.psum_tensor(name, shape, F32))

        def sem(name):
            return ctx.enter_context(nc.semaphore("a_" + name))

        wq = [sb(f"wq_{s}", [P, KT, QW], F32R) for s in "hl"]
        wkv = [sb(f"wkv_{s}", [P, KT, KVW], F32R) for s in "hl"]
        wd = [sb(f"wd_{s}", [P, NH, HIDDEN], F32R) for s in "hl"]
        x_in = sb("x_in", [P, TB, HIDDEN])
        acc = sb("acc", [P, TB, HIDDEN])
        xn = sb("xn", [P, TB, HIDDEN])
        xT = [sb(f"xT_{s}", [P, KT, BANK], F32R) for s in "hl"]
        kT = [sb(f"kT_{s}", [P, G, BANK], F32R) for s in "hl"]
        v = [sb(f"v_{s}", [P, TB, G * D], F32R) for s in "hl"]
        qT = [sb(f"qT_{s}", [P, 2, BANK], F32R) for s in "hl"]
        probs = sb("probs", [P, 2, 3 * P])
        pT = [sb(f"pT_{s}", [P, 2, 3 * P], F32R) for s in "hl"]
        cT = [sb(f"cT_{s}", [P, G, HPG, BANK], F32R) for s in "hl"]
        ident = sb("ident", [P, P])
        ident_b = sb("ident_b", [P, P], BF16)
        causal = sb("causal", [P, P], BF16)
        stats = sb("stats", [P, TB, 6])
        mv = sb("mv", [P, TB, 2])
        veps = sb("veps", [P, TB])
        rstd = sb("rstd", [P, TB])
        minus_half = sb("minus_half", [P, TB])
        negmax = sb("negmax", [P, 2, 2])
        rowsum = sb("rowsum", [P, 2, 2])
        rinv = sb("rinv", [P, 2, 2])

        ps_proj = [psum(f"ps_proj{i}", [P, BANK]) for i in range(2)]
        ps_s = [psum(f"ps_s{i}", [P, BANK]) for i in range(2)]
        ps_pT = [psum(f"ps_pT{i}", [P, BANK]) for i in range(2)]
        ps_c = psum("ps_c", [P, BANK])
        ps_d = psum("ps_d", [P, BANK])

        consts = sem("consts")
        w_loaded = [sem("w_loaded0"), sem("w_loaded1")]
        w_high = sem("w_high")
        w_low = sem("w_low")
        x_loaded = sem("x_loaded")
        acc_loaded = sem("acc_loaded")
        stored = sem("stored")
        stats_done = sem("stats_done")
        aggr_done = sem("aggr_done")
        veps_done = sem("veps_done")
        rstd_done = sem("rstd_done")
        xn_done = sem("xn_done")
        proj_filled = sem("proj_filled")
        proj_high = sem("proj_high")
        proj_low = sem("proj_low")
        s_filled = sem("s_filled")
        max_done = sem("max_done")
        exp_done = sem("exp_done")
        rinv_done = sem("rinv_done")
        probs_done = sem("probs_done")
        pT_filled = sem("pT_filled")
        pT_high = sem("pT_high")
        pT_low = sem("pT_low")
        c_filled = sem("c_filled")
        c_high = sem("c_high")
        c_low = sem("c_low")
        d_filled = sem("d_filled")
        d_added = sem("d_added")

        def tokens(rows, pair):
            return rows[pair].rearrange("(n p) h -> p n h", p=P)

        CH = TB * HIDDEN

        def chunks(half):
            out = []
            for kt0 in range(0, KT, CH // QW):
                out.append(([w[:, kt0:kt0 + CH // QW, :] for w in wq],
                            w_q[kt0 * P:(kt0 + CH // QW) * P, half * QW:(half + 1) * QW]
                            .rearrange("(k p) e -> p k e", p=P)))
            for part in range(2):
                out.append(([w[:, :, part * G * D:(part + 1) * G * D] for w in wkv],
                            w_kv[:, (part * GROUPS + half * G) * D:(part * GROUPS + half * G + G) * D]
                            .rearrange("(k p) e -> p k e", p=P)))
            for h0 in range(0, NH, TB):
                r0 = (half * NH + h0) * D
                out.append(([w[:, h0:h0 + TB, :] for w in wd],
                            w_dense[r0:r0 + TB * D, :].rearrange("(k p) e -> p k e", p=P)))
            return out

        NCH = len(chunks(0))
        stage = [x_in, xn]

        def staged(n, like):
            flat = stage[n % 2][:, :, :].rearrange("p n h -> p (n h)")
            k, e = like.shape[1], like.shape[2]
            return flat[:, 0:k * e].rearrange("p (k e) -> p k e", k=k)

        def pairs(eng, half, body):
            with eng.Fori(half * PAIRS, (half + 1) * PAIRS - 1) as t:
                body(t, False)
            body((half + 1) * PAIRS - 1, True)

        with nc.Block() as block:
            @block.sync
            def _(sp):
                sp.sem_inc(stored, 16)
                for half in range(HALVES):
                    x_base = half * PAIRS
                    for n, ((high, _low), src) in enumerate(chunks(half)):
                        N = half * NCH + n
                        if n >= 2:
                            sp.wait_ge(w_low, N - 1)
                        elif half:
                            sp.wait_ge(proj_low, FILLS * PAIRS)
                            sp.wait_ge(xn_done, half * PAIRS)
                        sp.dma_start(staged(n, high), src).then_inc(w_loaded[n % 2], 16)
                    sp.wait_ge(w_low, (half + 1) * NCH)
                    sp.dma_start(x_in[:], tokens(x_rows, 0)).then_inc(x_loaded, 16)

                    def body(t, last):
                        if not last:
                            wait_alone(sp, xn_done, t + 1, (consts, 6))
                            sp.dma_start(x_in[:], tokens(x_rows, t + 1 - x_base)).then_inc(x_loaded, 16)
                        wait_alone(sp, stored, 16 * (t + 1), (consts, 6))
                        rows = x_rows if half == 0 else x1_rows
                        sp.dma_start(acc[:], tokens(rows, t - x_base)).then_inc(acc_loaded, 16)
                        wait_alone(sp, d_added, G * TB * (t + 1) + 1, (consts, 6))
                        sp.dma_start(tokens(x1_rows, t - x_base), acc[:]).then_inc(stored, 16)

                    pairs(sp, half, body)
                sp.wait_ge(stored, 16 * (HALVES * PAIRS + 1))

            @block.gpsimd
            def _(pool):
                nc.gpsimd.memset(ident[:], 0.0).then_inc(consts, 1)
                nc.gpsimd.memset(causal[:], 0.0).then_inc(consts, 1)
                nc.gpsimd.memset(minus_half[:], -0.5).then_inc(consts, 1)
                pool.wait_ge(consts, 3)
                nc.gpsimd.affine_select(out=ident[:], in_=ident[:], compare_op=ALU.not_equal, fill=1.0, base=0,
                                        pattern=[[-1, P]], channel_multiplier=1).then_inc(consts, 1)
                nc.gpsimd.affine_select(out=causal[:], in_=causal[:], compare_op=ALU.is_ge, fill=NEG, base=0,
                                        pattern=[[-1, P]], channel_multiplier=1).then_inc(consts, 1)
                pool.wait_ge(consts, 5)
                nc.gpsimd.tensor_copy(ident_b[:], ident[:]).then_inc(consts, 1)

                def norm_scale(t):
                    wait_alone(pool, aggr_done, TB * (t + 1), (consts, 6))
                    nc.gpsimd.tensor_scalar(veps[:], mv[:, :, 1], LN_EPS, None, ALU.add).then_inc(veps_done, 1)
                    pool.wait_ge(veps_done, t + 1)
                    nc.gpsimd.tensor_tensor(veps[:], veps[:], minus_half[:], ALU.pow).then_inc(rstd_done, 1)

                for half in range(HALVES):
                    norm_scale(half * PAIRS)

                    def body(t, last):
                        for u in range(UNITS):
                            U = UNITS * t + u
                            s = u % 2
                            wait_alone(pool, rinv_done, U + 1, (consts, 6))
                            nc.gpsimd.tensor_scalar(probs[:, s, 0:P], probs[:, s, 0:P], rinv[:, s, 0:1], None, ALU.mult)
                            nc.gpsimd.tensor_scalar(probs[:, s, P:3 * P], probs[:, s, P:3 * P], rinv[:, s, 1:2], None,
                                                    ALU.mult).then_inc(probs_done, 1)
                            if u == 4 and not last:
                                norm_scale(t + 1)

                    pairs(pool, half, body)

            @block.scalar
            def _(act):
                def prologue(t):
                    for j in range(KT):
                        act.wait_ge(proj_filled, FILLS * t + j + 1)
                        nc.scalar.activation(xT[0][:, j, :], ps_proj[j % 2][:], ACT.Copy).then_inc(proj_high, 1)
                    for g in range(G):
                        act.wait_ge(proj_filled, FILLS * t + KT + g + 1)
                        nc.scalar.activation(kT[0][:, g, :], ps_proj[g % 2][:], ACT.Copy).then_inc(proj_high, 1)

                def values(t):
                    for n in range(2):
                        act.wait_ge(proj_filled, FILLS * t + KT + G + n + 1)
                        nc.scalar.activation(v[0][:, 2 * n:2 * n + 2, :], ps_proj[n % 2][:], ACT.Copy).then_inc(proj_high, 1)

                def query(t, m):
                    act.wait_ge(proj_filled, FILLS * t + 8 + m + 1)
                    nc.scalar.activation(qT[0][:, m % 2, :], ps_proj[m % 2][:], ACT.Copy, scale=SCALE).then_inc(proj_high, 1)

                def probs_transposed(t, u):
                    act.wait_ge(pT_filled, UNITS * t + u + 1)
                    nc.scalar.activation(pT[0][:, u % 2, :], ps_pT[u % 2][:, 0:3 * P], ACT.Copy).then_inc(pT_high, 1)

                def context(t, n):
                    act.wait_ge(c_filled, NH * t + n + 1)
                    nc.scalar.activation(cT[0][:, n // HPG, n % HPG, :], ps_c[:], ACT.Copy).then_inc(c_high, 1)

                for half in range(HALVES):
                    for n, ((high, _low), _src) in enumerate(chunks(half)):
                        N = half * NCH + n
                        if half and n == NCH - NH // TB:
                            act.wait_ge(d_filled, G * TB * PAIRS)
                        act.wait_ge(w_loaded[n % 2], 16 * (half * ((NCH + 1 - n % 2) // 2) + n // 2 + 1))
                        nc.scalar.activation(high, staged(n, high), ACT.Copy).then_inc(w_high, 1)
                    prologue(half * PAIRS)
                    values(half * PAIRS)

                    def body(t, last):
                        query(t, 0)
                        for u in range(UNITS):
                            U = UNITS * t + u
                            s = u % 2
                            if u >= 1:
                                probs_transposed(t, u - 1)
                            act.wait_ge(max_done, U + 1)
                            nc.scalar.activation(probs[:, s, 0:P], ps_s[s][:, 0:P], ACT.Exp, bias=negmax[:, s, 0:1],
                                                 accum_out=rowsum[:, s, 0:1])
                            nc.scalar.activation(probs[:, s, P:3 * P], ps_s[s][:, P:3 * P], ACT.Exp,
                                                 bias=negmax[:, s, 1:2], accum_out=rowsum[:, s, 1:2]).then_inc(exp_done, 1)
                            if u % 2 == 0 and u // 2 + 1 < NH:
                                query(t, u // 2 + 1)
                            if u % 2 == 1 and u >= 3:
                                context(t, (u - 3) // 2)
                        if not last:
                            for j in range(KT):
                                act.wait_ge(proj_filled, FILLS * (t + 1) + j + 1)
                                nc.scalar.activation(xT[0][:, j, :], ps_proj[j % 2][:], ACT.Copy).then_inc(proj_high, 1)
                        probs_transposed(t, UNITS - 1)
                        if not last:
                            for g in range(G):
                                act.wait_ge(proj_filled, FILLS * (t + 1) + KT + g + 1)
                                nc.scalar.activation(kT[0][:, g, :], ps_proj[g % 2][:], ACT.Copy).then_inc(proj_high, 1)
                        context(t, NH - 1)
                        if not last:
                            values(t + 1)

                    pairs(act, half, body)

            @block.vector
            def _(dve):
                def low(dst, ps, h):
                    return nc.vector.tensor_tensor(dst, ps, h.bitcast(F32), ALU.subtract)

                def normalise(t):
                    dve.wait_ge(x_loaded, 16 * (t + 1))
                    for n in range(TB):
                        nc.vector.bn_stats(stats[:, n, :], x_in[:, n, :]).then_inc(stats_done, 1)
                    wait_alone(dve, stats_done, TB * (t + 1), (consts, 6))
                    for n in range(TB):
                        nc.vector.bn_aggr(mv[:, n, :], stats[:, n, :]).then_inc(aggr_done, 1)

                def apply_norm(t):
                    dve.wait_ge(rstd_done, t + 1)
                    for n in range(TB):
                        ins = nc.vector.tensor_scalar(xn[:, n, :], x_in[:, n, :], mv[:, n, 0:1], veps[:, n:n + 1],
                                                      ALU.subtract, ALU.mult)
                    ins.then_inc(xn_done, 1)

                def xT_low(t):
                    for j in range(KT):
                        dve.wait_ge(proj_high, FILLS * t + j + 1)
                        low(xT[1][:, j, :], ps_proj[j % 2][:], xT[0][:, j, :]).then_inc(proj_low, 1)

                def k_low(t):
                    for g in range(G):
                        dve.wait_ge(proj_high, FILLS * t + KT + g + 1)
                        low(kT[1][:, g, :], ps_proj[g % 2][:], kT[0][:, g, :]).then_inc(proj_low, 1)

                def v_low(t, n):
                    dve.wait_ge(proj_high, FILLS * t + KT + G + n + 1)
                    src = v[0][:, 2 * n:2 * n + 2, :].rearrange("p a b -> p (a b)")
                    dst = v[1][:, 2 * n:2 * n + 2, :].rearrange("p a b -> p (a b)")
                    low(dst, ps_proj[n % 2][:], src).then_inc(proj_low, 1)

                def q_low(t, m):
                    dve.wait_ge(proj_high, FILLS * t + 8 + m + 1)
                    nc.vector.scalar_tensor_tensor(qT[1][:, m % 2, :], ps_proj[m % 2][:], SCALE,
                                                   qT[0][:, m % 2, :].bitcast(F32), ALU.mult,
                                                   ALU.subtract).then_inc(proj_low, 1)

                def pT_low_part(t, u):
                    dve.wait_ge(pT_high, UNITS * t + u + 1)
                    low(pT[1][:, u % 2, :], ps_pT[u % 2][:, 0:3 * P], pT[0][:, u % 2, :]).then_inc(pT_low, 1)

                def c_low_part(t, n):
                    dve.wait_ge(c_high, NH * t + n + 1)
                    low(cT[1][:, n // HPG, n % HPG, :], ps_c[:], cT[0][:, n // HPG, n % HPG, :]).then_inc(c_low, 1)

                def add_dense(t, g, n):
                    if g == 0 and n == 0:
                        dve.wait_ge(acc_loaded, 16 * (t + 1))
                    dve.wait_ge(d_filled, TB * (G * t + g) + n + 1)
                    nc.vector.tensor_tensor(acc[:, n, :], ps_d[:], acc[:, n, :], ALU.add).then_inc(d_added, 1)

                dve.sem_inc(c_low, 1)
                dve.sem_inc(d_added, 1)
                for half in range(HALVES):
                    for n, ((high, lowp), _src) in enumerate(chunks(half)):
                        dve.wait_ge(w_high, half * NCH + n + 1)
                        nc.vector.tensor_tensor(lowp, staged(n, high), high.bitcast(F32), ALU.subtract).then_inc(w_low, 1)
                    t0 = half * PAIRS
                    normalise(t0)
                    apply_norm(t0)
                    xT_low(t0)
                    k_low(t0)
                    for n in range(2):
                        v_low(t0, n)

                    def body(t, last):
                        q_low(t, 0)
                        for u in range(UNITS):
                            U = UNITS * t + u
                            s = u % 2
                            dve.wait_ge(s_filled, U + 1)
                            nc.vector.tensor_reduce(negmax[:, s, 0:1], ps_s[s][:, 0:P], AX.X, ALU.max, negate=True)
                            nc.vector.tensor_reduce(negmax[:, s, 1:2], ps_s[s][:, P:3 * P], AX.X, ALU.max,
                                                    negate=True).then_inc(max_done, 1)
                            if u >= 1:
                                pT_low_part(t, u - 1)
                            dve.wait_ge(exp_done, U + 1)
                            nc.vector.reciprocal(rinv[:, s, :], rowsum[:, s, :]).then_inc(rinv_done, 1)
                            if u % 2 == 0 and u // 2 + 1 < NH:
                                q_low(t, u // 2 + 1)
                            if u % 2 == 1 and u >= 3:
                                c_low_part(t, (u - 3) // 2)
                            if UNITS - 5 <= u < UNITS - 1:
                                add_dense(t, 0, u - (UNITS - 5))
                            if u == 3 and not last:
                                normalise(t + 1)
                            if u == 6 and not last:
                                apply_norm(t + 1)
                        if not last:
                            xT_low(t + 1)
                        pT_low_part(t, UNITS - 1)
                        if not last:
                            k_low(t + 1)
                        c_low_part(t, NH - 1)
                        if not last:
                            v_low(t + 1, 0)
                        add_dense(t, 1, 0)
                        if not last:
                            v_low(t + 1, 1)
                        for n in range(1, TB):
                            add_dense(t, 1, n)

                    pairs(dve, half, body)

            @block.tensor
            def _(pe):
                def product3(out, w, w_at, m, m_at, first=True, last=True):
                    for a, b, st, en in ((0, 0, first, False), (0, 1, False, False), (1, 0, False, last)):
                        ins = nc.tensor.matmul(out, w[a][w_at], m[b][m_at], start=st, stop=en)
                    return ins

                def bank_free(F):
                    if isinstance(F, int) and F < 2:
                        return
                    pe.wait_ge(proj_low, F - 1)

                def xT_fill(t):
                    pe.wait_ge(xn_done, t + 1)
                    for j in range(KT):
                        bank_free(FILLS * t + j)
                        for n in range(TB):
                            ins = nc.tensor.transpose(ps_proj[j % 2][:, n * P:(n + 1) * P], xn[:, n, j * P:(j + 1) * P], ident[:])
                        ins.then_inc(proj_filled, 1)

                def k_fill(t):
                    pe.wait_ge(proj_low, FILLS * t + KT)
                    for g in range(G):
                        bank_free(FILLS * t + KT + g)
                        for kt in range(KT):
                            ins = product3(ps_proj[g % 2][:], wkv, (slice(None), kt, slice(g * D, (g + 1) * D)),
                                           xT, (slice(None), kt, slice(None)), kt == 0, kt == KT - 1)
                        ins.then_inc(proj_filled, 1)

                def v_fill(t, n):
                    bank_free(FILLS * t + KT + G + n)
                    for i in range(2):
                        blk = 2 * n + i
                        for kt in range(KT):
                            ins = product3(ps_proj[n % 2][:, i * G * D:(i + 1) * G * D],
                                           xT, (slice(None), kt, slice(blk * P, (blk + 1) * P)),
                                           wkv, (slice(None), kt, slice(G * D, 2 * G * D)), kt == 0, kt == KT - 1)
                    ins.then_inc(proj_filled, 1)

                def q_fill(t, m, part):
                    if part == 0:
                        bank_free(FILLS * t + 8 + m)
                    for kt in range(part * KT // 2, (part + 1) * KT // 2):
                        ins = product3(ps_proj[m % 2][:], wq, (slice(None), kt, slice(m * D, (m + 1) * D)),
                                       xT, (slice(None), kt, slice(None)), kt == 0, kt == KT - 1)
                    if part == 1:
                        ins.then_inc(proj_filled, 1)

                def scores(t, u):
                    m, b = u // 2, u % 2
                    g, s = m // HPG, u % 2
                    if b == 0:
                        pe.wait_ge(proj_low, FILLS * t + 8 + m + 1)
                    for qb in range(2):
                        c0, n = qb * P, (qb + 1) * P
                        q0 = b * SEQ + qb * P
                        product3(ps_s[s][:, c0:c0 + n], qT, (slice(None), m % 2, slice(q0, q0 + P)),
                                 kT, (slice(None), g, slice(b * SEQ, b * SEQ + n)), True, False)
                        ins = nc.tensor.matmul(ps_s[s][:, c0 + n - P:c0 + n], ident_b[:], causal[:], start=False, stop=True)
                    ins.then_inc(s_filled, 1)

                def transposes(t, u):
                    s = u % 2
                    pe.wait_ge(probs_done, UNITS * t + u + 1)
                    for j in range(3):
                        ins = nc.tensor.transpose(ps_pT[s][:, j * P:(j + 1) * P], probs[:, s, j * P:(j + 1) * P], ident[:])
                    ins.then_inc(pT_filled, 1)

                def values_product(t, u):
                    m, b = u // 2, u % 2
                    g, s = m // HPG, u % 2
                    pe.wait_ge(pT_low, UNITS * t + u + 1)
                    if b == 0:
                        pe.wait_ge(c_low, NH * t + m + 1)
                    vs = slice(g * D, (g + 1) * D)
                    product3(ps_c[:, b * SEQ:(b + 1) * SEQ], v, (slice(None), 2 * b, vs),
                             pT, (slice(None), s, slice(0, 2 * P)), True, False)
                    ins = product3(ps_c[:, b * SEQ + P:(b + 1) * SEQ], v, (slice(None), 2 * b + 1, vs),
                                   pT, (slice(None), s, slice(2 * P, 3 * P)), False, True)
                    if b == 1:
                        ins.then_inc(c_filled, 1)

                def dense(t, g, n):
                    if n == 0:
                        pe.wait_ge(c_low, NH * t + (g + 1) * HPG + 1)
                    pe.wait_ge(d_added, TB * (G * t + g) + n + 1)
                    for j in range(HPG):
                        ins = product3(ps_d[:], cT, (slice(None), g, j, slice(n * P, (n + 1) * P)),
                                       wd, (slice(None), g * HPG + j, slice(None)), j == 0, j == HPG - 1)
                    ins.then_inc(d_filled, 1)

                pe.wait_ge(consts, 6)
                for half in range(HALVES):
                    t0 = half * PAIRS
                    xT_fill(t0)
                    pe.wait_ge(w_low, (half + 1) * NCH)
                    k_fill(t0)
                    for n in range(2):
                        v_fill(t0, n)

                    def body(t, last):
                        for part in range(2):
                            q_fill(t, 0, part)
                        q_fill(t, 1, 0)
                        for u in range(UNITS):
                            scores(t, u)
                            if u % 2 == 0 and u // 2 + 1 < NH:
                                q_fill(t, u // 2 + 1, 1)
                            if u % 2 == 1 and u // 2 + 2 < NH:
                                q_fill(t, u // 2 + 2, 0)
                            if u >= 1:
                                transposes(t, u - 1)
                            if u >= 2:
                                values_product(t, u - 2)
                            if UNITS - 5 <= u < UNITS - 1:
                                dense(t, 0, u - (UNITS - 5))
                        if not last:
                            xT_fill(t + 1)
                        values_product(t, UNITS - 2)
                        transposes(t, UNITS - 1)
                        if not last:
                            k_fill(t + 1)
                        values_product(t, UNITS - 1)
                        if not last:
                            v_fill(t + 1, 0)
                        dense(t, 1, 0)
                        if not last:
                            v_fill(t + 1, 1)
                        for n in range(1, TB):
                            dense(t, 1, n)

                    pairs(pe, half, body)


def cross_attention_phase(nc, x1_seq, context_seq, mask, mask_cols, w_qT, b_q, w_kT, b_k, w_vT, b_v, aux_dram, rinv_dram, x2_seq):
    B, C, T = x1_seq.shape
    DH = 16
    HQ = 4
    QUADS = C // (DH * HQ)
    CT = C // P
    TBL = T // P
    AUX, AUXROWS = 3 * DH, 6
    MAXROW = 96
    NEG4 = -4.0e6
    AUX_STEPS = 11
    TC = T // 32
    FILLS = 10
    PRO = 7
    assert T == BANK and DH == 16 and QUADS == 4 and CT == 2

    with ExitStack() as ctx:
        def sb(name, shape, dt=F32):
            return ctx.enter_context(nc.sbuf_tensor("b_" + name, shape, dt))

        def psum(name, shape):
            return ctx.enter_context(nc.psum_tensor("b_" + name, shape, F32))

        def sem(name):
            return ctx.enter_context(nc.semaphore("b_" + name))

        stack = sb("stack", [P, QUADS, 2, HQ, T], F32R)
        probs = sb("probs", [P, 2, HQ, T])
        v_stack = sb("v_stack", [P, TBL, C // DH, 32])
        v_raw = sb("v_raw", [P, TBL, C])
        w = {n: [sb(f"w{n}_{s}", [P, CT, C], F32R) for s in "hl"] for n in "qkv"}
        w_stage = sb("w_stage", [P, 3, CT, C])
        bias = {n: sb(f"bias_{n}", [P, CT]) for n in "qk"}
        bias_v = sb("bias_v", [P, C])
        x_in = sb("x_in", [P, CT, T])
        c_in = sb("c_in", [P, CT, T])
        xn = sb("xn", [P, CT, T])
        xs = [sb(f"x_{s}", [P, CT, T], F32R) for s in "hl"]
        cs = [sb(f"c_{s}", [P, CT, T], F32R) for s in "hl"]
        raw = {n: sb(f"raw_{n}", [P, T]) for n in "qk"}
        tile = {n: [[sb(f"{n}{half}_{s}", [P, T], F32R) for s in "hl"] for half in range(2)] for n in "qk"}
        mask_b = sb("mask_b", [P, T])
        mask_col = sb("mask_col", [P, TBL])
        mask_r = sb("mask_r", [P, TC])
        mask_rows, one_minus, neg_row = (probs[0:B, 0, i, :] for i in range(3))
        stats = sb("stats", [P, CT, 6])
        mv = sb("mv", [P, CT, 2])
        rstd = sb("rstd", [P, CT])
        minus_half = sb("minus_half", [P, CT])
        ident = sb("ident", [P, P])
        negmax = sb("negmax", [P, TBL, HQ])
        nm_split = sb("nm_split", [P, TBL, 2, HQ])
        nm_rows = sb("nm_rows", [2 * HQ, T])
        o_sb = sb("o_sb", [P, QUADS, T])
        sums = sb("sums", [P, TC])
        rsum = sb("rsum", [P, TC])
        r_out = sb("r_out", [P, TC])
        out_tiles = sb("out_tiles", [P, 3, QUADS, T])
        r_b, x_res, y = (out_tiles[:, i, :, :] for i in range(3))
        aux = out_tiles[0:B].rearrange("b i q t -> b (i q t)").rearrange("b (r s t) -> b r s t", r=AUXROWS, s=2)
        assert 3 * QUADS == 2 * AUXROWS

        ps_e = [psum(f"ps_e{i}", [P, 2, BANK]) for i in range(2)]
        ps_m = [psum(f"ps_m{i}", [P, BANK]) for i in range(3)]
        ps_o = psum("ps_o", [P, BANK])

        consts = sem("consts")
        w_loaded = sem("w_loaded")
        w_high = sem("w_high")
        w_low = sem("w_low")
        mrow_loaded = sem("mrow_loaded")
        aux_step = sem("aux_step")
        aux_stored = sem("aux_stored")
        xc_loaded = sem("xc_loaded")
        mask_b_loaded = sem("mask_b_loaded")
        mask_col_loaded = sem("mask_col_loaded")
        mask_r_loaded = sem("mask_r_loaded")
        stats_done = sem("stats_done")
        aggr_done = sem("aggr_done")
        veps_done = sem("veps_done")
        rstd_done = sem("rstd_done")
        xn_done = sem("xn_done")
        xs_high = sem("xs_high")
        xs_low = sem("xs_low")
        cs_high = sem("cs_high")
        cs_low = sem("cs_low")
        proj_filled = sem("proj_filled")
        raw_done = sem("raw_done")
        tile_high = sem("tile_high")
        tile_low = sem("tile_low")
        v_done = sem("v_done")
        vbias_done = sem("vbias_done")
        stacked = [sem(f"stacked{q}") for q in range(QUADS)]
        m_filled = sem("m_filled")
        m_reduced = sem("m_reduced")
        nm_high = sem("nm_high")
        nm_low = sem("nm_low")
        nm_rows_done = sem("nm_rows_done")
        nm_stacked = sem("nm_stacked")
        e_filled = sem("e_filled")
        e_done = sem("e_done")
        o_filled = sem("o_filled")
        o_out = sem("o_out")
        sums_loaded = sem("sums_loaded")
        r_step = sem("r_step")
        r_done = sem("r_done")
        r_stored = sem("r_stored")
        r_loaded = [sem(f"r_loaded{q}") for q in range(QUADS)]
        o_scaled = sem("o_scaled")
        y_done = sem("y_done")
        xres_clear = sem("xres_clear")
        xres_loaded = sem("xres_loaded")
        y_stored = sem("y_stored")

        ORDER = ["m1", "k0", "q0", "m2", "v0", "v1", "m3", "q1", "k1", "m0"]
        LAST_ORDER = ["m1", "m2", "m3"]
        PRO_ORDER = ["k0", "q0", "v0", "v1", "q1", "k1", "m0"]
        assert len(ORDER) == FILLS and len(PRO_ORDER) == PRO

        def fill_no(where, name):
            if where is None:
                return PRO_ORDER.index(name)
            b, last = where
            return FILLS * b + PRO + (LAST_ORDER if last else ORDER).index(name)

        AFTER = {(0, 3): "k0", (1, 0): "q0", (1, 1): "v0", (1, 2): "v1", (2, 1): "q1", (2, 2): "k1"}

        def turns(last):
            order = []
            for q in range(QUADS):
                for k in range(TBL):
                    blocks = [] if last and q >= 2 else [("M", q, 4 * k + n) for n in range(4)]
                    order += blocks[:2]
                    if (q, k) in AFTER and not last:
                        order.append(("P", AFTER[q, k]))
                    order += blocks[2:]
                    if k == 0 and not (last and q == 3):
                        order.append(("T", (q + 1) % QUADS))
            return order

        BODY_TURNS = turns(False)
        PRO_TURNS = ([("P", name) for name in PRO_ORDER[:-1]] + [("M", 2, k) for k in range(16)] + [("T", 0)]
                     + [("M", 3, k) for k in range(16)])
        TURNS = {"prologue": PRO_TURNS, "body": BODY_TURNS, "last": turns(True)}
        BANKS = len(ps_m)
        SHIFT = {"prologue": (len(BODY_TURNS) - len(PRO_TURNS)) % BANKS, "body": 0, "last": 0}

        def kind(where):
            return "prologue" if where is None else ("last" if where[1] else "body")

        def bank_of(where, fill):
            return ps_m[(TURNS[kind(where)].index(fill) + SHIFT[kind(where)]) % BANKS]

        def user_before(where, fill):
            i = TURNS[kind(where)].index(fill) - BANKS
            if i >= 0:
                return 0, TURNS[kind(where)][i]
            if where is None:
                return None
            back = (len(BODY_TURNS) - 1) % BANKS
            mine = (i + BANKS) % BANKS
            return -1, BODY_TURNS[len(BODY_TURNS) - 1 - (back - mine) % BANKS]

        TILES = ["k0", "q0", "q1", "k1"]

        def tile_no(b, name):
            return 4 * b + TILES.index(name)

        def loop(eng, body):
            body(0, True, False)
            with eng.Fori(1, B - 2) as b:
                body(b, False, False)
            body(B - 2, False, False)
            body(B - 1, False, True)

        def static(b):
            return isinstance(b, int)

        with nc.Block() as block:
            @block.sync
            def _(sp):
                for n, t in enumerate((w_qT, w_kT, w_vT)):
                    sp.dma_start(w_stage[:, n, :, :], t.rearrange("(k p) o -> p k o", p=P)).then_inc(w_loaded, 16)
                sp.dma_start(bias["q"][:], b_q).then_inc(w_loaded, 16)
                sp.dma_start(bias["k"][:], b_k).then_inc(w_loaded, 16)
                sp.dma_start(bias_v[:], b_v.to_broadcast([P, C])).then_inc(w_loaded, 16)
                sp.dma_start(mask_rows, mask).then_inc(mrow_loaded, 16)

                def load_xc(b):
                    sp.dma_start(x_in[:], x1_seq[b].rearrange("(k p) t -> p k t", p=P)).then_inc(xc_loaded, 16)
                    sp.dma_start(c_in[:], context_seq[b].rearrange("(k p) t -> p k t", p=P)).then_inc(xc_loaded, 16)

                def load_mask_b(b):
                    sp.dma_start(mask_b[:], mask[b].rearrange("(o t) -> o t", o=1).to_broadcast([P, T])).then_inc(mask_b_loaded, 16)

                def load_mask_col(b):
                    sp.dma_start(mask_col[:], mask_cols[b]).then_inc(mask_col_loaded, 16)

                def load_mask_r(b):
                    sp.dma_start(mask_r[:], mask[b].rearrange("(o c t) -> o c t", o=1, c=32)
                                 .to_broadcast([HQ, 32, TC])).then_inc(mask_r_loaded, 16)

                def stack_quad(b, q):
                    half, p0 = q // 2, (q % 2) * HQ * DH
                    for side, name, part, row in ((0, "q", 0, 0), (0, "q", 0, DH), (0, "q", 1, 2 * DH),
                                                  (1, "k", 0, 0), (1, "k", 1, DH), (1, "k", 0, 2 * DH)):
                        sp.dma_start(stack[row:row + DH, q, side, :, :].bitcast(F32),
                                     tile[name][half][part][p0:p0 + HQ * DH, :].bitcast(F32)).then_inc(stacked[q], 16)
                    for side in range(2):
                        sp.dma_start(stack[AUX:AUX + AUXROWS, q, side, :, :].bitcast(F32),
                                     aux_dram[b][:, side:side + 1, :].to_broadcast([AUXROWS, HQ, T])).then_inc(stacked[q], 16)

                def stack_negmax(b, q):
                    wait_alone(sp, nm_rows_done, QUADS * b + q + 1, (consts, 7))
                    sp.dma_start(stack[MAXROW:MAXROW + 2, q, 0, :, :].bitcast(F32), nm_rows[:]).then_inc(nm_stacked, 16)

                def sums_out(g, q):
                    wait_alone(sp, o_out, g + 1, (consts, 7))
                    sp.dma_start(sums[:], o_sb[DH::32, q, :]).then_inc(sums_loaded, 16)

                def reciprocals(g, q):
                    wait_alone(sp, r_done, g + 1, (consts, 7))
                    sp.dma_start(rinv_dram[q].rearrange("(p c) -> p c", p=P), r_out[:]).then_inc(r_stored, 16)
                    wait_alone(sp, r_stored, 16 * (g + 1), (consts, 7))
                    sp.dma_start(r_b[:, q, :], rinv_dram[q].rearrange("(j o t) -> j o t", j=HQ, o=1)
                                 .to_broadcast([HQ, 32, T])).then_inc(r_loaded[q], 16)

                def rows(seq, b, j):
                    return seq[b].rearrange("(q j d) t -> j d q t", q=QUADS, j=HQ)[j]

                def load_res(b):
                    for j in range(HQ):
                        sp.dma_start(x_res[32 * j:32 * j + DH, :, :], rows(x1_seq, b, j)).then_inc(xres_loaded, 16)

                def store_y(b):
                    for j in range(HQ):
                        sp.dma_start(rows(x2_seq, b, j), y[32 * j:32 * j + DH, :, :]).then_inc(y_stored, 16)

                load_xc(0)
                load_mask_b(0)
                load_mask_col(0)
                load_mask_r(0)
                sp.wait_ge(aux_step, AUX_STEPS)
                sp.dma_start(aux_dram.rearrange("b r s t -> b (r s t)"),
                             aux.rearrange("b r s t -> b (r s t)")).then_inc(aux_stored, 16)
                sp.wait_ge(aux_stored, 16)
                sp.wait_ge(xres_clear, 1)
                load_res(0)
                sp.wait_ge(consts, 5)
                sp.wait_ge(tile_low, tile_no(0, "q0") + 1)
                stack_quad(0, 0)
                stack_quad(0, 1)
                sp.wait_ge(xs_low, 1)
                sp.wait_ge(cs_low, 1)
                load_xc(1)
                sp.wait_ge(tile_low, tile_no(0, "k1") + 1)
                load_mask_b(1)
                stack_quad(0, 2)
                stack_negmax(0, 0)

                def body(b, first, last):
                    g = QUADS * b
                    if not first:
                        wait_alone(sp, e_filled, 8 * g, (consts, 7))
                    stack_quad(b, 3)
                    stack_negmax(b, 1)
                    if not first:
                        sums_out(g - 1, 3)
                        reciprocals(g - 1, 3)
                        load_mask_r(b)
                    stack_negmax(b, 2)
                    if not last:
                        wait_alone(sp, v_done, QUADS * (b + 1), (consts, 7))
                        load_mask_col(b + 1)
                    sums_out(g, 0)
                    if not first:
                        wait_alone(sp, y_done, g, (consts, 7))
                        store_y(b - 1)
                        load_res(b)
                    if not last:
                        wait_alone(sp, xs_low, b + 2, (consts, 7))
                        wait_alone(sp, cs_low, b + 2, (consts, 7))
                        if not (static(b) and b + 2 >= B):
                            load_xc(b + 2)
                        wait_alone(sp, tile_low, tile_no(b + 1, "q0") + 1, (consts, 7))
                        wait_alone(sp, e_filled, 8 * (g + 1), (consts, 7))
                        stack_quad(b + 1, 0)
                    reciprocals(g, 0)
                    if not last:
                        wait_alone(sp, e_filled, 8 * (g + 2), (consts, 7))
                        stack_quad(b + 1, 1)
                    stack_negmax(b, 3)
                    sums_out(g + 1, 1)
                    reciprocals(g + 1, 1)
                    if not last:
                        wait_alone(sp, tile_low, tile_no(b + 1, "k1") + 1, (consts, 7))
                        if not (static(b) and b + 2 >= B):
                            load_mask_b(b + 2)
                        wait_alone(sp, e_filled, 8 * (g + 3), (consts, 7))
                        stack_quad(b + 1, 2)
                        stack_negmax(b + 1, 0)
                    sums_out(g + 2, 2)
                    reciprocals(g + 2, 2)

                loop(sp, body)
                sums_out(QUADS * B - 1, 3)
                reciprocals(QUADS * B - 1, 3)
                sp.wait_ge(y_done, QUADS * B)
                store_y(B - 1)
                sp.wait_ge(y_stored, 16 * HQ * B)

            @block.gpsimd
            def _(pool):
                nc.gpsimd.memset(ident[:], 0.0).then_inc(consts, 1)
                nc.gpsimd.memset(minus_half[:], -0.5).then_inc(consts, 1)
                nc.gpsimd.memset(stack[:].rearrange("p a b c t -> p (a b c t)").bitcast(F32), 0.0).then_inc(consts, 1)
                pool.wait_ge(consts, 3)
                nc.gpsimd.affine_select(out=ident[:], in_=ident[:], compare_op=ALU.not_equal, fill=1.0, base=0,
                                        pattern=[[-1, P]], channel_multiplier=1).then_inc(consts, 1)
                pool.wait_ge(consts, 4)
                nc.gpsimd.memset(stack[MAXROW:MAXROW + 2, :, 1, :, :].bitcast(F32), 1.0).then_inc(consts, 1)
                pool.wait_ge(consts, 5)
                nc.gpsimd.memset(v_stack[:], 0.0).then_inc(consts, 1)
                pool.wait_ge(consts, 6)
                nc.gpsimd.memset(v_stack[:, :, :, DH:DH + 1], 1.0).then_inc(consts, 1)
                pool.wait_ge(aux_stored, 16)
                nc.gpsimd.memset(x_res, 0.0).then_inc(xres_clear, 1)

                def norm_scale(b):
                    wait_alone(pool, aggr_done, CT * (b + 1), (consts, 7))
                    nc.gpsimd.tensor_scalar(rstd[:], mv[:, :, 1], LN_EPS, None, ALU.add).then_inc(veps_done, 1)
                    pool.wait_ge(veps_done, b + 1)
                    nc.gpsimd.tensor_tensor(rstd[:], rstd[:], minus_half[:], ALU.pow).then_inc(rstd_done, 1)

                def low(dst, full, high, high_sem, n, out_sem):
                    pool.wait_ge(high_sem, n)
                    nc.gpsimd.tensor_tensor(dst, full, high.bitcast(F32), ALU.subtract).then_inc(out_sem, 1)

                def context_low(b):
                    low(cs[1][:], c_in[:], cs[0][:], cs_high, b + 1, cs_low)

                def x_low(b):
                    low(xs[1][:], xn[:], xs[0][:], xs_high, b + 1, xs_low)

                def tile_low_part(b, name):
                    n, half = name[0], int(name[1])
                    if not (static(b) and b == 0):
                        pool.wait_ge(stacked[2 * half + 1], 16 * 8 * b)
                    low(tile[n][half][1][:], raw[n][:], tile[n][half][0][:], tile_high, tile_no(b, name) + 1, tile_low)

                def values(b, q):
                    if q == 0:
                        wait_alone(pool, vbias_done, 2 * (b + 1), (consts, 7))
                        wait_alone(pool, mask_col_loaded, 16 * (b + 1), (consts, 7))
                    if not (static(b) and b == 0):
                        wait_alone(pool, o_filled, QUADS * (b - 1) + q + 1, (consts, 7))
                    for k in range(TBL):
                        ins = nc.gpsimd.tensor_scalar(
                            v_stack[:, k, HQ * q:HQ * q + HQ, 0:DH],
                            v_raw[:, k, HQ * DH * q:HQ * DH * (q + 1)].rearrange("p (h d) -> p h d", h=HQ),
                            mask_col[:, k:k + 1], None, ALU.mult)
                    ins.then_inc(v_done, 1)

                def residual(b, g, q):
                    pool.wait_ge(r_loaded[q], 16 * (b + 1))
                    nc.gpsimd.tensor_tensor(r_b[:, q, :], o_sb[:, q, :], r_b[:, q, :], ALU.mult).then_inc(o_scaled, 1)
                    if q == 0:
                        pool.wait_ge(xres_loaded, 16 * HQ * (b + 1))
                        if not (static(b) and b == 0):
                            pool.wait_ge(y_stored, 16 * HQ * b)
                    pool.wait_ge(o_scaled, g + 2)
                    nc.gpsimd.tensor_tensor(y[:, q, :], r_b[:, q, :], x_res[:, q, :], ALU.add).then_inc(y_done, 1)

                pool.wait_ge(consts, 7)
                pool.sem_inc(o_scaled, 1)
                norm_scale(0)
                context_low(0)
                x_low(0)
                for name in TILES:
                    tile_low_part(0, name)
                for q in range(3):
                    values(0, q)

                def body(b, first, last):
                    g = QUADS * b
                    if not last:
                        norm_scale(b + 1)
                        context_low(b + 1)
                    values(b, 3)
                    if not last:
                        x_low(b + 1)
                        tile_low_part(b + 1, "k0")
                    if not first:
                        residual(b - 1, g - 1, 3)
                    if not last:
                        tile_low_part(b + 1, "q0")
                    if not last:
                        values(b + 1, 0)
                    residual(b, g, 0)
                    if not last:
                        values(b + 1, 1)
                        tile_low_part(b + 1, "q1")
                        tile_low_part(b + 1, "k1")
                    residual(b, g + 1, 1)
                    if not last:
                        values(b + 1, 2)
                    residual(b, g + 2, 2)

                loop(pool, body)
                residual(B - 1, QUADS * B - 1, 3)

            @block.scalar
            def _(act):
                for n, name in enumerate("qkv"):
                    if n == 0:
                        act.wait_ge(w_loaded, 16 * 6)
                    nc.scalar.activation(w[name][0][:], w_stage[:, n, :, :], ACT.Copy).then_inc(w_high, 1)

                def context_high(b):
                    act.wait_ge(xc_loaded, 32 * (b + 1))
                    if not (static(b) and b == 0):
                        act.wait_ge(tile_high, 4 * b)
                    nc.scalar.activation(cs[0][:], c_in[:], ACT.Copy).then_inc(cs_high, 1)

                def x_high(b):
                    act.wait_ge(xn_done, b + 1)
                    nc.scalar.activation(xs[0][:], xn[:], ACT.Copy).then_inc(xs_high, 1)

                def tile_high_part(b, name):
                    n, half = name[0], int(name[1])
                    act.wait_ge(raw_done, tile_no(b, name) + 1)
                    if not (static(b) and b == 0):
                        act.wait_ge(stacked[2 * half + 1], 16 * 8 * b)
                    nc.scalar.activation(tile[n][half][0][:], raw[n][:], ACT.Copy).then_inc(tile_high, 1)

                def negmax_rows(where, b, q):
                    g = QUADS * b + q
                    act.wait_ge(proj_filled, fill_no(where, f"m{q}") + 1)
                    act.wait_ge(nm_stacked, 16 * g)
                    nc.scalar.activation(nm_rows[:], bank_of(where, ("T", q))[0:2 * HQ, :], ACT.Copy).then_inc(nm_rows_done, 1)

                def exps(g, k):
                    for p in range(2):
                        act.wait_ge(e_filled, 8 * g + 2 * k + p + 1)
                        nc.scalar.activation(probs[:, k % 2, 2 * p:2 * p + 2, :], ps_e[p][:], ACT.Exp,
                                             scale=0.25).then_inc(e_done, 1)

                def output(g, q):
                    act.wait_ge(o_filled, g + 1)
                    if not (static(g) and g < QUADS):
                        act.wait_ge(o_scaled, g - QUADS + 2)
                    nc.scalar.activation(o_sb[:, q, :], ps_o[:], ACT.Copy).then_inc(o_out, 1)

                context_high(0)
                x_high(0)
                for name in TILES:
                    tile_high_part(0, name)
                negmax_rows(None, 0, 0)

                def body(b, first, last):
                    g = QUADS * b
                    where = (b, last)
                    exps(g, 0)
                    if not first:
                        output(g - 1, 3)
                    negmax_rows(where, b, 1)
                    if not last:
                        context_high(b + 1)
                    exps(g, 1)
                    if not last:
                        x_high(b + 1)
                    exps(g, 2)
                    exps(g, 3)
                    if not last:
                        tile_high_part(b + 1, "k0")
                    exps(g + 1, 0)
                    output(g, 0)
                    if not last:
                        tile_high_part(b + 1, "q0")
                    negmax_rows(where, b, 2)
                    for k in (1, 2, 3):
                        exps(g + 1, k)
                    exps(g + 2, 0)
                    output(g + 1, 1)
                    negmax_rows(where, b, 3)
                    exps(g + 2, 1)
                    if not last:
                        tile_high_part(b + 1, "q1")
                    exps(g + 2, 2)
                    if not last:
                        tile_high_part(b + 1, "k1")
                    exps(g + 2, 3)
                    exps(g + 3, 0)
                    output(g + 2, 2)
                    if not last:
                        negmax_rows(where, b + 1, 0)
                    for k in (1, 2, 3):
                        exps(g + 3, k)

                loop(act, body)
                output(QUADS * B - 1, 3)

            @block.vector
            def _(dve):
                dve.wait_ge(w_loaded, 16 * 6)
                for n, name in enumerate("qkv"):
                    dve.wait_ge(w_high, n + 1)
                    nc.vector.tensor_tensor(w[name][1][:], w_stage[:, n, :, :], w[name][0][:].bitcast(F32),
                                            ALU.subtract).then_inc(w_low, 1)

                steps = [0]

                def aux_op(ins):
                    steps[0] += 1
                    ins.then_inc(aux_step, 1)
                    dve.wait_ge(aux_step, steps[0])

                def split_rows(full, side, highs, lows):
                    aux_op(nc.vector.tensor_copy(aux[:, highs[0], side, :].bitcast(F32R), full))
                    aux_op(nc.vector.tensor_tensor(aux[:, lows[0], side, :].bitcast(F32R), full,
                                                   aux[:, highs[0], side, :], ALU.subtract))
                    for r in highs[1:]:
                        nc.vector.tensor_copy(aux[:, r, side, :], aux[:, highs[0], side, :])

                dve.wait_ge(mrow_loaded, 16)
                aux_op(nc.vector.tensor_scalar(one_minus, mask_rows, -1.0, 1.0, ALU.mult, ALU.add))
                split_rows(one_minus, 0, (0, 2), (1,))
                split_rows(mask_rows, 0, (3, 5), (4,))
                aux_op(nc.vector.memset(neg_row, NEG4))
                split_rows(neg_row, 1, (0, 1), (2,))
                aux_op(nc.vector.tensor_scalar(one_minus, one_minus, NEG4, None, ALU.mult))
                aux_op(nc.vector.tensor_copy(aux[:, 3, 1, :].bitcast(F32R), one_minus))
                nc.vector.tensor_copy(aux[:, 4, 1, :], aux[:, 3, 1, :])
                nc.vector.tensor_tensor(aux[:, 5, 1, :].bitcast(F32R), one_minus, aux[:, 3, 1, :],
                                        ALU.subtract).then_inc(aux_step, 1)
                assert steps[0] + 1 == AUX_STEPS

                def normalise(b):
                    dve.wait_ge(xc_loaded, 32 * (b + 1))
                    for k in range(CT):
                        nc.vector.bn_stats(stats[:, k, :], x_in[:, k, :]).then_inc(stats_done, 1)
                    wait_alone(dve, stats_done, CT * (b + 1), (consts, 7))
                    for k in range(CT):
                        nc.vector.bn_aggr(mv[:, k, :], stats[:, k, :]).then_inc(aggr_done, 1)

                def apply_norm(b):
                    dve.wait_ge(rstd_done, b + 1)
                    for k in range(CT):
                        ins = nc.vector.tensor_scalar(xn[:, k, :], x_in[:, k, :], mv[:, k, 0:1], rstd[:, k:k + 1],
                                                      ALU.subtract, ALU.mult)
                    ins.then_inc(xn_done, 1)

                def raw_tile(where, b, name):
                    n, half = name[0], int(name[1])
                    dve.wait_ge(proj_filled, fill_no(where, name) + 1)
                    if name in ("k0", "q0"):
                        if name == "k0":
                            dve.wait_ge(mask_b_loaded, 16 * (b + 1))
                        if not (static(b) and b == 0):
                            dve.wait_ge(tile_low, 4 * b)
                    else:
                        dve.wait_ge(tile_low, tile_no(b, n + "0") + 1)
                    nc.vector.scalar_tensor_tensor(raw[n][:], bank_of(where, ("P", name))[:], bias[n][:, half:half + 1], mask_b[:], ALU.add,
                                                   ALU.mult).then_inc(raw_done, 1)

                def raw_values(where, b, i):
                    dve.wait_ge(proj_filled, fill_no(where, f"v{i}") + 1)
                    if i == 0 and not (static(b) and b == 0):
                        dve.wait_ge(v_done, QUADS * b)
                    for k in range(2):
                        ins = nc.vector.tensor_tensor(v_raw[:, 2 * i + k, :], bank_of(where, ("P", f"v{i}"))[:, k * C:(k + 1) * C], bias_v[:], ALU.add)
                    ins.then_inc(vbias_done, 1)

                def maxima(where, q, g, k0, k1):
                    for k in range(k0, k1):
                        if k == 0 and not (static(g) and g == 0):
                            dve.wait_ge(nm_low, g)
                        dve.wait_ge(m_filled, 16 * g + k + 1)
                        nc.vector.tensor_reduce(negmax[:, k // HQ, k % HQ:k % HQ + 1], bank_of(where, ("M", q, k))[:], AX.X, ALU.max,
                                                negate=True).then_inc(m_reduced, 1)

                def split_maxima(g):
                    dve.wait_ge(m_reduced, 16 * (g + 1))
                    nc.vector.tensor_copy(nm_split[:, :, 0, :].bitcast(F32R), negmax[:]).then_inc(nm_high, 1)
                    dve.wait_ge(nm_high, g + 1)
                    nc.vector.tensor_tensor(nm_split[:, :, 1, :].bitcast(F32R), negmax[:], nm_split[:, :, 0, :],
                                            ALU.subtract).then_inc(nm_low, 1)

                def reciprocal(g):
                    dve.wait_ge(sums_loaded, 16 * (g + 1))
                    nc.vector.reciprocal(rsum[:], sums[:]).then_inc(r_step, 1)
                    dve.wait_ge(r_step, g + 1)

                def masked_reciprocal(g, b, q):
                    reciprocal(g)
                    if q == 0:
                        dve.wait_ge(mask_r_loaded, 16 * (b + 1))
                    if not (static(g) and g == 0):
                        dve.wait_ge(r_stored, 16 * g)
                    nc.vector.tensor_tensor(r_out[:], rsum[:], mask_r[:], ALU.mult).then_inc(r_done, 1)

                normalise(0)
                apply_norm(0)
                for name in ("k0", "q0"):
                    raw_tile(None, 0, name)
                raw_values(None, 0, 0)
                raw_values(None, 0, 1)
                for name in ("q1", "k1"):
                    raw_tile(None, 0, name)
                for g in range(2):
                    maxima(None, g + 2, g, 0, 16)
                    split_maxima(g)

                def body(b, first, last):
                    g = QUADS * b
                    where = (b, last)
                    nxt = b + 1
                    for q in range(QUADS):
                        for k in range(TBL):
                            name = AFTER.get((q, k))
                            if not (last and q >= 2):
                                maxima(where, q, g + q + 2, 4 * k, 4 * k + 2)
                            if name and not last:
                                if name[0] == "v":
                                    raw_values(where, nxt, int(name[1]))
                                else:
                                    raw_tile(where, nxt, name)
                            if not (last and q >= 2):
                                maxima(where, q, g + q + 2, 4 * k + 2, 4 * k + 4)
                            if (q, k) == (0, 0) and not last:
                                normalise(nxt)
                            if (q, k) == (0, 1) and not last:
                                apply_norm(nxt)
                            if (q, k) == (0, 2) and not first:
                                masked_reciprocal(g - 1, b - 1, 3)
                            if q and k == 2:
                                masked_reciprocal(g + q - 1, b, q - 1)
                        if not (last and q >= 2):
                            split_maxima(g + q + 2)

                loop(dve, body)
                masked_reciprocal(QUADS * B - 1, B - 1, 3)

            @block.tensor
            def _(pe):
                ROWS = {"max": MAXROW, "exp": MAXROW + 2}

                def bank(where, b, fill):
                    before = user_before(where, fill)
                    if before is not None:
                        back, (what, *which) = before
                        at = b + back
                        if what == "M":
                            pe.wait_ge(m_reduced, 16 * (QUADS * at + which[0] + 2) + which[1] + 1)
                        elif what == "T":
                            pe.wait_ge(nm_rows_done, QUADS * (at if which[0] else at + 1) + which[0] + 1)
                        elif which[0][0] == "v":
                            pe.wait_ge(vbias_done, 2 * (at + 1) + int(which[0][1]) + 1)
                        else:
                            pe.wait_ge(raw_done, tile_no(at + 1, which[0]) + 1)
                    return bank_of(where, fill)

                def products(out, pairs):
                    n = len(pairs)
                    for i, (s, m) in enumerate(pairs):
                        for k, (a, c) in enumerate(((0, 0), (0, 1), (1, 0))):
                            ins = nc.tensor.matmul(out, s(a), m(c), start=(i == 0 and k == 0), stop=(i == n - 1 and k == 2))
                    return ins

                def project(where, b, name):
                    n, half = name[0], int(name[1])
                    src = xs if n == "q" else cs
                    pe.wait_ge(xs_low if n == "q" else cs_low, b + 1)
                    ps_p = bank(where, b - 1, ("P", name))
                    products(ps_p[:], [(lambda a, k=k: w[n][a][:, k, half * P:(half + 1) * P],
                                        lambda c, k=k: src[c][:, k, :]) for k in range(CT)]).then_inc(proj_filled, 1)

                def project_values(where, b, i):
                    ps_p = bank(where, b - 1, ("P", f"v{i}"))
                    for j in range(2):
                        blk = 2 * i + j
                        ins = products(ps_p[:, j * C:(j + 1) * C],
                                       [(lambda a, k=k: cs[a][:, k, blk * P:(blk + 1) * P],
                                         lambda c, k=k: w["v"][c][:, k, :]) for k in range(CT)])
                    ins.then_inc(proj_filled, 1)

                def negmax_transpose(where, b, q):
                    g = QUADS * b + q
                    pe.wait_ge(nm_low, g + 1)
                    ps_p = bank(where, b if q else b - 1, ("T", q))
                    for k in range(TBL):
                        ins = nc.tensor.transpose(ps_p[0:2 * HQ, k * P:(k + 1) * P],
                                                  nm_split[:, k, :, :].rearrange("p s h -> p (s h)"), ident[:])
                    ins.then_inc(proj_filled, 1)

                def max_scores(where, b, step, k0, k1):
                    g = QUADS * b + step + 2
                    q = (step + 2) % QUADS
                    for k in range(k0, k1):
                        blk, h = k // HQ, k % HQ
                        if k == 0:
                            pe.wait_ge(stacked[q], 16 * 8 * (b + (step + 2) // QUADS + 1))
                        nc.tensor.matmul(bank(where, b, ("M", step, k))[:], stack[0:MAXROW, q, 0, h, blk * P:(blk + 1) * P],
                                         stack[0:MAXROW, q, 1, h, :], start=True, stop=True).then_inc(m_filled, 1)

                def exp_scores(g, q, k, p):
                    if k == 0 and p == 0:
                        pe.wait_ge(nm_stacked, 16 * (g + 1))
                    if not (static(g) and 8 * g + 2 * k + p < 2):
                        pe.wait_ge(e_done, 8 * g + 2 * k + p - 1)
                    for i in range(2):
                        h = 2 * p + i
                        ins = nc.tensor.matmul(ps_e[p][:, i, :], stack[0:MAXROW + 2, q, 1, h, k * P:(k + 1) * P],
                                               stack[0:MAXROW + 2, q, 0, h, :], start=True, stop=True)
                    ins.then_inc(e_filled, 1)

                def values_product(g, q, k, between=None):
                    pe.wait_ge(e_done, 8 * g + 2 * k + 2)
                    if k == 0:
                        pe.wait_ge(v_done, g + 1)
                        pe.wait_ge(o_out, g)
                    for h in range(HQ):
                        if h == HQ // 2 and between:
                            between()
                        ins = nc.tensor.matmul(ps_o[32 * h:32 * h + 32, :], v_stack[:, k, HQ * q + h, :],
                                               probs[:, k % 2, h, :], start=(k == 0), stop=(k == TBL - 1))
                    if k == TBL - 1:
                        ins.then_inc(o_filled, 1)

                pe.wait_ge(consts, 7)
                pe.wait_ge(w_low, 3)
                project(None, 0, "k0")
                project(None, 0, "q0")
                project_values(None, 0, 0)
                project_values(None, 0, 1)
                project(None, 0, "q1")
                project(None, 0, "k1")
                max_scores(None, -1, 2, 0, 16)
                negmax_transpose(None, 0, 0)
                max_scores(None, -1, 3, 0, 16)

                def body(b, first, last):
                    g = QUADS * b
                    where = (b, last)
                    for q in range(QUADS):
                        for k in range(TBL):

                            def max_block(n):
                                if not (last and q >= 2):
                                    max_scores(where, b, q, 4 * k + n, 4 * k + n + 1)

                            exp_scores(g + q, q, k, 0)
                            max_block(0)
                            exp_scores(g + q, q, k, 1)
                            max_block(1)
                            name = AFTER.get((q, k))
                            if name and not last:
                                if name[0] == "v":
                                    project_values(where, b + 1, int(name[1]))
                                else:
                                    project(where, b + 1, name)
                            third = lambda: max_block(2)
                            if k > 0:
                                values_product(g + q, q, k - 1, third)
                            elif q > 0:
                                values_product(g + q - 1, q - 1, TBL - 1, third)
                            elif not first:
                                values_product(g - 1, QUADS - 1, TBL - 1, third)
                            else:
                                third()
                            max_block(3)
                            if k == 0 and q < 3:
                                negmax_transpose(where, b, q + 1)
                            if k == 0 and q == 3 and not last:
                                negmax_transpose(where, b + 1, 0)

                loop(pe, body)
                values_product(QUADS * B - 1, QUADS - 1, TBL - 1)


def in_steps(eng, steps, step, first=2, last=2):
    for n in range(first):
        step(n, n // 2, n % 2)
    end = steps - last
    with eng.Fori(first // 2, end // 2) as t:
        for i in range(2):
            step(2 * t + i, t, i)
    for n in range(end, steps):
        step(n, n // 2, n % 2)


def in_groups(eng, groups, group):
    group(0, 0, 0)
    with eng.Fori(0, (groups - 2) // 3) as t:
        for i in range(1, 4):
            group(3 * t + i, t + i // 3, i % 3)
    group(groups - 1, (groups - 1) // 3, (groups - 1) % 3)


def experts_scratch(nc):
    E, T, H = 8, 4096, 512
    return [nc.dram_tensor("rows_by_expert", [E * (T + P) + P, H + 4], F32, kind="Internal").ap(),
            nc.dram_tensor("expert_outputs", [2 * T + P, H], F32, kind="Internal").ap()]


def experts_phase(nc, x2_rows, w_gT, w_13T, w_2T, bias, out_rows, rows, y2):
    GROUPS, GT, H = x2_rows.shape
    T = GROUPS * GT
    E = w_gT.shape[1]
    FF = w_2T.shape[1]
    TB = GT // P
    KT = H // P
    FT = FF // P
    assert GT == BANK and 2 * FF == BANK and H == BANK and E == GROUPS
    REGION = T + P
    PAD_ROW = E * REGION
    W0, W1, BEST, TOKEN, ROW = H, H + 1, H + 2, H + 3, H + 4
    TILES = 2 * T // P + E
    PASSES = ((0, 0), (0, 1), (1, 0))

    with ExitStack() as ctx:
        def sb(name, shape, dt=F32):
            return ctx.enter_context(nc.sbuf_tensor("c_" + name, shape, dt))

        def early(tensors, place_of):
            with ExitStack() as at_first:
                early_ones = [at_first.enter_context(nc.sbuf_tensor("c_" + name, shape, dt)) for name, shape, dt in tensors]
            return *early_ones, sb(*place_of)

        w13_high = sb("w13_h", [P, E, KT, 2 * FF], F32R)
        w13_raw, w13_low = early([("w13_raw", [P, E, KT, 2 * FF], F32)], ("w13_l", [P, E, KT, 2 * FF], F32R))
        xT_high, xT_low, w2 = early([(f"xT_{s}", [P, KT, GT], F32R) for s in "hl"], ("w2", [P, E, FT, H]))
        w13 = [w13_high, w13_low]
        ident = sb("ident", [P, P])
        tile_expert = sb("tile_expert", [P, TILES])
        tile_expert_int = sb("tile_expert_int", [P, TILES], I32)
        tile_row_int = sb("tile_row_int", [P, TILES], I32)

        route_tokens(nc, x2_rows, w_gT, w_13T, w_2T, bias, rows, w13, w13_raw, [xT_high, xT_low], w2, ident, tile_expert, tile_expert_int,
                     tile_row_int, GROUPS, GT, TB, KT, FT, T, H, E, REGION, PAD_ROW, W0, W1, BEST, TOKEN, ROW, TILES, PASSES)
        run_experts(nc, rows, y2, w13, w2, ident, tile_expert, tile_expert_int, tile_row_int,
                    KT, FT, FF, T, H, E, W0, W1, BEST, TOKEN, ROW, TILES, PASSES)
    combine(nc, x2_rows, y2, out_rows, T, H)


def route_tokens(nc, x2_rows, w_gT, w_13T, w_2T, bias, rows, w13, w13_raw, xT, w2, ident, tile_expert, tile_expert_int,
                 tile_row_int, GROUPS, GT, TB, KT, FT, T, H, E, REGION, PAD_ROW, W0, W1, BEST, TOKEN, ROW, TILES, PASSES):
    with ExitStack() as ctx:
        def sb(name, shape, dt=F32):
            return ctx.enter_context(nc.sbuf_tensor("r_" + name, shape, dt))

        def psum(name, shape):
            return ctx.enter_context(nc.psum_tensor("r_" + name, shape, F32))

        def sem(name):
            return ctx.enter_context(nc.semaphore("r_" + name))

        xn = [sb(f"xn{i}", [P, TB, ROW]) for i in range(3)]
        wg_raw = sb("wg_raw", [P, KT, E])
        wg = [sb(f"wg_{s}", [P, KT, E], F32R) for s in "hl"]
        bias_b = sb("bias_b", [P, E])
        minus_half = sb("minus_half", [P, TB])
        stats = sb("stats", [P, TB, 6])
        mv = sb("mv", [P, TB, 2])
        rstd = sb("rstd", [P, TB])
        STEPS = T // P
        NUMS = E + TB + STEPS + TILES
        nums_int = sb("nums_int", [P, NUMS], I32)
        nums = sb("nums", [P, NUMS])
        expert_no = nums[:, 0:E]
        token_in_group = nums[:, E:E + TB]
        times_128 = nums[:, E + TB:E + TB + STEPS]
        tile_no = nums[:, E + TB + STEPS:]
        region_row = sb("region_row", [P, E])
        next_row = sb("next_row", [P, E])
        token = sb("token", [P, TB])
        lower = sb("lower", [P, E, E])
        before_bf = sb("before_bf", [P, P], BF16)
        ones_bf = sb("ones_bf", [P, P], BF16)
        chosen_bf = sb("chosen_bf", [P, TB + 1, E], BF16)
        ez = sb("ez", [P, TB, E])
        sig = sb("sig", [P, TB, E])
        score = sb("score", [P, TB, E])
        above = sb("above", [P, TB, E, E])
        equal = sb("equal", [P, TB, E, E])
        rank = sb("rank", [P, TB, E])
        total = sb("total", [P, TB])
        inv = sb("inv", [P, TB])
        weight = sb("weight", [P, TB, E])
        is_rank = sb("is_rank", [P, TB, 2, E])
        picked = sb("picked", [P, TB, 2, E])
        place = sb("place", [P, TB, E])
        place_rank = sb("place_rank", [P, TB, 2])
        place_int = [sb(f"place_int{i}", [P, TB, 2], I32) for i in range(3)]
        pad_rows = sb("pad_rows", [P, ROW])
        pad_place = sb("pad_place", [P, E], I32)
        n_rows = sb("n_rows", [P, E])
        n_tiles = sb("n_tiles", [P, E])
        first_tile = sb("first_tile", [P, E + 1])
        more_rows = sb("more_rows", [P, E, STEPS])
        started = sb("started", [P, TILES, E - 1])
        tile_row = sb("tile_row", [P, TILES])
        tile_first = sb("tile_first", [P, TILES])
        tile_used = sb("tile_used", [P, TILES])
        ps_x = [psum(f"ps_x{i}", [P, BANK]) for i in range(4)]
        ps_r = psum("ps_r", [P, TB, E])
        ps_c = psum("ps_c", [P, TB + 1, E])
        consts = sem("consts")
        numbers = sem("numbers")
        small_loaded = sem("small_loaded")
        wg_high = sem("wg_high")
        wg_low = sem("wg_low")
        x2_loaded = [sem(f"x2_loaded{i}") for i in range(3)]
        w13_loaded = [sem(f"w13_loaded{e}") for e in range(E)]
        w2_loaded = sem("w2_loaded")
        w13_high = sem("w13_high")
        w13_low = sem("w13_low")
        stats_done = sem("stats_done")
        aggr_done = sem("aggr_done")
        veps_done = sem("veps_done")
        rstd_done = sem("rstd_done")
        xn_done = sem("xn_done")
        xT_filled = sem("xT_filled")
        xT_high = sem("xT_high")
        xT_low = sem("xT_low")
        logits_done = sem("logits_done")
        ez_done = sem("ez_done")
        route = sem("route")
        chosen_done = sem("chosen_done")
        counted = sem("counted")
        placed = sem("placed")
        scattered = [sem(f"scattered{i}") for i in range(3)]
        pads_placed = sem("pads_placed")
        padded = sem("padded")
        pad_tile_out = sem("pad_tile_out")
        table = sem("table")

        with nc.Block() as block:
            @block.sync
            def _(sp):
                sp.dma_start(wg_raw[:], w_gT.rearrange("(k p) e -> p k e", p=P)).then_inc(small_loaded, 16)
                sp.dma_start(bias_b[:], bias.to_broadcast([P, E])).then_inc(small_loaded, 16)

                for G in range(GROUPS):
                    if G >= 3:
                        sp.wait_ge(scattered[G % 3], 16 * 2 * TB * (G // 3))
                    sp.dma_start(xn[G % 3][:, :, 0:H], x2_rows[G].rearrange("(n p) h -> p n h", p=P)).then_inc(x2_loaded[G % 3], 16)
                sp.dma_start(rows[PAD_ROW:PAD_ROW + P], pad_rows[:]).then_inc(pad_tile_out, 16)
                sp.wait_ge(logits_done, TB * GROUPS)
                sp.dma_start(w2[:], w_2T.rearrange("e (k p) h -> p e k h", p=P)).then_inc(w2_loaded, 16)
                sp.wait_ge(pad_tile_out, 16)
                sp.wait_ge(padded, 16 * E)
                for i in range(3):
                    sp.wait_ge(scattered[i], 16 * 2 * TB * len(range(i, GROUPS, 3)))
                sp.wait_ge(w2_loaded, 16)

            @block.gpsimd
            def _(pool):
                nc.gpsimd.memset(ident[:], 0.0).then_inc(consts, 1)
                nc.gpsimd.memset(minus_half[:], -0.5).then_inc(consts, 1)
                nc.gpsimd.memset(ones_bf[:], 1.0).then_inc(consts, 1)
                nc.gpsimd.memset(before_bf[:], 1.0).then_inc(consts, 1)
                nc.gpsimd.memset(lower[:], 1.0).then_inc(consts, 1)
                nc.gpsimd.memset(pad_rows[:, 0:BEST], 0.0).then_inc(consts, 1)
                nc.gpsimd.memset(pad_rows[:, BEST:TOKEN], -1.0).then_inc(consts, 1)
                nc.gpsimd.memset(chosen_bf[:], 0.0).then_inc(consts, 1)
                pool.wait_ge(consts, 8)
                nc.gpsimd.affine_select(out=ident[:], in_=ident[:], compare_op=ALU.not_equal, fill=1.0, base=0,
                                        pattern=[[-1, P]], channel_multiplier=1).then_inc(consts, 1)
                nc.gpsimd.affine_select(out=before_bf[:], in_=before_bf[:], compare_op=ALU.is_gt, fill=0.0, base=0,
                                        pattern=[[1, P]], channel_multiplier=-1).then_inc(consts, 1)
                nc.gpsimd.affine_select(out=lower[:], in_=lower[:], compare_op=ALU.is_gt, fill=0.0, base=0,
                                        pattern=[[1, E], [-1, E]], channel_multiplier=0).then_inc(consts, 1)
                at = 0
                for step, count, per_partition in ((1, E, 0), (P, TB, 1), (P, STEPS, 0), (1, TILES, 0)):
                    nc.gpsimd.iota(nums_int[:, at:at + count], pattern=[[step, count]], base=0,
                                   channel_multiplier=per_partition).then_inc(numbers, 1)
                    at += count

                def rstd_of(G):
                    wait_alone(pool, aggr_done, TB * (G + 1), (consts, 11))
                    nc.gpsimd.tensor_scalar(rstd[:], mv[:, :, 1], LN_EPS, None, ALU.add).then_inc(veps_done, 1)
                    pool.wait_ge(veps_done, G + 1)
                    nc.gpsimd.tensor_tensor(rstd[:], rstd[:], minus_half[:], ALU.pow).then_inc(rstd_done, 1)

                def group(G, t, i):
                    if not isinstance(G, int) or G < GROUPS - 1:
                        rstd_of(G + 1)
                    wait_alone(pool, placed, G + 1, (consts, 11))
                    for n in range(TB):
                        for k in range(2):
                            nc.gpsimd.indirect_dma_start(rows, bass.IndirectOffsetOnAxis(place_int[i][:, n, k:k + 1], 0),
                                                         xn[i][:, n, :], None).then_inc(scattered[i], 16)

                rstd_of(0)
                in_groups(pool, GROUPS, group)
                pool.wait_ge(pads_placed, 1)
                for e in range(E):
                    nc.gpsimd.indirect_dma_start(rows, bass.IndirectOffsetOnAxis(pad_place[:, e:e + 1], 0),
                                                 pad_rows[:], None).then_inc(padded, 16)

            @block.scalar
            def _(act):
                for e in range(E):
                    act.dma_start(w13_raw[:, e], w_13T[e].rearrange("(k p) f -> p k f", p=P)).then_inc(w13_loaded[e], 16)

                def highs(G):
                    for j in range(KT):
                        act.wait_ge(xT_filled, KT * G + j + 1)
                        nc.scalar.activation(xT[0][:, j, :], ps_x[j][:], ACT.Copy).then_inc(xT_high, 1)

                def group(G, t, i):
                    act.wait_ge(logits_done, TB * (G + 1))
                    nc.scalar.activation(ez[:], ps_r[:], ACT.Exp, scale=-1.0).then_inc(ez_done, 1)
                    if not isinstance(G, int) or G < GROUPS - 1:
                        highs(G + 1)

                act.wait_ge(small_loaded, 32)
                nc.scalar.activation(wg[0][:], wg_raw[:], ACT.Copy).then_inc(wg_high, 1)
                highs(0)
                for e in range(2):
                    act.wait_ge(w13_loaded[e], 16)
                    nc.scalar.activation(w13[0][:, e], w13_raw[:, e], ACT.Copy).then_inc(w13_high, 1)
                in_groups(act, GROUPS, group)
                for e in range(2, E):
                    act.wait_ge(w13_loaded[e], 16)
                    nc.scalar.activation(w13[0][:, e], w13_raw[:, e], ACT.Copy).then_inc(w13_high, 1)

            @block.vector
            def _(dve):
                R = 21

                def normalise(G, t, i):
                    dve.wait_ge(x2_loaded[i], 16 * (t + 1))
                    for n in range(TB):
                        nc.vector.bn_stats(stats[:, n, :], xn[i][:, n, 0:H]).then_inc(stats_done, 1)
                    if not isinstance(G, int) or G:
                        wait_alone(dve, stats_done, TB * (G + 1), (xn_done, 1))
                    else:
                        dve.wait_ge(stats_done, TB)
                    for n in range(TB):
                        nc.vector.bn_aggr(mv[:, n, :], stats[:, n, :]).then_inc(aggr_done, 1)
                    dve.wait_ge(rstd_done, G + 1)
                    for n in range(TB):
                        ins = nc.vector.tensor_scalar(xn[i][:, n, 0:H], xn[i][:, n, 0:H], mv[:, n, 0:1],
                                                      rstd[:, n:n + 1], ALU.subtract, ALU.mult)
                    ins.then_inc(xn_done, 1)

                def route_group(G, i):
                    k = [0]

                    def then(ins):
                        k[0] += 1
                        ins.then_inc(route, 1)
                        dve.wait_ge(route, R * G + k[0])

                    v = nc.vector
                    mine = score[:, :, :, None].to_broadcast([P, TB, E, E])
                    other = score[:, :, None, :].to_broadcast([P, TB, E, E])
                    dve.wait_ge(ez_done, G + 1)
                    then(v.tensor_scalar(ez[:], ez[:], 1.0, None, ALU.add))
                    then(v.reciprocal(sig[:], ez[:]))
                    then(v.tensor_tensor(score[:], sig[:], bias_b[:, None, :].to_broadcast([P, TB, E]), ALU.add))
                    v.tensor_tensor(above[:], other, mine, ALU.is_gt)
                    then(v.tensor_tensor(equal[:], other, mine, ALU.is_equal))
                    then(v.tensor_tensor(equal[:], equal[:], lower[:, None, :, :].to_broadcast([P, TB, E, E]), ALU.mult))
                    then(v.tensor_tensor(above[:], above[:], equal[:], ALU.add))
                    then(v.tensor_reduce(rank[:], above[:], AX.X, ALU.add))
                    v.tensor_scalar(chosen_bf[:, 0:TB, :], rank[:], 1.5, None, ALU.is_lt).then_inc(chosen_done, 1)
                    for r in range(2):
                        v.tensor_scalar(is_rank[:, :, r, :], rank[:], float(r), None, ALU.is_equal)
                    then(v.scalar_tensor_tensor(weight[:], rank[:], 1.5, sig[:], ALU.is_lt, ALU.mult))
                    then(v.tensor_reduce(total[:], weight[:], AX.X, ALU.add))
                    then(v.reciprocal(inv[:], total[:]))
                    then(v.tensor_tensor(weight[:], weight[:], inv[:, :, None].to_broadcast([P, TB, E]), ALU.mult))
                    then(v.tensor_tensor(picked[:], is_rank[:], weight[:, :, None, :].to_broadcast([P, TB, 2, E]), ALU.mult))
                    then(v.tensor_reduce(xn[i][:, :, W0:W1 + 1], picked[:], AX.X, ALU.add))
                    then(v.tensor_tensor(place[:], is_rank[:, :, 0, :], expert_no[:, None, :].to_broadcast([P, TB, E]), ALU.mult))
                    then(v.tensor_reduce(xn[i][:, :, BEST], place[:], AX.X, ALU.add))
                    v.tensor_copy(xn[i][:, :, TOKEN], token[:])
                    dve.wait_ge(counted, G + 1)
                    then(v.tensor_tensor(place[:], ps_c[:, 0:TB, :], next_row[:, None, :].to_broadcast([P, TB, E]), ALU.add))
                    then(v.tensor_tensor(picked[:], is_rank[:], place[:, :, None, :].to_broadcast([P, TB, 2, E]), ALU.mult))
                    then(v.tensor_reduce(place_rank[:], picked[:], AX.X, ALU.add))
                    then(v.tensor_copy(place_int[i][:], place_rank[:]))
                    then(v.tensor_scalar(token[:], token[:], float(GT), None, ALU.add))
                    then(v.tensor_tensor(next_row[:], next_row[:], ps_c[:, TB, :], ALU.add))
                    assert k[0] == R
                    v.tensor_copy(total[:], place_rank[:, :, 0]).then_inc(placed, 1)

                def lows(G):
                    for j in range(KT):
                        dve.wait_ge(xT_high, KT * G + j + 1)
                        nc.vector.tensor_tensor(xT[1][:, j, :], ps_x[j][:], xT[0][:, j, :].bitcast(F32),
                                                ALU.subtract).then_inc(xT_low, 1)

                def group(G, t, i):
                    lows(G)
                    if not isinstance(G, int) or G < GROUPS - 1:
                        normalise(G + 1, t + i // 2, (i + 1) % 3)
                    route_group(G, i)

                def weights_low(e):
                    dve.wait_ge(w13_high, e + 1)
                    nc.vector.tensor_tensor(w13[1][:, e], w13_raw[:, e], w13[0][:, e].bitcast(F32),
                                            ALU.subtract).then_inc(w13_low, 1)

                dve.wait_ge(wg_high, 1)
                nc.vector.tensor_tensor(wg[1][:], wg_raw[:], wg[0][:].bitcast(F32), ALU.subtract).then_inc(wg_low, 1)
                normalise(0, 0, 0)
                dve.wait_ge(numbers, 4)
                nc.vector.tensor_copy(nums[:], nums_int[:]).then_inc(numbers, 1)
                dve.wait_ge(numbers, 5)
                dve.wait_ge(consts, 11)
                nc.vector.tensor_scalar(region_row[:], expert_no, float(REGION), None, ALU.mult)
                nc.vector.tensor_scalar(next_row[:], expert_no, float(REGION), None, ALU.mult)
                nc.vector.tensor_scalar(pad_rows[:, TOKEN:ROW], token_in_group[:, 0:1], float(T), None, ALU.add)
                nc.vector.tensor_copy(token[:], token_in_group).then_inc(numbers, 1)
                dve.wait_ge(numbers, 6)
                in_groups(dve, GROUPS, group)

                steps = [0]

                def then(ins):
                    steps[0] += 1
                    ins.then_inc(table, 1)
                    dve.wait_ge(table, steps[0])

                v = nc.vector
                v.tensor_tensor(pad_place[:], next_row[:], token_in_group[:, 0:1].to_broadcast([P, E]), ALU.add).then_inc(pads_placed, 1)
                then(v.tensor_tensor(n_rows[:], next_row[:], region_row[:], ALU.subtract))
                then(v.tensor_tensor(more_rows[:], n_rows[:, :, None].to_broadcast([P, E, STEPS]),
                                     times_128[:, None, :].to_broadcast([P, E, STEPS]), ALU.is_gt))
                v.memset(first_tile[:, 0:1], 0.0)
                then(v.tensor_reduce(n_tiles[:], more_rows[:], AX.X, ALU.add))
                for e in range(E):
                    then(v.tensor_tensor(first_tile[:, e + 1:e + 2], first_tile[:, e:e + 1], n_tiles[:, e:e + 1], ALU.add))
                then(v.tensor_tensor(started[:], tile_no[:, :, None].to_broadcast([P, TILES, E - 1]),
                                     first_tile[:, None, 1:E].to_broadcast([P, TILES, E - 1]), ALU.is_ge))
                then(v.tensor_reduce(tile_expert[:], started[:], AX.X, ALU.add))
                then(v.tensor_tensor(started[:], started[:], n_tiles[:, None, 0:E - 1].to_broadcast([P, TILES, E - 1]), ALU.mult))
                then(v.tensor_reduce(tile_first[:], started[:], AX.X, ALU.add))
                v.tensor_copy(tile_expert_int[:], tile_expert[:])
                v.tensor_scalar(tile_used[:], tile_no, first_tile[:, E:E + 1], None, ALU.is_lt)
                then(v.tensor_tensor(tile_first[:], tile_no, tile_first[:], ALU.subtract))
                then(v.tensor_scalar(tile_row[:], tile_expert[:], float(REGION), -float(PAD_ROW), ALU.mult, ALU.add))
                then(v.scalar_tensor_tensor(tile_row[:], tile_first[:], float(P), tile_row[:], ALU.mult, ALU.add))
                then(v.tensor_tensor(tile_row[:], tile_row[:], tile_used[:], ALU.mult))
                then(v.tensor_scalar(tile_row_int[:], tile_row[:], float(PAD_ROW), None, ALU.add))
                for e in range(E):
                    weights_low(e)
                dve.wait_ge(w13_low, E)

            @block.tensor
            def _(pe):
                def transposes(G, i):
                    pe.wait_ge(xn_done, G + 1)
                    for j in range(KT):
                        for n in range(TB):
                            ins = nc.tensor.transpose(ps_x[j][:, n * P:(n + 1) * P], xn[i][:, n, j * P:(j + 1) * P], ident[:])
                        ins.then_inc(xT_filled, 1)

                def group(G, t, i):
                    pe.wait_ge(xT_low, KT * (G + 1))
                    for b in range(TB):
                        for j in range(KT):
                            for m, (a, c) in enumerate(PASSES):
                                ins = nc.tensor.matmul(ps_r[:, b, :], xT[a][:, j, b * P:(b + 1) * P], wg[c][:, j, :],
                                                       start=(j == 0 and m == 0), stop=(j == KT - 1 and m == 2))
                        ins.then_inc(logits_done, 1)
                    if not isinstance(G, int) or G < GROUPS - 1:
                        transposes(G + 1, (i + 1) % 3)
                    pe.wait_ge(chosen_done, G + 1)
                    nc.tensor.matmul(ps_c[:], before_bf[:], chosen_bf[:], start=True, stop=False)
                    for s in range(1, TB + 1):
                        ins = nc.tensor.matmul(ps_c[:, s:, :], ones_bf[:], chosen_bf[:, 0:TB + 1 - s, :],
                                               start=False, stop=(s == TB))
                    ins.then_inc(counted, 1)

                pe.wait_ge(consts, 11)
                pe.wait_ge(wg_low, 1)
                transposes(0, 0)
                in_groups(pe, GROUPS, group)


def run_experts(nc, rows, y2, w13, w2, ident, tile_expert, tile_expert_int, tile_row_int,
                KT, FT, FF, T, H, E, W0, W1, BEST, TOKEN, ROW, TILES, PASSES):
    LAST_ROW = rows.shape[0] - P
    with ExitStack() as ctx:
        def sb(name, shape, dt=F32):
            return ctx.enter_context(nc.sbuf_tensor("e_" + name, shape, dt))

        def psum(name, shape):
            return ctx.enter_context(nc.psum_tensor("e_" + name, shape, F32))

        def sem(name):
            return ctx.enter_context(nc.semaphore("e_" + name))

        row = [sb(f"row{i}", [P, ROW]) for i in range(2)]
        xT = [sb(f"xT_{s}", [P, KT, P], F32R) for s in "hl"]
        gate = sb("gate", [P, FF])
        g = sb("g", [P, FF])
        gT = sb("gT", [P, FT, P])
        y = [sb(f"y{i}", [P, H]) for i in range(2)]
        is_best = sb("is_best", [P, 1])
        not_best = sb("not_best", [P, 1])
        best_weight = sb("best_weight", [P, 1])
        weight = [sb(f"weight{i}", [P, 1]) for i in range(2)]
        place = [sb(f"place{i}", [P, 1]) for i in range(2)]
        place_int = [sb(f"place_int{i}", [P, 1], I32) for i in range(2)]
        ps_x = [psum(f"ps_x{i}", [P, KT, P]) for i in range(2)]
        ps_h = [psum(f"ps_h{i}", [P, 2 * FF]) for i in range(2)]
        ps_g = psum("ps_g", [P, FT, P])
        ps_y = [psum(f"ps_y{i}", [P, H]) for i in range(2)]

        row_loaded = [sem(f"row_loaded{i}") for i in range(2)]
        x_transposed = sem("x_transposed")
        x_high = sem("x_high")
        x_low = sem("x_low")
        h_filled = sem("h_filled")
        gate_done = sem("gate_done")
        g_done = sem("g_done")
        g_transposed = sem("g_transposed")
        gT_done = sem("gT_done")
        y_filled = sem("y_filled")
        y_copied = sem("y_copied")
        y_out = sem("y_out")
        which = sem("which")
        meta_done = sem("meta_done")
        place_done = sem("place_done")

        with nc.Block() as block:
            @block.sync
            def _(sp):
                def tile(u, t, i):
                    if not isinstance(u, int) or u >= 2:
                        wait_alone(sp, meta_done, u - 1, (row_loaded[0], 16))
                    r = sp.value_load(tile_row_int[0:1, u:u + 1] if isinstance(u, int) else tile_row_int[0:1, bass.ds(u, 1)],
                                      min_val=0, max_val=LAST_ROW)
                    sp.dma_start(row[i][:], rows[bass.ds(r, P), :]).then_inc(row_loaded[i], 16)

                in_steps(sp, TILES, tile, last=0)

            @block.gpsimd
            def _(pool):
                def out(u, i):
                    wait_alone(pool, y_copied, u + 2, (y_copied, 1))
                    if not isinstance(u, int) or u:
                        wait_alone(pool, y_out, 16 * u, (y_copied, 1))
                    nc.gpsimd.indirect_dma_start(y2, bass.IndirectOffsetOnAxis(place_int[i][:], 0), y[i][:], None).then_inc(y_out, 16)

                def tile(u, t, i):
                    if not isinstance(u, int) or u:
                        out(u - 1, 1 - i)

                in_steps(pool, TILES, tile, first=4)
                out(TILES - 1, 1)
                pool.wait_ge(y_out, 16 * TILES)

            @block.scalar
            def _(act):
                def high(u, i):
                    act.wait_ge(x_transposed, u + 1)
                    nc.scalar.activation(xT[0][:], ps_x[i][:], ACT.Copy).then_inc(x_high, 1)

                def gT_copy(u):
                    act.wait_ge(g_transposed, u + 1)
                    nc.scalar.activation(gT[:], ps_g[:], ACT.Copy).then_inc(gT_done, 1)

                def tile(u, t, i):
                    if not isinstance(u, int) or u:
                        gT_copy(u - 1)
                    if not isinstance(u, int) or u < TILES - 1:
                        high(u + 1, 1 - i)
                    act.wait_ge(h_filled, u + 1)
                    nc.scalar.activation(gate[:], ps_h[i][:, 0:FF], ACT.Silu).then_inc(gate_done, 1)

                high(0, 0)
                in_steps(act, TILES, tile)
                gT_copy(TILES - 1)

            @block.vector
            def _(dve):
                S = 3

                def low(u, i):
                    dve.wait_ge(x_high, u + 1)
                    nc.vector.tensor_tensor(xT[1][:], ps_x[i][:], xT[0][:].bitcast(F32), ALU.subtract).then_inc(x_low, 1)

                def meta(u, t, i):
                    expert = tile_expert[:, u:u + 1] if isinstance(u, int) else tile_expert[:, bass.ds(u, 1)]
                    v = nc.vector
                    dve.wait_ge(row_loaded[i], 16 * (t + 1))
                    v.tensor_tensor(is_best[:], row[i][:, BEST:BEST + 1], expert, ALU.is_equal).then_inc(which, 1)
                    v.tensor_tensor(not_best[:], row[i][:, BEST:BEST + 1], expert, ALU.not_equal).then_inc(which, 1)
                    dve.wait_ge(which, S * u + 2)
                    v.tensor_tensor(best_weight[:], row[i][:, W0:W0 + 1], is_best[:], ALU.mult).then_inc(which, 1)
                    v.scalar_tensor_tensor(place[i][:], not_best[:], float(T), row[i][:, TOKEN:TOKEN + 1], ALU.mult, ALU.add)
                    dve.wait_ge(which, S * u + 3)
                    v.scalar_tensor_tensor(weight[i][:], row[i][:, W1:W1 + 1], not_best[:], best_weight[:],
                                           ALU.mult, ALU.add).then_inc(meta_done, 1)

                def y_copy(u, i):
                    if not isinstance(u, int) or u >= 2:
                        dve.wait_ge(y_out, 16 * (u - 1))
                    nc.vector.tensor_copy(place_int[i][:], place[i][:]).then_inc(place_done, 1)
                    dve.wait_ge(y_filled, u + 1)
                    nc.vector.tensor_copy(y[i][:], ps_y[i][:]).then_inc(y_copied, 1)

                def tile(u, t, i):
                    if not isinstance(u, int) or u < TILES - 1:
                        low(u + 1, 1 - i)
                    dve.wait_ge(gate_done, u + 1)
                    dve.wait_ge(meta_done, u + 1)
                    nc.vector.scalar_tensor_tensor(g[:], ps_h[i][:, FF:], weight[i][:], gate[:], ALU.mult,
                                                   ALU.mult).then_inc(g_done, 1)
                    if not isinstance(u, int) or u:
                        y_copy(u - 1, 1 - i)
                        dve.wait_ge(place_done, u)
                    if not isinstance(u, int) or u < TILES - 1:
                        meta(u + 1, t + i, 1 - i)

                dve.sem_inc(y_copied, 1)
                low(0, 0)
                meta(0, 0, 0)
                in_steps(dve, TILES, tile, first=4)
                y_copy(TILES - 1, 1)

            @block.tensor
            def _(pe):
                def transposes(u, t, i):
                    pe.wait_ge(row_loaded[i], 16 * (t + 1))
                    for j in range(KT):
                        ins = nc.tensor.transpose(ps_x[i][:, j, :], row[i][:, j * P:(j + 1) * P], ident[:])
                    ins.then_inc(x_transposed, 1)

                def g_transposes(u):
                    pe.wait_ge(g_done, u + 1)
                    for f in range(FT):
                        ins = nc.tensor.transpose(ps_g[:, f, :], g[:, f * P:(f + 1) * P], ident[:])
                    ins.then_inc(g_transposed, 1)

                def down(u, i, e):
                    pe.wait_ge(gT_done, u + 1)
                    if not isinstance(u, int) or u >= 2:
                        pe.wait_ge(y_copied, u)
                    for f in range(FT):
                        w = w2[:, e, f, :] if isinstance(e, int) else w2[:, bass.ds(e, 1), f, :].rearrange("p o h -> p (o h)")
                        ins = nc.tensor.matmul(ps_y[i][:], gT[:, f, :], w, start=(f == 0), stop=(f == FT - 1))
                    ins.then_inc(y_filled, 1)

                def expert_of(u):
                    at = tile_expert_int[0:1, u:u + 1] if isinstance(u, int) else tile_expert_int[0:1, bass.ds(u, 1)]
                    return pe.value_load(at, min_val=0, max_val=E - 1)

                def tile(u, t, i):
                    first = isinstance(u, int) and u == 0
                    e = expert_of(u)
                    e_before = None if first else expert_of(u - 1)
                    pe.wait_ge(x_low, u + 1)
                    m = 0
                    for j in range(KT):
                        for a, c in PASSES:
                            if m == 9 and not first:
                                g_transposes(u - 1)
                            ins = nc.tensor.matmul(ps_h[i][:], xT[a][:, j, :],
                                                   w13[c][:, bass.ds(e, 1), j, :].rearrange("p o f -> p (o f)"),
                                                   start=(m == 0), stop=(m == 3 * KT - 1))
                            m += 1
                    ins.then_inc(h_filled, 1)
                    if not isinstance(u, int) or u < TILES - 1:
                        transposes(u + 1, t + i, 1 - i)
                    if not first:
                        down(u - 1, 1 - i, e_before)

                transposes(0, 0, 0)
                in_steps(pe, TILES, tile)
                g_transposes(TILES - 1)
                down(TILES - 1, 1, expert_of(TILES - 1))


def combine(nc, x2_rows, y2, out_rows, T, H):
    B = 2
    SLOTS = 4
    STEPS = T // (B * P)

    def blocks(flat, n, base=0):
        return flat[bass.ds(n * (B * P) + base, B * P), :].rearrange("(p b) h -> p b h", b=B)

    x2_flat = x2_rows.rearrange("g n h -> (g n) h")
    out_flat = out_rows.rearrange("g n h -> (g n) h")
    with ExitStack() as ctx:
        def slots(name):
            return [ctx.enter_context(nc.sbuf_tensor(f"s_{name}{i}", [P, B, H], F32)) for i in range(SLOTS)]

        def sems(name):
            return [ctx.enter_context(nc.semaphore(f"s_{name}{i}")) for i in range(SLOTS)]

        x, y_best, y_second = slots("x"), slots("y_best"), slots("y_second")
        x_loaded, best_loaded, second_loaded = sems("x_loaded"), sems("best_loaded"), sems("second_loaded")
        stored = sems("stored")
        first_sum = ctx.enter_context(nc.semaphore("s_first_sum"))
        summed = ctx.enter_context(nc.semaphore("s_summed"))

        def in_fours(eng, step):
            for n in range(SLOTS):
                step(n, 0, n)
            with eng.Fori(1, STEPS // SLOTS) as t:
                for i in range(SLOTS):
                    step(SLOTS * t + i, t, i)

        with nc.Block() as block:
            @block.sync
            def _(sp):
                def load(n, t, i):
                    if not isinstance(n, int):
                        sp.wait_ge(stored[i], 16 * t)
                    sp.dma_start(x[i][:], blocks(x2_flat, n)).then_inc(x_loaded[i], 16)
                    sp.dma_start(y_best[i][:], blocks(y2, n)).then_inc(best_loaded[i], 16)
                    sp.dma_start(y_second[i][:], blocks(y2, n, T)).then_inc(second_loaded[i], 16)

                in_fours(sp, load)

            @block.vector
            def _(dve):
                def add(n, t, i):
                    dve.wait_ge(x_loaded[i], 16 * (t + 1))
                    dve.wait_ge(best_loaded[i], 16 * (t + 1))
                    nc.vector.tensor_tensor(x[i][:], x[i][:], y_best[i][:], ALU.add).then_inc(first_sum, 1)
                    dve.wait_ge(second_loaded[i], 16 * (t + 1))
                    dve.wait_ge(first_sum, n + 1)
                    nc.vector.tensor_tensor(x[i][:], x[i][:], y_second[i][:], ALU.add).then_inc(summed, 1)

                in_fours(dve, add)

            @block.scalar
            def _(act):
                def store(n, t, i):
                    act.wait_ge(summed, n + 1)
                    act.dma_start(blocks(out_flat, n), x[i][:]).then_inc(stored[i], 16)

                in_fours(act, store)
                for i in range(SLOTS):
                    act.wait_ge(stored[i], 16 * (STEPS // SLOTS))


def decoder_layer(nc, x, context, mask, mask_cols, a_wq, a_wkv, a_wd, x_wq, x_bq, x_wk, x_bk, x_wv, x_bv,
                  f_wg, f_w13, f_w2, f_bias, out):
    B, S, H = x.shape
    GROUPS = 4
    HEADS = a_wq.shape[1] // P
    x1 = nc.dram_tensor("x1", [B, S, H], F32, kind="Internal").ap()
    x2 = nc.dram_tensor("x2", [B, S, H], F32, kind="Internal").ap()
    aux = nc.dram_tensor("mask_rows_split", [B, 6, 2, H], F32, kind="Internal").ap()
    rinv = nc.dram_tensor("row_sum_inverses", [4, 4 * H], F32, kind="Internal").ap()

    def by_512(t):
        return t.rearrange("(g b) s h -> g (b s) h", b=BANK // S)

    attention_phase(nc, by_512(x), a_wq, a_wkv, a_wd, by_512(x1), B * S, H, S, HEADS, GROUPS)
    cross_attention_phase(nc, x1, context, mask, mask_cols, x_wq, x_bq, x_wk, x_bk, x_wv, x_bv, aux, rinv, x2)
    experts_phase(nc, by_512(x2), f_wg, f_w13, f_w2, f_bias, by_512(out), *experts_scratch(nc))


def kernel(**inputs):
    import numpy as np
    import concourse.bacc as bacc
    from concourse.bass_utils import run_bass_kernel_spmd

    a = {name: np.asarray(value) for name, value in inputs.items()}
    B, S, H = a["x"].shape
    C = a["L0_xattn_Wq"].shape[0]
    mask = a["mask_Bx1x2048_fk1"].reshape(B, H)

    def by_quads(w):
        return w.reshape(4, 4, 16, -1).transpose(0, 2, 1, 3).reshape(C, -1)

    laid = {
        "x": a["x"],
        "context": a["ctx_2048"],
        "mask": mask,
        "mask_cols": mask.reshape(B, H // 128, 128).transpose(0, 2, 1),
        "a_wq": a["L0_attn_w_q"],
        "a_wkv": a["L0_attn_w_kv"],
        "a_wd": a["L0_attn_w_dense"],
        "x_wq": by_quads(a["L0_xattn_Wq"]).T,
        "x_bq": by_quads(a["L0_xattn_bq"]).reshape(C // 128, 128).T,
        "x_wk": by_quads(a["L0_xattn_Wk"]).T,
        "x_bk": by_quads(a["L0_xattn_bk"]).reshape(C // 128, 128).T,
        "x_wv": a["L0_xattn_Wv"].T,
        "x_bv": a["L0_xattn_bv"].reshape(1, C),
        "f_wg": a["L0_ffn_Wg"].T,
        "f_w13": np.concatenate([a["L0_ffn_W1"], a["L0_ffn_W3"]], axis=1).transpose(0, 2, 1),
        "f_w2": a["L0_ffn_W2"].transpose(0, 2, 1),
        "f_bias": a["L0_ffn_bias"].reshape(1, -1),
    }
    nc = bacc.Bacc("TRN2", target_bir_lowering=False, num_devices=1)
    arrays = {f"in_{name}": np.ascontiguousarray(value) for name, value in laid.items()}
    args = [nc.dram_tensor(f"in_{name}", list(arrays[f"in_{name}"].shape), F32, kind="ExternalInput").ap() for name in laid]
    out = nc.dram_tensor("out", [B, S, H], F32, kind="ExternalOutput").ap()
    decoder_layer(nc, *args, out)
    r = run_bass_kernel_spmd(nc, [arrays], core_ids=[0])
    return r.results[0]["out"]
```

```python
from contextlib import ExitStack

import concourse.bass as bass
from concourse import mybir

F32 = mybir.dt.float32
F32R = mybir.dt.float32r
BF16 = mybir.dt.bfloat16
I32 = mybir.dt.int32
ACT = mybir.ActivationFunctionType
ALU = mybir.AluOpType
AX = mybir.AxisListType

P = 128
BANK = 512
LN_EPS = 1e-5


def wait_alone(eng, sem, value, past):
    if not isinstance(value, int):
        value = eng.to_reg(value)
    eng.wait_ge(*past)
    eng.wait_ge(sem, value)


def attention_phase(nc, x_rows, w_q, w_kv, w_dense, x1_rows, TOKENS, HIDDEN, SEQ, HEADS, GROUPS):
    D = P
    HALVES = 2
    G = GROUPS // HALVES
    HPG = HEADS // GROUPS
    NH = G * HPG
    TB = BANK // P
    KT = HIDDEN // P
    PAIRS = TOKENS // BANK
    UNITS = 2 * NH
    SCALE = float(D) ** -0.5
    FILLS = 16
    assert SEQ == 2 * P and FILLS == KT + G + TB // 2 + NH
    QW, KVW = NH * D, 2 * G * D
    XT_STEPS = {UNITS - 2: (0, 2), UNITS - 1: (2, KT)}
    NEG = -1.0e30

    with ExitStack() as ctx:
        def sb(name, shape, dt=F32):
            return ctx.enter_context(nc.sbuf_tensor(name, shape, dt))

        def psum(name, shape):
            return ctx.enter_context(nc.psum_tensor(name, shape, F32))

        def sem(name):
            return ctx.enter_context(nc.semaphore("a_" + name))

        def split_weights(name, shape):
            high = sb(name + "_h", shape, F32R)
            with nc.sbuf_tensor(name + "_raw", shape, F32) as raw:
                pass
            return [high, sb(name + "_l", shape, F32R)], raw

        wq, wq_raw = split_weights("wq", [P, KT, QW])
        wkv, wkv_raw = split_weights("wkv", [P, KT, KVW])
        wd, wd_raw = split_weights("wd", [P, NH, HIDDEN])
        x_in = sb("x_in", [P, TB, HIDDEN])
        acc = sb("acc", [P, TB, HIDDEN])
        xn = sb("xn", [P, TB, HIDDEN])
        xT = [sb(f"xT_{s}", [P, KT, BANK], F32R) for s in "hl"]
        kT = [sb(f"kT_{s}", [P, G, BANK], F32R) for s in "hl"]
        v = [sb(f"v_{s}", [P, TB, G * D], F32R) for s in "hl"]
        qT = [sb(f"qT_{s}", [P, 2, BANK], F32R) for s in "hl"]
        probs = sb("probs", [P, 2, 3 * P])
        pT = [sb(f"pT_{s}", [P, 2, 3 * P], F32R) for s in "hl"]
        cT = [sb(f"cT_{s}", [P, G, HPG, BANK], F32R) for s in "hl"]
        ident = sb("ident", [P, P])
        ident_b = sb("ident_b", [P, P], BF16)
        causal = sb("causal", [P, P], BF16)
        stats = sb("stats", [P, TB, 6])
        mv = sb("mv", [P, TB, 2])
        veps = sb("veps", [P, TB])
        minus_half = sb("minus_half", [P, TB])
        negmax = sb("negmax", [P, 2, 2])
        rowsum = sb("rowsum", [P, 2, 2])
        rinv = sb("rinv", [P, 2, 2])

        ps_proj = [psum(f"ps_proj{i}", [P, BANK]) for i in range(2)]
        ps_s = [psum(f"ps_s{i}", [P, BANK]) for i in range(2)]
        ps_pT = [psum(f"ps_pT{i}", [P, BANK]) for i in range(2)]
        ps_c = psum("ps_c", [P, BANK])
        ps_d = psum("ps_d", [P, BANK])

        consts = sem("consts")
        w_loaded = [sem(f"w_loaded{n}") for n in range(6)]
        w_high = sem("w_high")
        w_low = sem("w_low")
        x_loaded = sem("x_loaded")
        acc_loaded = sem("acc_loaded")
        stored = sem("stored")
        stats_done = sem("stats_done")
        aggr_done = sem("aggr_done")
        veps_done = sem("veps_done")
        rstd_done = sem("rstd_done")
        xn_done = sem("xn_done")
        proj_filled = sem("proj_filled")
        proj_high = sem("proj_high")
        proj_low = sem("proj_low")
        s_filled = sem("s_filled")
        max_done = sem("max_done")
        exp_done = sem("exp_done")
        rinv_done = sem("rinv_done")
        probs_done_first = sem("probs_done_first")
        probs_done = sem("probs_done")
        pT_filled = sem("pT_filled")
        pT_high = sem("pT_high")
        pT_low = sem("pT_low")
        c_filled = sem("c_filled")
        c_high = sem("c_high")
        c_low = sem("c_low")
        d_filled = sem("d_filled")
        d_added = sem("d_added")

        def dense_bank(g, n):
            return ps_c if g == G - 1 and n % 2 else ps_d

        def tokens(rows, pair):
            return rows[pair].rearrange("(n p) h -> p n h", p=P)

        def chunks(half):
            out = []
            for part in range(2):
                at = (slice(None), slice(None), slice(part * G * D, (part + 1) * G * D))
                c0 = (part * GROUPS + half * G) * D
                out.append((wkv[0][at], wkv[1][at], wkv_raw[at],
                            w_kv[:, c0:c0 + G * D].rearrange("(k p) e -> p k e", p=P)))
            for part in range(2):
                k0, k1 = part * KT // 2, (part + 1) * KT // 2
                at = (slice(None), slice(k0, k1), slice(None))
                out.append((wq[0][at], wq[1][at], wq_raw[at],
                            w_q[k0 * P:k1 * P, half * QW:(half + 1) * QW].rearrange("(k p) e -> p k e", p=P)))
            for part in range(2):
                h0, h1 = part * NH // 2, (part + 1) * NH // 2
                at = (slice(None), slice(h0, h1), slice(None))
                out.append((wd[0][at], wd[1][at], wd_raw[at],
                            w_dense[(half * NH + h0) * D:(half * NH + h1) * D, :].rearrange("(k p) e -> p k e", p=P)))
            return out

        KV, QUERY, DENSE = (0, 1), (2, 3), (4, 5)
        NCH = len(chunks(0))
        SPLIT_AT_TURN = ({6: 0, 7: 1, UNITS - 1: 2}, {7: 0, 8: 1})
        SPLIT_AT_FRESH = ({6: 4, 7: 5}, {7: 4, 8: 5})

        def pairs(body):
            def run(eng):
                with eng.Fori(0, PAIRS - 1) as t:
                    body(t, "plain", 0)
                body(PAIRS - 1, "turn", 0)
                body(PAIRS, "fresh", 1)
                with eng.Fori(PAIRS + 1, HALVES * PAIRS - 1) as t:
                    body(t, "plain", 1)
                body(HALVES * PAIRS - 1, "last", 1)
            return run

        assert HALVES == 2

        with nc.Block() as block:
            @block.sync
            def _(sp):
                sp.sem_inc(stored, 16)

                def load_weights(half, which):
                    for n in which:
                        _high, _low, raw, src = chunks(half)[n]
                        sp.dma_start(raw, src).then_inc(w_loaded[n], 16)

                sp.dma_start(x_in[:], tokens(x_rows, 0)).then_inc(x_loaded, 16)
                load_weights(0, KV)
                load_weights(0, QUERY)
                load_weights(0, DENSE)

                def body(t, kind, half):
                    if kind != "last":
                        wait_alone(sp, xn_done, TB * (t + 1), (consts, 6))
                        nxt = 0 if kind == "turn" else t + 1 - half * PAIRS
                        sp.dma_start(x_in[:], tokens(x_rows, nxt)).then_inc(x_loaded, 16)
                    if kind == "fresh":
                        load_weights(1, DENSE)
                    if kind == "turn":
                        sp.wait_ge(proj_filled, FILLS * t + KT + G + 2)
                        load_weights(1, KV)
                    wait_alone(sp, stored, 16 * (t + 1), (consts, 6))
                    rows = x_rows if half == 0 else x1_rows
                    sp.dma_start(acc[:], tokens(rows, t - half * PAIRS)).then_inc(acc_loaded, 16)
                    if kind == "turn":
                        sp.wait_ge(proj_filled, FILLS * (t + 1))
                        load_weights(1, QUERY)
                    wait_alone(sp, d_added, G * TB * (t + 1) + 1, (consts, 6))
                    sp.dma_start(tokens(x1_rows, t - half * PAIRS), acc[:]).then_inc(stored, 16)

                pairs(body)(sp)
                sp.wait_ge(stored, 16 * (HALVES * PAIRS + 1))

            @block.gpsimd
            def _(pool):
                nc.gpsimd.memset(ident[:], 0.0).then_inc(consts, 1)
                nc.gpsimd.memset(causal[:], 0.0).then_inc(consts, 1)
                nc.gpsimd.memset(minus_half[:], -0.5).then_inc(consts, 1)
                pool.wait_ge(consts, 3)
                nc.gpsimd.affine_select(out=ident[:], in_=ident[:], compare_op=ALU.not_equal, fill=1.0, base=0,
                                        pattern=[[-1, P]], channel_multiplier=1).then_inc(consts, 1)
                nc.gpsimd.affine_select(out=causal[:], in_=causal[:], compare_op=ALU.is_ge, fill=NEG, base=0,
                                        pattern=[[-1, P]], channel_multiplier=1).then_inc(consts, 1)
                pool.wait_ge(consts, 5)
                nc.gpsimd.tensor_copy(ident_b[:], ident[:]).then_inc(consts, 1)

                def norm_scale(t):
                    wait_alone(pool, aggr_done, TB * (t + 1), (consts, 6))
                    nc.gpsimd.tensor_scalar(veps[:], mv[:, :, 1], LN_EPS, None, ALU.add).then_inc(veps_done, 1)
                    pool.wait_ge(veps_done, t + 1)
                    nc.gpsimd.tensor_tensor(veps[:], veps[:], minus_half[:], ALU.pow).then_inc(rstd_done, 1)

                norm_scale(0)

                def body(t, kind, half):
                    for u in range(UNITS):
                        s = u % 2
                        wait_alone(pool, rinv_done, UNITS * t + u + 1, (consts, 6))
                        nc.gpsimd.tensor_scalar(probs[:, s, P:3 * P], probs[:, s, P:3 * P], rinv[:, s, 1:2], None,
                                                ALU.mult).then_inc(probs_done, 1)
                        if u == TB + 3 and kind != "last":
                            norm_scale(t + 1)

                pairs(body)(pool)

            @block.scalar
            def _(act):
                def inputs_high(t):
                    for j in range(KT):
                        act.wait_ge(proj_filled, FILLS * t + j + 1)
                        nc.scalar.activation(xT[0][:, j, :], ps_proj[j % 2][:], ACT.Copy).then_inc(proj_high, 1)

                def keys_high(t):
                    for g in range(G):
                        act.wait_ge(proj_filled, FILLS * t + KT + g + 1)
                        nc.scalar.activation(kT[0][:, g, :], ps_proj[g % 2][:], ACT.Copy).then_inc(proj_high, 1)

                def values(t, n):
                    act.wait_ge(proj_filled, FILLS * t + KT + G + n + 1)
                    nc.scalar.activation(v[0][:, 2 * n:2 * n + 2, :], ps_proj[n % 2][:], ACT.Copy).then_inc(proj_high, 1)

                def query(t, m):
                    act.wait_ge(proj_filled, FILLS * t + 8 + m + 1)
                    nc.scalar.activation(qT[0][:, m % 2, :], ps_proj[m % 2][:], ACT.Copy, scale=SCALE).then_inc(proj_high, 1)

                def probs_transposed(t, u):
                    act.wait_ge(pT_filled, UNITS * t + u + 1)
                    nc.scalar.activation(pT[0][:, u % 2, :], ps_pT[u % 2][:, 0:3 * P], ACT.Copy).then_inc(pT_high, 1)

                def exponentials(t, u):
                    s = u % 2
                    act.wait_ge(max_done, UNITS * t + u + 1)
                    nc.scalar.activation(probs[:, s, 0:P], ps_s[s][:, 0:P], ACT.Exp, bias=negmax[:, s, 0:1],
                                         accum_out=rowsum[:, s, 0:1])
                    nc.scalar.activation(probs[:, s, P:3 * P], ps_s[s][:, P:3 * P], ACT.Exp,
                                         bias=negmax[:, s, 1:2], accum_out=rowsum[:, s, 1:2]).then_inc(exp_done, 1)

                def context(t, n):
                    act.wait_ge(c_filled, NH * t + n + 1)
                    nc.scalar.activation(cT[0][:, n // HPG, n % HPG, :], ps_c[:], ACT.Copy).then_inc(c_high, 1)

                def weights_high(half, n):
                    high, _low, raw, _src = chunks(half)[n]
                    act.wait_ge(w_loaded[n], 16 * (half + 1))
                    nc.scalar.activation(high, raw, ACT.Copy).then_inc(w_high, 1)

                for n in KV:
                    weights_high(0, n)
                inputs_high(0)
                for n in QUERY:
                    weights_high(0, n)
                keys_high(0)
                for n in range(2):
                    weights_high(0, DENSE[n])
                    values(0, n)
                query(0, 0)
                exponentials(0, 0)

                def body(t, kind, half):
                    last = kind == "last"
                    for u in range(UNITS):
                        if u:
                            exponentials(t, u)
                        if u % 2 == 0 and u // 2 + 1 < NH:
                            query(t, u // 2 + 1)
                        if u % 2 == 1 and u >= 3:
                            context(t, (u - 3) // 2)
                        if u >= 1:
                            probs_transposed(t, u - 1)
                        if u in XT_STEPS and not last:
                            for j in range(*XT_STEPS[u]):
                                act.wait_ge(proj_filled, FILLS * (t + 1) + j + 1)
                                nc.scalar.activation(xT[0][:, j, :], ps_proj[j % 2][:], ACT.Copy).then_inc(proj_high, 1)
                        if kind == "turn" and u in SPLIT_AT_TURN[0]:
                            weights_high(1, SPLIT_AT_TURN[0][u])
                        if kind == "fresh" and u in SPLIT_AT_FRESH[0]:
                            weights_high(1, SPLIT_AT_FRESH[0][u])
                    probs_transposed(t, UNITS - 1)
                    if kind == "turn":
                        weights_high(1, QUERY[1])
                    if not last:
                        for g in range(G):
                            act.wait_ge(proj_filled, FILLS * (t + 1) + KT + g + 1)
                            nc.scalar.activation(kT[0][:, g, :], ps_proj[g % 2][:], ACT.Copy).then_inc(proj_high, 1)
                    context(t, NH - 1)
                    if not last:
                        for n in range(2):
                            values(t + 1, n)
                        query(t + 1, 0)
                        exponentials(t + 1, 0)

                pairs(body)(act)

            @block.vector
            def _(dve):
                def low(dst, ps, h):
                    return nc.vector.tensor_tensor(dst, ps, h.bitcast(F32), ALU.subtract)

                def row_stats(t, n):
                    if n == 0:
                        dve.wait_ge(x_loaded, 16 * (t + 1))
                    nc.vector.bn_stats(stats[:, n, :], x_in[:, n, :]).then_inc(stats_done, 1)

                def mean_and_variance(t):
                    wait_alone(dve, stats_done, TB * (t + 1), (consts, 6))
                    for n in range(TB):
                        nc.vector.bn_aggr(mv[:, n, :], stats[:, n, :]).then_inc(aggr_done, 1)

                def apply_norm(t, n):
                    if n == 0:
                        dve.wait_ge(rstd_done, t + 1)
                    nc.vector.tensor_scalar(xn[:, n, :], x_in[:, n, :], mv[:, n, 0:1], veps[:, n:n + 1],
                                            ALU.subtract, ALU.mult).then_inc(xn_done, 1)

                def xT_low(t, j0=0, j1=KT):
                    for j in range(j0, j1):
                        dve.wait_ge(proj_high, FILLS * t + j + 1)
                        low(xT[1][:, j, :], ps_proj[j % 2][:], xT[0][:, j, :]).then_inc(proj_low, 1)

                def k_low(t):
                    for g in range(G):
                        dve.wait_ge(proj_high, FILLS * t + KT + g + 1)
                        low(kT[1][:, g, :], ps_proj[g % 2][:], kT[0][:, g, :]).then_inc(proj_low, 1)

                def v_low(t, n):
                    dve.wait_ge(proj_high, FILLS * t + KT + G + n + 1)
                    src = v[0][:, 2 * n:2 * n + 2, :].rearrange("p a b -> p (a b)")
                    dst = v[1][:, 2 * n:2 * n + 2, :].rearrange("p a b -> p (a b)")
                    low(dst, ps_proj[n % 2][:], src).then_inc(proj_low, 1)

                def q_low(t, m):
                    dve.wait_ge(proj_high, FILLS * t + 8 + m + 1)
                    nc.vector.scalar_tensor_tensor(qT[1][:, m % 2, :], ps_proj[m % 2][:], SCALE,
                                                   qT[0][:, m % 2, :].bitcast(F32), ALU.mult,
                                                   ALU.subtract).then_inc(proj_low, 1)

                def maxima(t, u):
                    s = u % 2
                    dve.wait_ge(s_filled, UNITS * t + u + 1)
                    nc.vector.tensor_reduce(negmax[:, s, 0:1], ps_s[s][:, 0:P], AX.X, ALU.max, negate=True)
                    nc.vector.tensor_reduce(negmax[:, s, 1:2], ps_s[s][:, P:3 * P], AX.X, ALU.max,
                                            negate=True).then_inc(max_done, 1)

                def normaliser(t, u):
                    s = u % 2
                    dve.wait_ge(exp_done, UNITS * t + u + 1)
                    nc.vector.reciprocal(rinv[:, s, :], rowsum[:, s, :]).then_inc(rinv_done, 1)
                    dve.wait_ge(rinv_done, UNITS * t + u + 1)
                    nc.vector.tensor_scalar(probs[:, s, 0:P], probs[:, s, 0:P], rinv[:, s, 0:1], None,
                                            ALU.mult).then_inc(probs_done_first, 1)

                def pT_low_part(t, u):
                    dve.wait_ge(pT_high, UNITS * t + u + 1)
                    low(pT[1][:, u % 2, :], ps_pT[u % 2][:, 0:3 * P], pT[0][:, u % 2, :]).then_inc(pT_low, 1)

                def c_low_part(t, n):
                    dve.wait_ge(c_high, NH * t + n + 1)
                    low(cT[1][:, n // HPG, n % HPG, :], ps_c[:], cT[0][:, n // HPG, n % HPG, :]).then_inc(c_low, 1)

                def add_dense(t, g, n):
                    if g == 0 and n == 0:
                        dve.wait_ge(acc_loaded, 16 * (t + 1))
                    dve.wait_ge(d_filled, TB * (G * t + g) + n + 1)
                    nc.vector.tensor_tensor(acc[:, n, :], dense_bank(g, n)[:], acc[:, n, :], ALU.add).then_inc(d_added, 1)

                dve.sem_inc(c_low, 1)
                dve.sem_inc(d_added, 1)
                def weights_low(half, n):
                    high, low_part, raw, _src = chunks(half)[n]
                    dve.wait_ge(w_high, half * NCH + n + 1)
                    nc.vector.tensor_tensor(low_part, raw, high.bitcast(F32), ALU.subtract).then_inc(w_low, 1)

                for n in range(TB):
                    row_stats(0, n)
                mean_and_variance(0)
                for n in range(TB):
                    apply_norm(0, n)
                for n in KV:
                    weights_low(0, n)
                xT_low(0)
                for n in QUERY:
                    weights_low(0, n)
                k_low(0)
                for n in range(2):
                    weights_low(0, DENSE[n])
                    v_low(0, n)
                q_low(0, 0)
                maxima(0, 0)
                normaliser(0, 0)

                def body(t, kind, half):
                    last = kind == "last"
                    for u in range(UNITS):
                        if u:
                            maxima(t, u)
                        if not last:
                            if 3 <= u < 3 + TB:
                                row_stats(t + 1, u - 3)
                            if u == TB + 3:
                                mean_and_variance(t + 1)
                            if TB + 5 <= u < 2 * TB + 5:
                                apply_norm(t + 1, u - TB - 5)
                        if u:
                            normaliser(t, u)
                        if u % 2 == 0 and u // 2 + 1 < NH:
                            q_low(t, u // 2 + 1)
                        if u % 2 == 1 and u >= 3:
                            c_low_part(t, (u - 3) // 2)
                        if u >= 1:
                            pT_low_part(t, u - 1)
                        if not last:
                            if u in XT_STEPS:
                                xT_low(t + 1, *XT_STEPS[u])
                        if kind == "turn" and u in SPLIT_AT_TURN[1]:
                            weights_low(1, SPLIT_AT_TURN[1][u])
                        if kind == "fresh" and u in SPLIT_AT_FRESH[1]:
                            weights_low(1, SPLIT_AT_FRESH[1][u])
                        if UNITS - 4 <= u:
                            add_dense(t, 0, u - (UNITS - 4))
                    pT_low_part(t, UNITS - 1)
                    if kind == "turn":
                        for n in QUERY:
                            weights_low(1, n)
                    if not last:
                        k_low(t + 1)
                    c_low_part(t, NH - 1)
                    if not last:
                        v_low(t + 1, 0)
                    add_dense(t, 1, 0)
                    if not last:
                        v_low(t + 1, 1)
                    add_dense(t, 1, 1)
                    if not last:
                        q_low(t + 1, 0)
                        maxima(t + 1, 0)
                        normaliser(t + 1, 0)
                    for n in range(2, TB):
                        add_dense(t, 1, n)

                pairs(body)(dve)

            @block.tensor
            def _(pe):
                def product3(out, w, w_at, m, m_at, first=True, last=True):
                    for a, b, st, en in ((0, 0, first, False), (0, 1, False, False), (1, 0, False, last)):
                        ins = nc.tensor.matmul(out, w[a][w_at], m[b][m_at], start=st, stop=en)
                    return ins

                def bank_free(F):
                    if isinstance(F, int) and F < 2:
                        return
                    pe.wait_ge(proj_low, F - 1)

                def xT_fill(t, j0=0, j1=KT):
                    if j0 == 0:
                        pe.wait_ge(xn_done, TB * (t + 1))
                    for j in range(j0, j1):
                        bank_free(FILLS * t + j)
                        for n in range(TB):
                            ins = nc.tensor.transpose(ps_proj[j % 2][:, n * P:(n + 1) * P], xn[:, n, j * P:(j + 1) * P], ident[:])
                        ins.then_inc(proj_filled, 1)

                def k_fill(t, g):
                    if g == 0:
                        pe.wait_ge(proj_low, FILLS * t + KT)
                    bank_free(FILLS * t + KT + g)
                    for kt in range(KT):
                        ins = product3(ps_proj[g % 2][:], wkv, (slice(None), kt, slice(g * D, (g + 1) * D)),
                                       xT, (slice(None), kt, slice(None)), kt == 0, kt == KT - 1)
                    ins.then_inc(proj_filled, 1)

                def v_fill(t, n):
                    bank_free(FILLS * t + KT + G + n)
                    for i in range(2):
                        blk = 2 * n + i
                        for kt in range(KT):
                            ins = product3(ps_proj[n % 2][:, i * G * D:(i + 1) * G * D],
                                           xT, (slice(None), kt, slice(blk * P, (blk + 1) * P)),
                                           wkv, (slice(None), kt, slice(G * D, 2 * G * D)), kt == 0, kt == KT - 1)
                    ins.then_inc(proj_filled, 1)

                def q_fill(t, m, part):
                    if part == 0:
                        bank_free(FILLS * t + 8 + m)
                    for kt in range(part * KT // 2, (part + 1) * KT // 2):
                        ins = product3(ps_proj[m % 2][:], wq, (slice(None), kt, slice(m * D, (m + 1) * D)),
                                       xT, (slice(None), kt, slice(None)), kt == 0, kt == KT - 1)
                    if part == 1:
                        ins.then_inc(proj_filled, 1)

                def scores(t, u):
                    m, b = u // 2, u % 2
                    g, s = m // HPG, u % 2
                    if b == 0:
                        pe.wait_ge(proj_low, FILLS * t + 8 + m + 1)
                    for qb in range(2):
                        c0, n = qb * P, (qb + 1) * P
                        q0 = b * SEQ + qb * P
                        product3(ps_s[s][:, c0:c0 + n], qT, (slice(None), m % 2, slice(q0, q0 + P)),
                                 kT, (slice(None), g, slice(b * SEQ, b * SEQ + n)), True, False)
                        ins = nc.tensor.matmul(ps_s[s][:, c0 + n - P:c0 + n], ident_b[:], causal[:], start=False, stop=True)
                    ins.then_inc(s_filled, 1)

                def first_scores(t):
                    for part in range(2):
                        q_fill(t, 0, part)
                    q_fill(t, 1, 0)
                    scores(t, 0)

                def transposes(t, u):
                    s = u % 2
                    pe.wait_ge(probs_done_first, UNITS * t + u + 1)
                    pe.wait_ge(probs_done, UNITS * t + u + 1)
                    for j in range(3):
                        ins = nc.tensor.transpose(ps_pT[s][:, j * P:(j + 1) * P], probs[:, s, j * P:(j + 1) * P], ident[:])
                    ins.then_inc(pT_filled, 1)

                def values_product(t, u):
                    m, b = u // 2, u % 2
                    g, s = m // HPG, u % 2
                    pe.wait_ge(pT_low, UNITS * t + u + 1)
                    if b == 0:
                        pe.wait_ge(c_low, NH * t + m + 1)
                        if m == 0:
                            pe.wait_ge(d_added, TB * G * t + 1)
                    vs = slice(g * D, (g + 1) * D)
                    product3(ps_c[:, b * SEQ:(b + 1) * SEQ], v, (slice(None), 2 * b, vs),
                             pT, (slice(None), s, slice(0, 2 * P)), True, False)
                    ins = product3(ps_c[:, b * SEQ + P:(b + 1) * SEQ], v, (slice(None), 2 * b + 1, vs),
                                   pT, (slice(None), s, slice(2 * P, 3 * P)), False, True)
                    if b == 1:
                        ins.then_inc(c_filled, 1)

                def dense(t, g, n):
                    if n == 0:
                        pe.wait_ge(c_low, NH * t + (g + 1) * HPG + 1)
                    if g < G - 1:
                        pe.wait_ge(d_added, TB * (G * t + g) + n + 1)
                    elif n == 0:
                        pe.wait_ge(d_added, TB * (G * t + g) + 1)
                    elif n >= 2:
                        pe.wait_ge(d_added, TB * (G * t + g) + n - 1 + 1)
                    for j in range(HPG):
                        ins = product3(dense_bank(g, n)[:], cT, (slice(None), g, j, slice(n * P, (n + 1) * P)),
                                       wd, (slice(None), g * HPG + j, slice(None)), j == 0, j == HPG - 1)
                    ins.then_inc(d_filled, 1)

                pe.wait_ge(consts, 6)
                xT_fill(0)
                pe.wait_ge(w_low, KV[-1] + 1)
                for g in range(G):
                    k_fill(0, g)
                for n in range(2):
                    v_fill(0, n)
                pe.wait_ge(w_low, QUERY[-1] + 1)
                first_scores(0)

                def body(t, kind, half):
                    last = kind == "last"
                    for u in range(UNITS):
                        if u:
                            scores(t, u)
                        if u % 2 == 0 and u // 2 + 1 < NH:
                            q_fill(t, u // 2 + 1, 1)
                        if u % 2 == 1 and u // 2 + 2 < NH:
                            q_fill(t, u // 2 + 2, 0)
                        if u % 2 and u >= 2:
                            values_product(t, u - 2)
                        if u >= 1:
                            transposes(t, u - 1)
                        if u % 2 == 0 and u >= 2:
                            values_product(t, u - 2)
                        if u in XT_STEPS and not last:
                            xT_fill(t + 1, *XT_STEPS[u])
                        if u == UNITS - 4:
                            pe.wait_ge(w_low, NCH * (half + 1))
                        if UNITS - 4 <= u:
                            dense(t, 0, u - (UNITS - 4))
                    transposes(t, UNITS - 1)
                    if kind == "turn":
                        pe.wait_ge(w_low, NCH + KV[-1] + 1)
                    if not last:
                        k_fill(t + 1, 0)
                    values_product(t, UNITS - 2)
                    if not last:
                        k_fill(t + 1, 1)
                    values_product(t, UNITS - 1)
                    if not last:
                        v_fill(t + 1, 0)
                    dense(t, 1, 0)
                    if not last:
                        v_fill(t + 1, 1)
                    dense(t, 1, 1)
                    if kind == "turn":
                        pe.wait_ge(w_low, NCH + QUERY[-1] + 1)
                    if not last:
                        first_scores(t + 1)
                    for n in range(2, TB):
                        dense(t, 1, n)

                pairs(body)(pe)


def cross_attention_phase(nc, x1_seq, context_seq, mask, mask_cols, w_qT, b_q, w_kT, b_k, w_vT, b_v, aux_dram, rinv_dram, x2_seq):
    B, C, T = x1_seq.shape
    DH = 16
    HQ = 4
    QUADS = C // (DH * HQ)
    CT = C // P
    TBL = T // P
    AUX, AUXROWS = 3 * DH, 6
    MAXROW = 96
    NEG4 = -4.0e6
    AUX_STEPS = 11
    TC = T // 32
    FILLS = 10
    PRO = 7
    assert T == BANK and DH == 16 and QUADS == 4 and CT == 2

    with ExitStack() as ctx:
        def sb(name, shape, dt=F32):
            return ctx.enter_context(nc.sbuf_tensor("b_" + name, shape, dt))

        def psum(name, shape):
            return ctx.enter_context(nc.psum_tensor("b_" + name, shape, F32))

        def sem(name):
            return ctx.enter_context(nc.semaphore("b_" + name))

        stack = sb("stack", [P, QUADS, 2, HQ, T], F32R)
        probs = sb("probs", [P, 2, HQ, T])
        v_stack = sb("v_stack", [P, TBL, C // DH, 32])
        v_raw = sb("v_raw", [P, TBL, C])
        w = {n: [sb(f"w{n}_{s}", [P, CT, C], F32R) for s in "hl"] for n in "qkv"}
        w_stage = sb("w_stage", [P, 3, CT, C])
        bias = {n: sb(f"bias_{n}", [P, CT]) for n in "qk"}
        bias_v = sb("bias_v", [P, C])
        x_in = sb("x_in", [P, CT, T])
        c_in = sb("c_in", [P, CT, T])
        xn = sb("xn", [P, CT, T])
        xs = [sb(f"x_{s}", [P, CT, T], F32R) for s in "hl"]
        cs = [sb(f"c_{s}", [P, CT, T], F32R) for s in "hl"]
        raw = {n: sb(f"raw_{n}", [P, T]) for n in "qk"}
        tile = {n: [[sb(f"{n}{half}_{s}", [P, T], F32R) for s in "hl"] for half in range(2)] for n in "qk"}
        mask_b = sb("mask_b", [P, T])
        mask_col = sb("mask_col", [P, TBL])
        mask_r = sb("mask_r", [P, TC])
        mask_rows, one_minus, neg_row = (probs[0:B, 0, i, :] for i in range(3))
        stats = sb("stats", [P, CT, 6])
        mv = sb("mv", [P, CT, 2])
        rstd = sb("rstd", [P, CT])
        minus_half = sb("minus_half", [P, CT])
        ident = sb("ident", [P, P])
        negmax = sb("negmax", [P, TBL, HQ])
        nm_split = sb("nm_split", [P, TBL, 2, HQ])
        nm_rows = sb("nm_rows", [2 * HQ, T])
        o_sb = sb("o_sb", [P, QUADS, T])
        sums = sb("sums", [P, TC])
        rsum = sb("rsum", [P, TC])
        r_out = sb("r_out", [P, TC])
        out_tiles = sb("out_tiles", [P, 3, QUADS, T])
        r_b, x_res, y = (out_tiles[:, i, :, :] for i in range(3))
        aux = out_tiles[0:B].rearrange("b i q t -> b (i q t)").rearrange("b (r s t) -> b r s t", r=AUXROWS, s=2)
        assert 3 * QUADS == 2 * AUXROWS

        ps_e = [psum(f"ps_e{i}", [P, 2, BANK]) for i in range(2)]
        ps_m = [psum(f"ps_m{i}", [P, BANK]) for i in range(3)]
        ps_o = psum("ps_o", [P, BANK])

        consts = sem("consts")
        more_cleared = sem("more_cleared")
        w_loaded = sem("w_loaded")
        w_high = sem("w_high")
        w_low = sem("w_low")
        mrow_loaded = sem("mrow_loaded")
        aux_step = sem("aux_step")
        aux_stored = sem("aux_stored")
        xc_loaded = sem("xc_loaded")
        mask_b_loaded = sem("mask_b_loaded")
        mask_col_loaded = sem("mask_col_loaded")
        mask_r_loaded = sem("mask_r_loaded")
        stats_done = sem("stats_done")
        aggr_done = sem("aggr_done")
        veps_done = sem("veps_done")
        rstd_done = sem("rstd_done")
        xn_done = sem("xn_done")
        xs_high = sem("xs_high")
        xs_low = sem("xs_low")
        cs_high = sem("cs_high")
        cs_low = sem("cs_low")
        proj_filled = sem("proj_filled")
        raw_done = sem("raw_done")
        tile_high = sem("tile_high")
        tile_low = sem("tile_low")
        v_done = sem("v_done")
        vbias_done = sem("vbias_done")
        stacked = [sem(f"stacked{q}") for q in range(QUADS)]
        m_filled = sem("m_filled")
        m_reduced = sem("m_reduced")
        nm_high = sem("nm_high")
        nm_low = sem("nm_low")
        nm_rows_done = sem("nm_rows_done")
        nm_stacked = sem("nm_stacked")
        e_filled = sem("e_filled")
        e_done = sem("e_done")
        o_filled = sem("o_filled")
        o_out = sem("o_out")
        sums_loaded = sem("sums_loaded")
        r_step = sem("r_step")
        r_done = sem("r_done")
        r_stored = sem("r_stored")
        r_loaded = [sem(f"r_loaded{q}") for q in range(QUADS)]
        o_scaled = sem("o_scaled")
        y_done = sem("y_done")
        xres_clear = sem("xres_clear")
        xres_loaded = sem("xres_loaded")
        y_stored = sem("y_stored")

        ORDER = ["m1", "k0", "q0", "m2", "v0", "v1", "m3", "q1", "k1", "m0"]
        LAST_ORDER = ["m1", "m2", "m3"]
        PRO_ORDER = ["k0", "q0", "v0", "v1", "q1", "k1", "m0"]
        assert len(ORDER) == FILLS and len(PRO_ORDER) == PRO

        def fill_no(where, name):
            if where is None:
                return PRO_ORDER.index(name)
            b, last = where
            return FILLS * b + PRO + (LAST_ORDER if last else ORDER).index(name)

        AFTER = {(0, 3): "k0", (1, 0): "q0", (1, 1): "v0", (1, 2): "v1", (2, 1): "q1", (2, 2): "k1"}

        def turns(last):
            order = []
            for q in range(QUADS):
                for k in range(TBL):
                    blocks = [] if last and q >= 2 else [("M", q, 4 * k + n) for n in range(4)]
                    order += blocks[:2]
                    if (q, k) in AFTER and not last:
                        order.append(("P", AFTER[q, k]))
                    order += blocks[2:]
                    if k == 0 and not (last and q == 3):
                        order.append(("T", (q + 1) % QUADS))
            return order

        BODY_TURNS = turns(False)
        PRO_TURNS = ([("P", name) for name in PRO_ORDER[:-1]] + [("M", 2, k) for k in range(16)] + [("T", 0)]
                     + [("M", 3, k) for k in range(16)])
        TURNS = {"prologue": PRO_TURNS, "body": BODY_TURNS, "last": turns(True)}
        BANKS = len(ps_m)
        SHIFT = {"prologue": (len(BODY_TURNS) - len(PRO_TURNS)) % BANKS, "body": 0, "last": 0}

        def kind(where):
            return "prologue" if where is None else ("last" if where[1] else "body")

        def bank_of(where, fill):
            return ps_m[(TURNS[kind(where)].index(fill) + SHIFT[kind(where)]) % BANKS]

        def user_before(where, fill):
            i = TURNS[kind(where)].index(fill) - BANKS
            if i >= 0:
                return 0, TURNS[kind(where)][i]
            if where is None:
                return None
            back = (len(BODY_TURNS) - 1) % BANKS
            mine = (i + BANKS) % BANKS
            return -1, BODY_TURNS[len(BODY_TURNS) - 1 - (back - mine) % BANKS]

        TILES = ["k0", "q0", "q1", "k1"]

        def tile_no(b, name):
            return 4 * b + TILES.index(name)

        def loop(eng, body):
            body(0, True, False)
            with eng.Fori(1, B - 2) as b:
                body(b, False, False)
            body(B - 2, False, False)
            body(B - 1, False, True)

        def static(b):
            return isinstance(b, int)

        with nc.Block() as block:
            @block.sync
            def _(sp):
                for n, t in enumerate((w_qT, w_kT, w_vT)):
                    sp.dma_start(w_stage[:, n, :, :], t.rearrange("(k p) o -> p k o", p=P)).then_inc(w_loaded, 16)
                sp.dma_start(bias["q"][:], b_q).then_inc(w_loaded, 16)
                sp.dma_start(bias["k"][:], b_k).then_inc(w_loaded, 16)
                sp.dma_start(bias_v[:], b_v.to_broadcast([P, C])).then_inc(w_loaded, 16)
                sp.dma_start(mask_rows, mask).then_inc(mrow_loaded, 16)

                def load_xc(b):
                    sp.dma_start(x_in[:], x1_seq[b].rearrange("(k p) t -> p k t", p=P)).then_inc(xc_loaded, 16)
                    sp.dma_start(c_in[:], context_seq[b].rearrange("(k p) t -> p k t", p=P)).then_inc(xc_loaded, 16)

                def load_mask_b(b):
                    sp.dma_start(mask_b[:], mask[b].rearrange("(o t) -> o t", o=1).to_broadcast([P, T])).then_inc(mask_b_loaded, 16)

                def load_mask_col(b):
                    sp.dma_start(mask_col[:], mask_cols[b]).then_inc(mask_col_loaded, 16)

                def load_mask_r(b):
                    sp.dma_start(mask_r[:], mask[b].rearrange("(o c t) -> o c t", o=1, c=32)
                                 .to_broadcast([HQ, 32, TC])).then_inc(mask_r_loaded, 16)

                def stack_quad(b, q):
                    half, p0 = q // 2, (q % 2) * HQ * DH
                    for side, name, part, row in ((0, "q", 0, 0), (0, "q", 0, DH), (0, "q", 1, 2 * DH),
                                                  (1, "k", 0, 0), (1, "k", 1, DH), (1, "k", 0, 2 * DH)):
                        sp.dma_start(stack[row:row + DH, q, side, :, :].bitcast(F32),
                                     tile[name][half][part][p0:p0 + HQ * DH, :].bitcast(F32)).then_inc(stacked[q], 16)
                    for side in range(2):
                        sp.dma_start(stack[AUX:AUX + AUXROWS, q, side, :, :].bitcast(F32),
                                     aux_dram[b][:, side:side + 1, :].to_broadcast([AUXROWS, HQ, T])).then_inc(stacked[q], 16)

                def stack_negmax(b, q):
                    wait_alone(sp, nm_rows_done, QUADS * b + q + 1, (consts, 7))
                    sp.dma_start(stack[MAXROW:MAXROW + 2, q, 0, :, :].bitcast(F32), nm_rows[:]).then_inc(nm_stacked, 16)

                def sums_out(g, q):
                    wait_alone(sp, o_out, g + 1, (consts, 7))
                    sp.dma_start(sums[:], o_sb[DH::32, q, :]).then_inc(sums_loaded, 16)

                def reciprocals(g, q):
                    wait_alone(sp, r_done, g + 1, (consts, 7))
                    sp.dma_start(rinv_dram[q].rearrange("(p c) -> p c", p=P), r_out[:]).then_inc(r_stored, 16)
                    wait_alone(sp, r_stored, 16 * (g + 1), (consts, 7))
                    sp.dma_start(r_b[:, q, :], rinv_dram[q].rearrange("(j o t) -> j o t", j=HQ, o=1)
                                 .to_broadcast([HQ, 32, T])).then_inc(r_loaded[q], 16)

                def rows(seq, b, j):
                    return seq[b].rearrange("(q j d) t -> j d q t", q=QUADS, j=HQ)[j]

                def load_res(b):
                    for j in range(HQ):
                        sp.dma_start(x_res[32 * j:32 * j + DH, :, :], rows(x1_seq, b, j)).then_inc(xres_loaded, 16)

                def store_y(b):
                    for j in range(HQ):
                        sp.dma_start(rows(x2_seq, b, j), y[32 * j:32 * j + DH, :, :]).then_inc(y_stored, 16)

                load_xc(0)
                load_mask_b(0)
                load_mask_col(0)
                load_mask_r(0)
                sp.wait_ge(aux_step, AUX_STEPS)
                sp.dma_start(aux_dram.rearrange("b r s t -> b (r s t)"),
                             aux.rearrange("b r s t -> b (r s t)")).then_inc(aux_stored, 16)
                sp.wait_ge(aux_stored, 16)
                sp.wait_ge(consts, 5)
                sp.wait_ge(tile_low, tile_no(0, "q0") + 1)
                stack_quad(0, 0)
                stack_quad(0, 1)
                sp.wait_ge(xs_low, 1)
                sp.wait_ge(cs_low, 1)
                load_xc(1)
                sp.wait_ge(tile_low, tile_no(0, "k1") + 1)
                load_mask_b(1)
                stack_negmax(0, 0)
                sp.wait_ge(more_cleared, 2)
                stack_quad(0, 2)
                sp.wait_ge(xres_clear, 1)
                load_res(0)

                def body(b, first, last):
                    g = QUADS * b
                    if not first:
                        wait_alone(sp, e_filled, 8 * g, (consts, 7))
                    stack_quad(b, 3)
                    stack_negmax(b, 1)
                    if not first:
                        sums_out(g - 1, 3)
                        reciprocals(g - 1, 3)
                        load_mask_r(b)
                    stack_negmax(b, 2)
                    if not last:
                        wait_alone(sp, v_done, QUADS * (b + 1), (consts, 7))
                        load_mask_col(b + 1)
                    sums_out(g, 0)
                    if not last:
                        wait_alone(sp, tile_low, tile_no(b + 1, "q0") + 1, (consts, 7))
                        wait_alone(sp, e_filled, 8 * (g + 1), (consts, 7))
                        stack_quad(b + 1, 0)
                    reciprocals(g, 0)
                    if not first:
                        wait_alone(sp, y_done, g, (consts, 7))
                        store_y(b - 1)
                        load_res(b)
                    if not last:
                        wait_alone(sp, xs_low, b + 2, (consts, 7))
                        wait_alone(sp, cs_low, b + 2, (consts, 7))
                        if not (static(b) and b + 2 >= B):
                            load_xc(b + 2)
                    if not last:
                        wait_alone(sp, e_filled, 8 * (g + 2), (consts, 7))
                        stack_quad(b + 1, 1)
                    sums_out(g + 1, 1)
                    stack_negmax(b, 3)
                    reciprocals(g + 1, 1)
                    if not last:
                        wait_alone(sp, tile_low, tile_no(b + 1, "k1") + 1, (consts, 7))
                        if not (static(b) and b + 2 >= B):
                            load_mask_b(b + 2)
                        wait_alone(sp, e_filled, 8 * (g + 3), (consts, 7))
                        stack_quad(b + 1, 2)
                    sums_out(g + 2, 2)
                    if not last:
                        stack_negmax(b + 1, 0)
                    reciprocals(g + 2, 2)

                loop(sp, body)
                sums_out(QUADS * B - 1, 3)
                reciprocals(QUADS * B - 1, 3)
                sp.wait_ge(y_done, QUADS * B)
                store_y(B - 1)
                sp.wait_ge(y_stored, 16 * HQ * B)

            @block.gpsimd
            def _(pool):
                nc.gpsimd.memset(ident[:], 0.0).then_inc(consts, 1)
                nc.gpsimd.memset(minus_half[:], -0.5).then_inc(consts, 1)
                nc.gpsimd.memset(stack[:, 0:2].rearrange("p a b c t -> p (a b c t)").bitcast(F32), 0.0).then_inc(consts, 1)
                pool.wait_ge(consts, 3)
                nc.gpsimd.affine_select(out=ident[:], in_=ident[:], compare_op=ALU.not_equal, fill=1.0, base=0,
                                        pattern=[[-1, P]], channel_multiplier=1).then_inc(consts, 1)
                pool.wait_ge(consts, 4)
                nc.gpsimd.memset(stack[MAXROW:MAXROW + 2, 0:2, 1, :, :].bitcast(F32), 1.0).then_inc(consts, 1)
                def norm_scale(b):
                    wait_alone(pool, aggr_done, CT * (b + 1), (consts, 5))
                    nc.gpsimd.tensor_scalar(rstd[:], mv[:, :, 1], LN_EPS, None, ALU.add).then_inc(veps_done, 1)
                    pool.wait_ge(veps_done, b + 1)
                    nc.gpsimd.tensor_tensor(rstd[:], rstd[:], minus_half[:], ALU.pow).then_inc(rstd_done, 1)

                def low(dst, full, high, high_sem, n, out_sem):
                    pool.wait_ge(high_sem, n)
                    nc.gpsimd.tensor_tensor(dst, full, high.bitcast(F32), ALU.subtract).then_inc(out_sem, 1)

                def context_low(b):
                    low(cs[1][:], c_in[:], cs[0][:], cs_high, b + 1, cs_low)

                def x_low(b):
                    low(xs[1][:], xn[:], xs[0][:], xs_high, b + 1, xs_low)

                def tile_low_part(b, name):
                    n, half = name[0], int(name[1])
                    if not (static(b) and b == 0):
                        pool.wait_ge(stacked[2 * half + 1], 16 * 8 * b)
                    low(tile[n][half][1][:], raw[n][:], tile[n][half][0][:], tile_high, tile_no(b, name) + 1, tile_low)

                def values(b, q):
                    if q == 0:
                        wait_alone(pool, vbias_done, 2 * (b + 1), (consts, 7))
                        wait_alone(pool, mask_col_loaded, 16 * (b + 1), (consts, 7))
                    if not (static(b) and b == 0):
                        wait_alone(pool, o_filled, QUADS * (b - 1) + q + 1, (consts, 7))
                    for k in range(TBL):
                        ins = nc.gpsimd.tensor_scalar(
                            v_stack[:, k, HQ * q:HQ * q + HQ, 0:DH],
                            v_raw[:, k, HQ * DH * q:HQ * DH * (q + 1)].rearrange("p (h d) -> p h d", h=HQ),
                            mask_col[:, k:k + 1], None, ALU.mult)
                    ins.then_inc(v_done, 1)

                def residual(b, g, q):
                    pool.wait_ge(r_loaded[q], 16 * (b + 1))
                    nc.gpsimd.tensor_tensor(r_b[:, q, :], o_sb[:, q, :], r_b[:, q, :], ALU.mult).then_inc(o_scaled, 1)
                    if q == 0:
                        pool.wait_ge(xres_loaded, 16 * HQ * (b + 1))
                        if not (static(b) and b == 0):
                            pool.wait_ge(y_stored, 16 * HQ * b)
                    pool.wait_ge(o_scaled, g + 2)
                    nc.gpsimd.tensor_tensor(y[:, q, :], r_b[:, q, :], x_res[:, q, :], ALU.add).then_inc(y_done, 1)

                pool.wait_ge(consts, 5)
                pool.sem_inc(o_scaled, 1)
                norm_scale(0)
                context_low(0)
                x_low(0)
                nc.gpsimd.memset(v_stack[:], 0.0).then_inc(consts, 1)
                pool.wait_ge(consts, 6)
                nc.gpsimd.memset(v_stack[:, :, :, DH:DH + 1], 1.0).then_inc(consts, 1)
                for name in TILES:
                    tile_low_part(0, name)
                nc.gpsimd.memset(stack[:, 2:4].rearrange("p a b c t -> p (a b c t)").bitcast(F32), 0.0).then_inc(more_cleared, 1)
                pool.wait_ge(more_cleared, 1)
                nc.gpsimd.memset(stack[MAXROW:MAXROW + 2, 2:4, 1, :, :].bitcast(F32), 1.0).then_inc(more_cleared, 1)
                pool.wait_ge(more_cleared, 2)
                pool.wait_ge(aux_stored, 16)
                nc.gpsimd.memset(x_res, 0.0).then_inc(xres_clear, 1)
                for q in range(3):
                    values(0, q)

                def body(b, first, last):
                    g = QUADS * b
                    if not last:
                        norm_scale(b + 1)
                        context_low(b + 1)
                    values(b, 3)
                    if not last:
                        x_low(b + 1)
                        tile_low_part(b + 1, "k0")
                    if not first:
                        residual(b - 1, g - 1, 3)
                    if not last:
                        tile_low_part(b + 1, "q0")
                    if not last:
                        values(b + 1, 0)
                    residual(b, g, 0)
                    if not last:
                        values(b + 1, 1)
                        tile_low_part(b + 1, "q1")
                        tile_low_part(b + 1, "k1")
                    residual(b, g + 1, 1)
                    if not last:
                        values(b + 1, 2)
                    residual(b, g + 2, 2)

                loop(pool, body)
                residual(B - 1, QUADS * B - 1, 3)

            @block.scalar
            def _(act):
                for n, name in enumerate("qkv"):
                    if n == 0:
                        act.wait_ge(w_loaded, 16 * 6)
                    nc.scalar.activation(w[name][0][:], w_stage[:, n, :, :], ACT.Copy).then_inc(w_high, 1)

                def context_high(b):
                    act.wait_ge(xc_loaded, 32 * (b + 1))
                    if not (static(b) and b == 0):
                        act.wait_ge(tile_high, 4 * b)
                    nc.scalar.activation(cs[0][:], c_in[:], ACT.Copy).then_inc(cs_high, 1)

                def x_high(b):
                    act.wait_ge(xn_done, b + 1)
                    nc.scalar.activation(xs[0][:], xn[:], ACT.Copy).then_inc(xs_high, 1)

                def tile_high_part(b, name):
                    n, half = name[0], int(name[1])
                    act.wait_ge(raw_done, tile_no(b, name) + 1)
                    if not (static(b) and b == 0):
                        act.wait_ge(stacked[2 * half + 1], 16 * 8 * b)
                    nc.scalar.activation(tile[n][half][0][:], raw[n][:], ACT.Copy).then_inc(tile_high, 1)

                def negmax_rows(where, b, q):
                    g = QUADS * b + q
                    act.wait_ge(proj_filled, fill_no(where, f"m{q}") + 1)
                    act.wait_ge(nm_stacked, 16 * g)
                    nc.scalar.activation(nm_rows[:], bank_of(where, ("T", q))[0:2 * HQ, :], ACT.Copy).then_inc(nm_rows_done, 1)

                def exps(g, k):
                    for p in range(2):
                        act.wait_ge(e_filled, 8 * g + 2 * k + p + 1)
                        nc.scalar.activation(probs[:, k % 2, 2 * p:2 * p + 2, :], ps_e[p][:], ACT.Exp,
                                             scale=0.25).then_inc(e_done, 1)

                def output(g, q):
                    act.wait_ge(o_filled, g + 1)
                    if not (static(g) and g < QUADS):
                        act.wait_ge(o_scaled, g - QUADS + 2)
                    nc.scalar.activation(o_sb[:, q, :], ps_o[:], ACT.Copy).then_inc(o_out, 1)

                context_high(0)
                x_high(0)
                for name in TILES:
                    tile_high_part(0, name)
                negmax_rows(None, 0, 0)

                def body(b, first, last):
                    g = QUADS * b
                    where = (b, last)
                    exps(g, 0)
                    if not first:
                        output(g - 1, 3)
                    negmax_rows(where, b, 1)
                    exps(g, 1)
                    if not last:
                        context_high(b + 1)
                    exps(g, 2)
                    if not last:
                        x_high(b + 1)
                    exps(g, 3)
                    if not last:
                        tile_high_part(b + 1, "k0")
                    exps(g + 1, 0)
                    output(g, 0)
                    if not last:
                        tile_high_part(b + 1, "q0")
                    negmax_rows(where, b, 2)
                    for k in (1, 2, 3):
                        exps(g + 1, k)
                    exps(g + 2, 0)
                    output(g + 1, 1)
                    negmax_rows(where, b, 3)
                    exps(g + 2, 1)
                    if not last:
                        tile_high_part(b + 1, "q1")
                    exps(g + 2, 2)
                    if not last:
                        tile_high_part(b + 1, "k1")
                    exps(g + 2, 3)
                    exps(g + 3, 0)
                    output(g + 2, 2)
                    if not last:
                        negmax_rows(where, b + 1, 0)
                    for k in (1, 2, 3):
                        exps(g + 3, k)

                loop(act, body)
                output(QUADS * B - 1, 3)

            @block.vector
            def _(dve):
                dve.wait_ge(w_loaded, 16 * 6)
                for n, name in enumerate("qkv"):
                    dve.wait_ge(w_high, n + 1)
                    nc.vector.tensor_tensor(w[name][1][:], w_stage[:, n, :, :], w[name][0][:].bitcast(F32),
                                            ALU.subtract).then_inc(w_low, 1)

                def normalise(b):
                    dve.wait_ge(xc_loaded, 32 * (b + 1))
                    for k in range(CT):
                        nc.vector.bn_stats(stats[:, k, :], x_in[:, k, :]).then_inc(stats_done, 1)
                    wait_alone(dve, stats_done, CT * (b + 1), (w_high, 3))
                    for k in range(CT):
                        nc.vector.bn_aggr(mv[:, k, :], stats[:, k, :]).then_inc(aggr_done, 1)

                def apply_norm(b):
                    dve.wait_ge(rstd_done, b + 1)
                    for k in range(CT):
                        ins = nc.vector.tensor_scalar(xn[:, k, :], x_in[:, k, :], mv[:, k, 0:1], rstd[:, k:k + 1],
                                                      ALU.subtract, ALU.mult)
                    ins.then_inc(xn_done, 1)

                normalise(0)
                apply_norm(0)

                steps = [0]

                def aux_op(ins):
                    steps[0] += 1
                    ins.then_inc(aux_step, 1)
                    dve.wait_ge(aux_step, steps[0])

                def split_rows(full, side, highs, lows):
                    aux_op(nc.vector.tensor_copy(aux[:, highs[0], side, :].bitcast(F32R), full))
                    aux_op(nc.vector.tensor_tensor(aux[:, lows[0], side, :].bitcast(F32R), full,
                                                   aux[:, highs[0], side, :], ALU.subtract))
                    for r in highs[1:]:
                        nc.vector.tensor_copy(aux[:, r, side, :], aux[:, highs[0], side, :])

                dve.wait_ge(mrow_loaded, 16)
                aux_op(nc.vector.tensor_scalar(one_minus, mask_rows, -1.0, 1.0, ALU.mult, ALU.add))
                split_rows(one_minus, 0, (0, 2), (1,))
                split_rows(mask_rows, 0, (3, 5), (4,))
                aux_op(nc.vector.memset(neg_row, NEG4))
                split_rows(neg_row, 1, (0, 1), (2,))
                aux_op(nc.vector.tensor_scalar(one_minus, one_minus, NEG4, None, ALU.mult))
                aux_op(nc.vector.tensor_copy(aux[:, 3, 1, :].bitcast(F32R), one_minus))
                nc.vector.tensor_copy(aux[:, 4, 1, :], aux[:, 3, 1, :])
                nc.vector.tensor_tensor(aux[:, 5, 1, :].bitcast(F32R), one_minus, aux[:, 3, 1, :],
                                        ALU.subtract).then_inc(aux_step, 1)
                assert steps[0] + 1 == AUX_STEPS

                def raw_tile(where, b, name):
                    n, half = name[0], int(name[1])
                    dve.wait_ge(proj_filled, fill_no(where, name) + 1)
                    if name in ("k0", "q0"):
                        if name == "k0":
                            dve.wait_ge(mask_b_loaded, 16 * (b + 1))
                        if not (static(b) and b == 0):
                            dve.wait_ge(tile_low, 4 * b)
                    else:
                        dve.wait_ge(tile_low, tile_no(b, n + "0") + 1)
                    nc.vector.scalar_tensor_tensor(raw[n][:], bank_of(where, ("P", name))[:], bias[n][:, half:half + 1], mask_b[:], ALU.add,
                                                   ALU.mult).then_inc(raw_done, 1)

                def raw_values(where, b, i):
                    dve.wait_ge(proj_filled, fill_no(where, f"v{i}") + 1)
                    if i == 0 and not (static(b) and b == 0):
                        dve.wait_ge(v_done, QUADS * b)
                    for k in range(2):
                        ins = nc.vector.tensor_tensor(v_raw[:, 2 * i + k, :], bank_of(where, ("P", f"v{i}"))[:, k * C:(k + 1) * C], bias_v[:], ALU.add)
                    ins.then_inc(vbias_done, 1)

                def maxima(where, q, g, k0, k1):
                    for k in range(k0, k1):
                        if k == 0 and not (static(g) and g == 0):
                            dve.wait_ge(nm_low, g)
                        dve.wait_ge(m_filled, 16 * g + k + 1)
                        nc.vector.tensor_reduce(negmax[:, k // HQ, k % HQ:k % HQ + 1], bank_of(where, ("M", q, k))[:], AX.X, ALU.max,
                                                negate=True).then_inc(m_reduced, 1)

                def split_maxima(g):
                    dve.wait_ge(m_reduced, 16 * (g + 1))
                    nc.vector.tensor_copy(nm_split[:, :, 0, :].bitcast(F32R), negmax[:]).then_inc(nm_high, 1)
                    dve.wait_ge(nm_high, g + 1)
                    nc.vector.tensor_tensor(nm_split[:, :, 1, :].bitcast(F32R), negmax[:], nm_split[:, :, 0, :],
                                            ALU.subtract).then_inc(nm_low, 1)

                def reciprocal(g):
                    dve.wait_ge(sums_loaded, 16 * (g + 1))
                    nc.vector.reciprocal(rsum[:], sums[:]).then_inc(r_step, 1)
                    dve.wait_ge(r_step, g + 1)

                def masked_reciprocal(g, b, q):
                    reciprocal(g)
                    if q == 0:
                        dve.wait_ge(mask_r_loaded, 16 * (b + 1))
                    if not (static(g) and g == 0):
                        dve.wait_ge(r_stored, 16 * g)
                    nc.vector.tensor_tensor(r_out[:], rsum[:], mask_r[:], ALU.mult).then_inc(r_done, 1)

                for name in ("k0", "q0"):
                    raw_tile(None, 0, name)
                raw_values(None, 0, 0)
                raw_values(None, 0, 1)
                for name in ("q1", "k1"):
                    raw_tile(None, 0, name)
                for g in range(2):
                    maxima(None, g + 2, g, 0, 16)
                    split_maxima(g)

                def body(b, first, last):
                    g = QUADS * b
                    where = (b, last)
                    nxt = b + 1
                    for q in range(QUADS):
                        for k in range(TBL):
                            name = AFTER.get((q, k))
                            if not (last and q >= 2):
                                maxima(where, q, g + q + 2, 4 * k, 4 * k + 2)
                            if name and not last:
                                if name[0] == "v":
                                    raw_values(where, nxt, int(name[1]))
                                else:
                                    raw_tile(where, nxt, name)
                            if not (last and q >= 2):
                                maxima(where, q, g + q + 2, 4 * k + 2, 4 * k + 4)
                            if (q, k) == (0, 0) and not last:
                                normalise(nxt)
                            if (q, k) == (0, 1) and not last:
                                apply_norm(nxt)
                            if (q, k) == (0, 2) and not first:
                                masked_reciprocal(g - 1, b - 1, 3)
                            if q and k == 2:
                                masked_reciprocal(g + q - 1, b, q - 1)
                        if not (last and q >= 2):
                            split_maxima(g + q + 2)

                loop(dve, body)
                masked_reciprocal(QUADS * B - 1, B - 1, 3)

            @block.tensor
            def _(pe):
                ROWS = {"max": MAXROW, "exp": MAXROW + 2}

                def bank(where, b, fill):
                    before = user_before(where, fill)
                    if before is not None:
                        back, (what, *which) = before
                        at = b + back
                        if what == "M":
                            pe.wait_ge(m_reduced, 16 * (QUADS * at + which[0] + 2) + which[1] + 1)
                        elif what == "T":
                            pe.wait_ge(nm_rows_done, QUADS * (at if which[0] else at + 1) + which[0] + 1)
                        elif which[0][0] == "v":
                            pe.wait_ge(vbias_done, 2 * (at + 1) + int(which[0][1]) + 1)
                        else:
                            pe.wait_ge(raw_done, tile_no(at + 1, which[0]) + 1)
                    return bank_of(where, fill)

                def products(out, pairs):
                    n = len(pairs)
                    for i, (s, m) in enumerate(pairs):
                        for k, (a, c) in enumerate(((0, 0), (0, 1), (1, 0))):
                            ins = nc.tensor.matmul(out, s(a), m(c), start=(i == 0 and k == 0), stop=(i == n - 1 and k == 2))
                    return ins

                def project(where, b, name):
                    n, half = name[0], int(name[1])
                    src = xs if n == "q" else cs
                    pe.wait_ge(xs_low if n == "q" else cs_low, b + 1)
                    ps_p = bank(where, b - 1, ("P", name))
                    products(ps_p[:], [(lambda a, k=k: w[n][a][:, k, half * P:(half + 1) * P],
                                        lambda c, k=k: src[c][:, k, :]) for k in range(CT)]).then_inc(proj_filled, 1)

                def project_values(where, b, i):
                    ps_p = bank(where, b - 1, ("P", f"v{i}"))
                    for j in range(2):
                        blk = 2 * i + j
                        ins = products(ps_p[:, j * C:(j + 1) * C],
                                       [(lambda a, k=k: cs[a][:, k, blk * P:(blk + 1) * P],
                                         lambda c, k=k: w["v"][c][:, k, :]) for k in range(CT)])
                    ins.then_inc(proj_filled, 1)

                def negmax_transpose(where, b, q):
                    g = QUADS * b + q
                    pe.wait_ge(nm_low, g + 1)
                    ps_p = bank(where, b if q else b - 1, ("T", q))
                    for k in range(TBL):
                        ins = nc.tensor.transpose(ps_p[0:2 * HQ, k * P:(k + 1) * P],
                                                  nm_split[:, k, :, :].rearrange("p s h -> p (s h)"), ident[:])
                    ins.then_inc(proj_filled, 1)

                def max_scores(where, b, step, k0, k1):
                    g = QUADS * b + step + 2
                    q = (step + 2) % QUADS
                    for k in range(k0, k1):
                        blk, h = k // HQ, k % HQ
                        if k == 0:
                            pe.wait_ge(stacked[q], 16 * 8 * (b + (step + 2) // QUADS + 1))
                        nc.tensor.matmul(bank(where, b, ("M", step, k))[:], stack[0:MAXROW, q, 0, h, blk * P:(blk + 1) * P],
                                         stack[0:MAXROW, q, 1, h, :], start=True, stop=True).then_inc(m_filled, 1)

                def exp_scores(g, q, k, p):
                    if k == 0 and p == 0:
                        pe.wait_ge(nm_stacked, 16 * (g + 1))
                    if not (static(g) and 8 * g + 2 * k + p < 2):
                        pe.wait_ge(e_done, 8 * g + 2 * k + p - 1)
                    for i in range(2):
                        h = 2 * p + i
                        ins = nc.tensor.matmul(ps_e[p][:, i, :], stack[0:MAXROW + 2, q, 1, h, k * P:(k + 1) * P],
                                               stack[0:MAXROW + 2, q, 0, h, :], start=True, stop=True)
                    ins.then_inc(e_filled, 1)

                def values_product(g, q, k, between=None):
                    pe.wait_ge(e_done, 8 * g + 2 * k + 2)
                    if k == 0:
                        pe.wait_ge(v_done, g + 1)
                        pe.wait_ge(o_out, g)
                    for h in range(HQ):
                        if h == HQ // 2 and between:
                            between()
                        ins = nc.tensor.matmul(ps_o[32 * h:32 * h + 32, :], v_stack[:, k, HQ * q + h, :],
                                               probs[:, k % 2, h, :], start=(k == 0), stop=(k == TBL - 1))
                    if k == TBL - 1:
                        ins.then_inc(o_filled, 1)

                pe.wait_ge(consts, 4)
                pe.wait_ge(w_low, 3)
                project(None, 0, "k0")
                project(None, 0, "q0")
                project_values(None, 0, 0)
                project_values(None, 0, 1)
                project(None, 0, "q1")
                project(None, 0, "k1")
                max_scores(None, -1, 2, 0, 16)
                negmax_transpose(None, 0, 0)
                max_scores(None, -1, 3, 0, 16)

                def body(b, first, last):
                    g = QUADS * b
                    where = (b, last)
                    for q in range(QUADS):
                        for k in range(TBL):

                            def max_block(n):
                                if not (last and q >= 2):
                                    max_scores(where, b, q, 4 * k + n, 4 * k + n + 1)

                            exp_scores(g + q, q, k, 0)
                            max_block(0)
                            exp_scores(g + q, q, k, 1)
                            max_block(1)
                            name = AFTER.get((q, k))
                            if name and not last:
                                if name[0] == "v":
                                    project_values(where, b + 1, int(name[1]))
                                else:
                                    project(where, b + 1, name)
                            third = lambda: max_block(2)
                            if k > 0:
                                values_product(g + q, q, k - 1, third)
                            elif q > 0:
                                values_product(g + q - 1, q - 1, TBL - 1, third)
                            elif not first:
                                values_product(g - 1, QUADS - 1, TBL - 1, third)
                            else:
                                third()
                            max_block(3)
                            if k == 0 and q < 3:
                                negmax_transpose(where, b, q + 1)
                            if k == 0 and q == 3 and not last:
                                negmax_transpose(where, b + 1, 0)

                loop(pe, body)
                values_product(QUADS * B - 1, QUADS - 1, TBL - 1)


def in_steps(eng, steps, step, first=2, last=2):
    for n in range(first):
        step(n, n // 2, n % 2)
    end = steps - last
    with eng.Fori(first // 2, end // 2) as t:
        for i in range(2):
            step(2 * t + i, t, i)
    for n in range(end, steps):
        step(n, n // 2, n % 2)


def in_groups(eng, groups, group):
    group(0, 0, 0)
    with eng.Fori(0, (groups - 2) // 3) as t:
        for i in range(1, 4):
            group(3 * t + i, t + i // 3, i % 3)
    group(groups - 1, (groups - 1) // 3, (groups - 1) % 3)


def experts_scratch(nc):
    E, T, H = 8, 4096, 512
    return [nc.dram_tensor("rows_by_expert", [E * (T + P) + P, H + 4], F32, kind="Internal").ap()]


def experts_phase(nc, out, w_gT, w_13T, w_2T, bias, rows):
    GT, H = BANK, out.shape[1]
    GROUPS = (out.shape[0] - P) // GT
    x2_rows = out[0:GROUPS * GT].rearrange("(g n) h -> g n h", n=GT)
    T = GROUPS * GT
    E = w_gT.shape[1]
    FF = w_2T.shape[1]
    TB = GT // P
    KT = H // P
    FT = FF // P
    assert GT == BANK and 2 * FF == BANK and H == BANK and E == GROUPS
    REGION = T + P
    PAD_ROW = E * REGION
    W0, W1, BEST, TOKEN, ROW = H, H + 1, H + 2, H + 3, H + 4
    TILES = 2 * T // P + E - 1
    PASSES = ((0, 0), (0, 1), (1, 0))

    with ExitStack() as ctx:
        def sb(name, shape, dt=F32):
            return ctx.enter_context(nc.sbuf_tensor("c_" + name, shape, dt))

        def early(tensors, place_of):
            with ExitStack() as at_first:
                early_ones = [at_first.enter_context(nc.sbuf_tensor("c_" + name, shape, dt)) for name, shape, dt in tensors]
            return *early_ones, sb(*place_of)

        w13_high = sb("w13_h", [P, E, KT, 2 * FF], F32R)
        w13_raw, w13_low = early([("w13_raw", [P, E, KT, 2 * FF], F32)], ("w13_l", [P, E, KT, 2 * FF], F32R))
        xT_high, xT_low, w2 = early([(f"xT_{s}", [P, KT, GT], F32R) for s in "hl"], ("w2", [P, E, FT, H]))
        w13 = [w13_high, w13_low]
        ident = sb("ident", [P, P])
        tile_expert = sb("tile_expert", [P, TILES])
        tile_expert_int = sb("tile_expert_int", [P, TILES], I32)
        tile_row_int = sb("tile_row_int", [P, TILES], I32)

        route_tokens(nc, x2_rows, out, w_gT, w_13T, w_2T, bias, rows, w13, w13_raw, [xT_high, xT_low], w2, ident, tile_expert, tile_expert_int,
                     tile_row_int, GROUPS, GT, TB, KT, FT, T, H, E, REGION, PAD_ROW, W0, W1, BEST, TOKEN, ROW, TILES, PASSES)
        run_experts(nc, rows, out, w13, w2, ident, tile_expert, tile_expert_int, tile_row_int,
                    KT, FT, FF, H, E, W0, W1, BEST, TOKEN, ROW, TILES, PASSES)


def route_tokens(nc, x2_rows, out, w_gT, w_13T, w_2T, bias, rows, w13, w13_raw, xT, w2, ident, tile_expert, tile_expert_int,
                 tile_row_int, GROUPS, GT, TB, KT, FT, T, H, E, REGION, PAD_ROW, W0, W1, BEST, TOKEN, ROW, TILES, PASSES):
    with ExitStack() as ctx:
        def sb(name, shape, dt=F32):
            return ctx.enter_context(nc.sbuf_tensor("r_" + name, shape, dt))

        def psum(name, shape):
            return ctx.enter_context(nc.psum_tensor("r_" + name, shape, F32))

        def sem(name):
            return ctx.enter_context(nc.semaphore("r_" + name))

        xn = [sb(f"xn{i}", [P, TB, ROW]) for i in range(3)]
        wg_raw = sb("wg_raw", [P, KT, E])
        wg = [sb(f"wg_{s}", [P, KT, E], F32R) for s in "hl"]
        bias_b = sb("bias_b", [P, E])
        minus_half = sb("minus_half", [P, TB])
        logits_T = sb("logits_T", [E, GT])
        stats = sb("stats", [P, TB, 6])
        mv = sb("mv", [P, TB, 2])
        rstd = sb("rstd", [P, TB])
        STEPS = T // P
        NUMS = E + TB + STEPS + TILES
        nums_int = sb("nums_int", [P, NUMS], I32)
        nums = sb("nums", [P, NUMS])
        expert_no = nums[:, 0:E]
        token_in_group = nums[:, E:E + TB]
        times_128 = nums[:, E + TB:E + TB + STEPS]
        tile_no = nums[:, E + TB + STEPS:]
        region_row = sb("region_row", [P, E])
        next_row = sb("next_row", [P, E])
        token = sb("token", [P, TB])
        lower = sb("lower", [P, E, E])
        before_bf = sb("before_bf", [P, P], BF16)
        ones_bf = sb("ones_bf", [P, P], BF16)
        chosen_bf = sb("chosen_bf", [P, TB + 1, E], BF16)
        ez = sb("ez", [P, TB, E])
        sig = sb("sig", [P, TB, E])
        score = sb("score", [P, TB, E])
        above = sb("above", [P, TB, E, E])
        equal = sb("equal", [P, TB, E, E])
        rank = sb("rank", [P, TB, E])
        total = sb("total", [P, TB])
        inv = sb("inv", [P, TB])
        weight = sb("weight", [P, TB, E])
        is_rank = sb("is_rank", [P, TB, 2, E])
        picked = sb("picked", [P, TB, 2, E])
        place = sb("place", [P, TB, E])
        place_rank = sb("place_rank", [P, TB, 2])
        place_int = [sb(f"place_int{i}", [P, TB, 2], I32) for i in range(3)]
        pad_rows = sb("pad_rows", [P, ROW])
        pad_place = sb("pad_place", [P, E], I32)
        n_rows = sb("n_rows", [P, E])
        n_tiles = sb("n_tiles", [P, E])
        first_tile = sb("first_tile", [P, E + 1])
        more_rows = sb("more_rows", [P, E, STEPS])
        started = sb("started", [P, TILES, E - 1])
        tile_row = sb("tile_row", [P, TILES])
        tile_first = sb("tile_first", [P, TILES])
        tile_used = sb("tile_used", [P, TILES])
        ps_x = [psum(f"ps_x{i}", [P, BANK]) for i in range(4)]
        ps_rT = psum("ps_rT", [E, GT])
        ps_r = psum("ps_r", [P, TB, E])
        ps_c = psum("ps_c", [P, TB + 1, E])
        consts = sem("consts")
        numbers = sem("numbers")
        small_loaded = sem("small_loaded")
        wg_high = sem("wg_high")
        wg_low = sem("wg_low")
        x2_loaded = [sem(f"x2_loaded{i}") for i in range(3)]
        w13_loaded = sem("w13_loaded")
        w2_loaded = sem("w2_loaded")
        w13_high = sem("w13_high")
        w13_low = sem("w13_low")
        stats_done = sem("stats_done")
        aggr_done = sem("aggr_done")
        veps_done = sem("veps_done")
        logits_out = sem("logits_out")
        logits_copied = sem("logits_copied")
        rstd_done = sem("rstd_done")
        xn_done = sem("xn_done")
        xT_filled = sem("xT_filled")
        xT_high = sem("xT_high")
        xT_low = sem("xT_low")
        logits_done = sem("logits_done")
        ez_done = sem("ez_done")
        route = sem("route")
        chosen_done = sem("chosen_done")
        counted = sem("counted")
        placed = sem("placed")
        scattered = [sem(f"scattered{i}") for i in range(3)]
        pads_placed = sem("pads_placed")
        padded = sem("padded")
        pad_tile_out = sem("pad_tile_out")
        spare_cleared = sem("spare_cleared")
        table = sem("table")

        def expert(G):
            return slice(G, G + 1) if isinstance(G, int) else bass.ds(G, 1)

        with nc.Block() as block:
            @block.sync
            def _(sp):

                for G in range(GROUPS):
                    if G >= 3:
                        sp.wait_ge(scattered[G % 3], 16 * 2 * TB * (G // 3))
                    sp.dma_start(xn[G % 3][:, :, 0:H], x2_rows[G].rearrange("(n p) h -> p n h", p=P)).then_inc(x2_loaded[G % 3], 16)
                    if G == 0:
                        sp.dma_start(wg_raw[:], w_gT.rearrange("(k p) e -> p k e", p=P)).then_inc(small_loaded, 16)
                        sp.dma_start(bias_b[:], bias.to_broadcast([P, E])).then_inc(small_loaded, 16)
                sp.dma_start(rows[PAD_ROW:PAD_ROW + P], pad_rows[:]).then_inc(pad_tile_out, 16)
                sp.dma_start(out[T:T + P], pad_rows[:, 0:H]).then_inc(spare_cleared, 16)
                sp.wait_ge(logits_done, GROUPS)
                sp.dma_start(w2[:], w_2T.rearrange("e (k p) h -> p e k h", p=P)).then_inc(w2_loaded, 16)
                sp.wait_ge(pad_tile_out, 16)
                sp.wait_ge(spare_cleared, 16)
                sp.wait_ge(padded, 16 * E)
                for i in range(3):
                    sp.wait_ge(scattered[i], 16 * 2 * TB * len(range(i, GROUPS, 3)))
                sp.wait_ge(w2_loaded, 16)

            @block.gpsimd
            def _(pool):
                nc.gpsimd.memset(ident[:], 0.0).then_inc(consts, 1)
                nc.gpsimd.memset(minus_half[:], -0.5).then_inc(consts, 1)
                nc.gpsimd.memset(ones_bf[:], 1.0).then_inc(consts, 1)
                nc.gpsimd.memset(before_bf[:], 1.0).then_inc(consts, 1)
                nc.gpsimd.memset(lower[:], 1.0).then_inc(consts, 1)
                nc.gpsimd.memset(pad_rows[:, 0:BEST], 0.0).then_inc(consts, 1)
                nc.gpsimd.memset(pad_rows[:, BEST:TOKEN], -1.0).then_inc(consts, 1)
                nc.gpsimd.memset(chosen_bf[:], 0.0).then_inc(consts, 1)
                pool.wait_ge(consts, 8)
                nc.gpsimd.affine_select(out=ident[:], in_=ident[:], compare_op=ALU.not_equal, fill=1.0, base=0,
                                        pattern=[[-1, P]], channel_multiplier=1).then_inc(consts, 1)
                nc.gpsimd.affine_select(out=before_bf[:], in_=before_bf[:], compare_op=ALU.is_gt, fill=0.0, base=0,
                                        pattern=[[1, P]], channel_multiplier=-1).then_inc(consts, 1)
                nc.gpsimd.affine_select(out=lower[:], in_=lower[:], compare_op=ALU.is_gt, fill=0.0, base=0,
                                        pattern=[[1, E], [-1, E]], channel_multiplier=0).then_inc(consts, 1)
                at = 0
                for step, count, per_partition in ((1, E, 0), (P, TB, 1), (P, STEPS, 0), (1, TILES, 0)):
                    nc.gpsimd.iota(nums_int[:, at:at + count], pattern=[[step, count]], base=0,
                                   channel_multiplier=per_partition).then_inc(numbers, 1)
                    at += count

                def rstd_of(G):
                    wait_alone(pool, aggr_done, TB * (G + 1), (consts, 11))
                    nc.gpsimd.tensor_scalar(rstd[:], mv[:, :, 1], LN_EPS, None, ALU.add).then_inc(veps_done, 1)
                    pool.wait_ge(veps_done, G + 1)
                    nc.gpsimd.tensor_tensor(rstd[:], rstd[:], minus_half[:], ALU.pow).then_inc(rstd_done, 1)

                def send(G, i, blocks):
                    wait_alone(pool, placed, G + 1, (consts, 11))
                    for n in blocks:
                        for k in range(2):
                            nc.gpsimd.indirect_dma_start(rows, bass.IndirectOffsetOnAxis(place_int[i][:, n, k:k + 1], 0),
                                                         xn[i][:, n, :], None).then_inc(scattered[i], 16)

                def group(G, t, i):
                    first, last = isinstance(G, int) and G == 0, isinstance(G, int) and G == GROUPS - 1
                    if not first:
                        send(G - 1, (i + 2) % 3, range(TB // 2))
                    if not last:
                        rstd_of(G + 1)
                    if not first:
                        send(G - 1, (i + 2) % 3, range(TB // 2, TB))
                        wait_alone(pool, w13_high, G, (consts, 11))
                        e = expert(G - 1)
                        nc.gpsimd.tensor_tensor(w13[1][:, e], w13_raw[:, e], w13[0][:, e].bitcast(F32),
                                                ALU.subtract).then_inc(w13_low, 1)

                rstd_of(0)
                in_groups(pool, GROUPS, group)
                send(GROUPS - 1, (GROUPS - 1) % 3, range(TB))
                pool.wait_ge(pads_placed, 1)
                for e in range(E):
                    nc.gpsimd.indirect_dma_start(rows, bass.IndirectOffsetOnAxis(pad_place[:, e:e + 1], 0),
                                                 pad_rows[:], None).then_inc(padded, 16)

            @block.scalar
            def _(act):
                for e in range(E):
                    act.dma_start(w13_raw[:, e], w_13T[e].rearrange("(k p) f -> p k f", p=P)).then_inc(w13_loaded, 16)

                def highs(G):
                    for j in range(KT):
                        act.wait_ge(xT_filled, KT * G + j + 1)
                        nc.scalar.activation(xT[0][:, j, :], ps_x[j][:], ACT.Copy).then_inc(xT_high, 1)

                def group(G, t, i):
                    act.wait_ge(logits_out, G + 1)
                    nc.scalar.activation(logits_T[:], ps_rT[:], ACT.Copy).then_inc(logits_copied, 1)
                    act.wait_ge(logits_done, G + 1)
                    nc.scalar.activation(ez[:], ps_r[:], ACT.Exp, scale=-1.0).then_inc(ez_done, 1)
                    if not isinstance(G, int) or G < GROUPS - 1:
                        highs(G + 1)
                    if isinstance(G, int) and G == 0:
                        act.wait_ge(w13_loaded, 16 * E)
                    nc.scalar.activation(w13[0][:, expert(G)], w13_raw[:, expert(G)], ACT.Copy).then_inc(w13_high, 1)

                act.wait_ge(small_loaded, 32)
                nc.scalar.activation(wg[0][:], wg_raw[:], ACT.Copy).then_inc(wg_high, 1)
                highs(0)
                in_groups(act, GROUPS, group)

            @block.vector
            def _(dve):
                R = 21

                def normalise(G, t, i):
                    dve.wait_ge(x2_loaded[i], 16 * (t + 1))
                    for n in range(TB):
                        nc.vector.bn_stats(stats[:, n, :], xn[i][:, n, 0:H]).then_inc(stats_done, 1)
                    if not isinstance(G, int) or G:
                        wait_alone(dve, stats_done, TB * (G + 1), (xn_done, 1))
                    else:
                        dve.wait_ge(stats_done, TB)
                    for n in range(TB):
                        nc.vector.bn_aggr(mv[:, n, :], stats[:, n, :]).then_inc(aggr_done, 1)
                    dve.wait_ge(rstd_done, G + 1)
                    for n in range(TB):
                        ins = nc.vector.tensor_scalar(xn[i][:, n, 0:H], xn[i][:, n, 0:H], mv[:, n, 0:1],
                                                      rstd[:, n:n + 1], ALU.subtract, ALU.mult)
                    ins.then_inc(xn_done, 1)

                def route_group(G, i):
                    k = [0]

                    def then(ins):
                        k[0] += 1
                        ins.then_inc(route, 1)
                        dve.wait_ge(route, R * G + k[0])

                    v = nc.vector
                    mine = score[:, :, :, None].to_broadcast([P, TB, E, E])
                    other = score[:, :, None, :].to_broadcast([P, TB, E, E])
                    dve.wait_ge(ez_done, G + 1)
                    then(v.tensor_scalar(ez[:], ez[:], 1.0, None, ALU.add))
                    then(v.reciprocal(sig[:], ez[:]))
                    then(v.tensor_tensor(score[:], sig[:], bias_b[:, None, :].to_broadcast([P, TB, E]), ALU.add))
                    v.tensor_tensor(above[:], other, mine, ALU.is_gt)
                    then(v.tensor_tensor(equal[:], other, mine, ALU.is_equal))
                    then(v.tensor_tensor(equal[:], equal[:], lower[:, None, :, :].to_broadcast([P, TB, E, E]), ALU.mult))
                    then(v.tensor_tensor(above[:], above[:], equal[:], ALU.add))
                    then(v.tensor_reduce(rank[:], above[:], AX.X, ALU.add))
                    v.tensor_scalar(chosen_bf[:, 0:TB, :], rank[:], 1.5, None, ALU.is_lt).then_inc(chosen_done, 1)
                    for r in range(2):
                        v.tensor_scalar(is_rank[:, :, r, :], rank[:], float(r), None, ALU.is_equal)
                    then(v.scalar_tensor_tensor(weight[:], rank[:], 1.5, sig[:], ALU.is_lt, ALU.mult))
                    then(v.tensor_reduce(total[:], weight[:], AX.X, ALU.add))
                    then(v.reciprocal(inv[:], total[:]))
                    then(v.tensor_tensor(weight[:], weight[:], inv[:, :, None].to_broadcast([P, TB, E]), ALU.mult))
                    then(v.tensor_tensor(picked[:], is_rank[:], weight[:, :, None, :].to_broadcast([P, TB, 2, E]), ALU.mult))
                    then(v.tensor_reduce(xn[i][:, :, W0:W1 + 1], picked[:], AX.X, ALU.add))
                    then(v.tensor_tensor(place[:], is_rank[:, :, 0, :], expert_no[:, None, :].to_broadcast([P, TB, E]), ALU.mult))
                    then(v.tensor_reduce(xn[i][:, :, BEST], place[:], AX.X, ALU.add))
                    v.tensor_copy(xn[i][:, :, TOKEN], token[:])
                    dve.wait_ge(counted, G + 1)
                    then(v.tensor_tensor(place[:], ps_c[:, 0:TB, :], next_row[:, None, :].to_broadcast([P, TB, E]), ALU.add))
                    then(v.tensor_tensor(picked[:], is_rank[:], place[:, :, None, :].to_broadcast([P, TB, 2, E]), ALU.mult))
                    then(v.tensor_reduce(place_rank[:], picked[:], AX.X, ALU.add))
                    then(v.tensor_copy(place_int[i][:], place_rank[:]))
                    then(v.tensor_scalar(token[:], token[:], float(GT), None, ALU.add))
                    then(v.tensor_tensor(next_row[:], next_row[:], ps_c[:, TB, :], ALU.add))
                    assert k[0] == R
                    v.tensor_copy(total[:], place_rank[:, :, 0]).then_inc(placed, 1)

                def lows(G):
                    for j in range(KT):
                        dve.wait_ge(xT_high, KT * G + j + 1)
                        nc.vector.tensor_tensor(xT[1][:, j, :], ps_x[j][:], xT[0][:, j, :].bitcast(F32),
                                                ALU.subtract).then_inc(xT_low, 1)

                def group(G, t, i):
                    lows(G)
                    if not isinstance(G, int) or G < GROUPS - 1:
                        normalise(G + 1, t + i // 2, (i + 1) % 3)
                    route_group(G, i)

                normalise(0, 0, 0)
                dve.wait_ge(wg_high, 1)
                nc.vector.tensor_tensor(wg[1][:], wg_raw[:], wg[0][:].bitcast(F32), ALU.subtract).then_inc(wg_low, 1)
                dve.wait_ge(numbers, 4)
                nc.vector.tensor_copy(nums[:], nums_int[:]).then_inc(numbers, 1)
                dve.wait_ge(numbers, 5)
                dve.wait_ge(consts, 11)
                nc.vector.tensor_scalar(region_row[:], expert_no, float(REGION), None, ALU.mult)
                nc.vector.tensor_scalar(next_row[:], expert_no, float(REGION), None, ALU.mult)
                nc.vector.tensor_scalar(pad_rows[:, TOKEN:ROW], token_in_group[:, 0:1], float(T), None, ALU.add)
                nc.vector.tensor_copy(token[:], token_in_group).then_inc(numbers, 1)
                dve.wait_ge(numbers, 6)
                in_groups(dve, GROUPS, group)

                steps = [0]

                def then(ins):
                    steps[0] += 1
                    ins.then_inc(table, 1)
                    dve.wait_ge(table, steps[0])

                v = nc.vector
                v.tensor_tensor(pad_place[:], next_row[:], token_in_group[:, 0:1].to_broadcast([P, E]), ALU.add).then_inc(pads_placed, 1)
                then(v.tensor_tensor(n_rows[:], next_row[:], region_row[:], ALU.subtract))
                then(v.tensor_tensor(more_rows[:], n_rows[:, :, None].to_broadcast([P, E, STEPS]),
                                     times_128[:, None, :].to_broadcast([P, E, STEPS]), ALU.is_gt))
                v.memset(first_tile[:, 0:1], 0.0)
                then(v.tensor_reduce(n_tiles[:], more_rows[:], AX.X, ALU.add))
                for e in range(E):
                    then(v.tensor_tensor(first_tile[:, e + 1:e + 2], first_tile[:, e:e + 1], n_tiles[:, e:e + 1], ALU.add))
                then(v.tensor_tensor(started[:], tile_no[:, :, None].to_broadcast([P, TILES, E - 1]),
                                     first_tile[:, None, 1:E].to_broadcast([P, TILES, E - 1]), ALU.is_ge))
                then(v.tensor_reduce(tile_expert[:], started[:], AX.X, ALU.add))
                then(v.tensor_tensor(started[:], started[:], n_tiles[:, None, 0:E - 1].to_broadcast([P, TILES, E - 1]), ALU.mult))
                then(v.tensor_reduce(tile_first[:], started[:], AX.X, ALU.add))
                v.tensor_copy(tile_expert_int[:], tile_expert[:])
                v.tensor_scalar(tile_used[:], tile_no, first_tile[:, E:E + 1], None, ALU.is_lt)
                then(v.tensor_tensor(tile_first[:], tile_no, tile_first[:], ALU.subtract))
                then(v.tensor_scalar(tile_row[:], tile_expert[:], float(REGION), -float(PAD_ROW), ALU.mult, ALU.add))
                then(v.scalar_tensor_tensor(tile_row[:], tile_first[:], float(P), tile_row[:], ALU.mult, ALU.add))
                then(v.tensor_tensor(tile_row[:], tile_row[:], tile_used[:], ALU.mult))
                then(v.tensor_scalar(tile_row_int[:], tile_row[:], float(PAD_ROW), None, ALU.add))
                dve.wait_ge(w13_high, E)
                v.tensor_tensor(w13[1][:, E - 1], w13_raw[:, E - 1], w13[0][:, E - 1].bitcast(F32),
                                ALU.subtract).then_inc(w13_low, 1)
                dve.wait_ge(w13_low, E)

            @block.tensor
            def _(pe):
                def transposes(G, i):
                    pe.wait_ge(xn_done, G + 1)
                    for j in range(KT):
                        for n in range(TB):
                            ins = nc.tensor.transpose(ps_x[j][:, n * P:(n + 1) * P], xn[i][:, n, j * P:(j + 1) * P], ident[:])
                        ins.then_inc(xT_filled, 1)

                def group(G, t, i):
                    pe.wait_ge(xT_low, KT * (G + 1))
                    for j in range(KT):
                        for m, (a, c) in enumerate(PASSES):
                            ins = nc.tensor.matmul(ps_rT[:], wg[a][:, j, :], xT[c][:, j, :],
                                                   start=(j == 0 and m == 0), stop=(j == KT - 1 and m == 2))
                    ins.then_inc(logits_out, 1)
                    wait_alone(pe, logits_copied, G + 1, (consts, 11))
                    for b in range(TB):
                        ins = nc.tensor.transpose(ps_r[:, b, :], logits_T[:, b * P:(b + 1) * P], ident[0:E, 0:E])
                    ins.then_inc(logits_done, 1)
                    if not isinstance(G, int) or G < GROUPS - 1:
                        transposes(G + 1, (i + 1) % 3)
                    pe.wait_ge(chosen_done, G + 1)
                    nc.tensor.matmul(ps_c[:], before_bf[:], chosen_bf[:], start=True, stop=False)
                    for s in range(1, TB + 1):
                        ins = nc.tensor.matmul(ps_c[:, s:, :], ones_bf[:], chosen_bf[:, 0:TB + 1 - s, :],
                                               start=False, stop=(s == TB))
                    ins.then_inc(counted, 1)

                pe.wait_ge(consts, 11)
                transposes(0, 0)
                pe.wait_ge(wg_low, 1)
                in_groups(pe, GROUPS, group)


def run_experts(nc, rows, out, w13, w2, ident, tile_expert, tile_expert_int, tile_row_int,
                KT, FT, FF, H, E, W0, W1, BEST, TOKEN, ROW, TILES, PASSES):
    LAST_ROW = rows.shape[0] - P
    with ExitStack() as ctx:
        def sb(name, shape, dt=F32):
            return ctx.enter_context(nc.sbuf_tensor("e_" + name, shape, dt))

        def psum(name, shape):
            return ctx.enter_context(nc.psum_tensor("e_" + name, shape, F32))

        def sem(name):
            return ctx.enter_context(nc.semaphore("e_" + name))

        row = [sb(f"row{i}", [P, ROW]) for i in range(2)]
        xT = [sb(f"xT_{s}", [P, KT, P], F32R) for s in "hl"]
        gate = sb("gate", [P, FF])
        g = sb("g", [P, FF])
        gT = sb("gT", [P, FT, P])
        y = [sb(f"y{i}", [P, H]) for i in range(2)]
        is_best = sb("is_best", [P, 1])
        not_best = sb("not_best", [P, 1])
        best_weight = sb("best_weight", [P, 1])
        weight = [sb(f"weight{i}", [P, 1]) for i in range(2)]
        place = [sb(f"place{i}", [P, 1]) for i in range(2)]
        place_int = [sb(f"place_int{i}", [P, 1], I32) for i in range(2)]
        ps_x = [psum(f"ps_x{i}", [P, KT, P]) for i in range(2)]
        ps_h = [psum(f"ps_h{i}", [P, 2 * FF]) for i in range(2)]
        ps_g = psum("ps_g", [P, FT, P])
        ps_y = [psum(f"ps_y{i}", [P, H]) for i in range(2)]

        row_loaded = [sem(f"row_loaded{i}") for i in range(2)]
        x_transposed = sem("x_transposed")
        x_high = sem("x_high")
        x_low = sem("x_low")
        h_filled = sem("h_filled")
        gate_done = sem("gate_done")
        g_done = sem("g_done")
        g_transposed = sem("g_transposed")
        gT_done = sem("gT_done")
        y_filled = sem("y_filled")
        y_copied = sem("y_copied")
        y_out = sem("y_out")
        which = sem("which")
        meta_done = sem("meta_done")
        place_done = sem("place_done")

        with nc.Block() as block:
            @block.sync
            def _(sp):
                def tile(u, t, i):
                    if not isinstance(u, int) or u >= 2:
                        wait_alone(sp, meta_done, u - 1, (row_loaded[0], 16))
                    r = sp.value_load(tile_row_int[0:1, u:u + 1] if isinstance(u, int) else tile_row_int[0:1, bass.ds(u, 1)],
                                      min_val=0, max_val=LAST_ROW)
                    sp.dma_start(row[i][:], rows[bass.ds(r, P), :]).then_inc(row_loaded[i], 16)

                in_steps(sp, TILES, tile, last=1)

            @block.gpsimd
            def _(pool):
                def add_to_tokens(u, i):
                    wait_alone(pool, y_copied, u + 2, (y_copied, 1))
                    if not isinstance(u, int) or u:
                        wait_alone(pool, y_out, 16 * u, (y_copied, 1))
                    nc.gpsimd.indirect_dma_start(out, bass.IndirectOffsetOnAxis(place_int[i][:], 0), y[i][:], None,
                                                 compute_op=ALU.add).then_inc(y_out, 16)

                def tile(u, t, i):
                    if not isinstance(u, int) or u:
                        add_to_tokens(u - 1, 1 - i)

                in_steps(pool, TILES, tile, first=4, last=3)
                add_to_tokens(TILES - 1, (TILES - 1) % 2)
                pool.wait_ge(y_out, 16 * TILES)

            @block.scalar
            def _(act):
                def high(u, i):
                    act.wait_ge(x_transposed, u + 1)
                    nc.scalar.activation(xT[0][:], ps_x[i][:], ACT.Copy).then_inc(x_high, 1)

                def gT_copy(u):
                    act.wait_ge(g_transposed, u + 1)
                    nc.scalar.activation(gT[:], ps_g[:], ACT.Copy).then_inc(gT_done, 1)

                def tile(u, t, i):
                    if not isinstance(u, int) or u:
                        gT_copy(u - 1)
                    if not isinstance(u, int) or u < TILES - 1:
                        high(u + 1, 1 - i)
                    act.wait_ge(h_filled, u + 1)
                    nc.scalar.activation(gate[:], ps_h[i][:, 0:FF], ACT.Silu).then_inc(gate_done, 1)

                high(0, 0)
                in_steps(act, TILES, tile, last=3)
                gT_copy(TILES - 1)

            @block.vector
            def _(dve):
                S = 3

                def low(u, i):
                    dve.wait_ge(x_high, u + 1)
                    nc.vector.tensor_tensor(xT[1][:], ps_x[i][:], xT[0][:].bitcast(F32), ALU.subtract).then_inc(x_low, 1)

                def meta(u, t, i):
                    expert = tile_expert[:, u:u + 1] if isinstance(u, int) else tile_expert[:, bass.ds(u, 1)]
                    v = nc.vector
                    dve.wait_ge(row_loaded[i], 16 * (t + 1))
                    v.tensor_tensor(is_best[:], row[i][:, BEST:BEST + 1], expert, ALU.is_equal).then_inc(which, 1)
                    v.tensor_tensor(not_best[:], row[i][:, BEST:BEST + 1], expert, ALU.not_equal).then_inc(which, 1)
                    dve.wait_ge(which, S * u + 2)
                    v.tensor_tensor(best_weight[:], row[i][:, W0:W0 + 1], is_best[:], ALU.mult).then_inc(which, 1)
                    v.tensor_copy(place[i][:], row[i][:, TOKEN:TOKEN + 1])
                    dve.wait_ge(which, S * u + 3)
                    v.scalar_tensor_tensor(weight[i][:], row[i][:, W1:W1 + 1], not_best[:], best_weight[:],
                                           ALU.mult, ALU.add).then_inc(meta_done, 1)

                def y_copy(u, i):
                    if not isinstance(u, int) or u >= 2:
                        dve.wait_ge(y_out, 16 * (u - 1))
                    nc.vector.tensor_copy(place_int[i][:], place[i][:]).then_inc(place_done, 1)
                    dve.wait_ge(y_filled, u + 1)
                    nc.vector.tensor_copy(y[i][:], ps_y[i][:]).then_inc(y_copied, 1)

                def tile(u, t, i):
                    if not isinstance(u, int) or u < TILES - 1:
                        low(u + 1, 1 - i)
                    dve.wait_ge(gate_done, u + 1)
                    dve.wait_ge(meta_done, u + 1)
                    nc.vector.scalar_tensor_tensor(g[:], ps_h[i][:, FF:], weight[i][:], gate[:], ALU.mult,
                                                   ALU.mult).then_inc(g_done, 1)
                    if not isinstance(u, int) or u:
                        y_copy(u - 1, 1 - i)
                        dve.wait_ge(place_done, u)
                    if not isinstance(u, int) or u < TILES - 1:
                        meta(u + 1, t + i, 1 - i)

                dve.sem_inc(y_copied, 1)
                low(0, 0)
                meta(0, 0, 0)
                in_steps(dve, TILES, tile, first=4, last=3)
                y_copy(TILES - 1, (TILES - 1) % 2)

            @block.tensor
            def _(pe):
                def transposes(u, t, i):
                    pe.wait_ge(row_loaded[i], 16 * (t + 1))
                    for j in range(KT):
                        ins = nc.tensor.transpose(ps_x[i][:, j, :], row[i][:, j * P:(j + 1) * P], ident[:])
                    ins.then_inc(x_transposed, 1)

                def g_transposes(u):
                    pe.wait_ge(g_done, u + 1)
                    for f in range(FT):
                        ins = nc.tensor.transpose(ps_g[:, f, :], g[:, f * P:(f + 1) * P], ident[:])
                    ins.then_inc(g_transposed, 1)

                def down(u, i, e):
                    pe.wait_ge(gT_done, u + 1)
                    if not isinstance(u, int) or u >= 2:
                        pe.wait_ge(y_copied, u)
                    for f in range(FT):
                        w = w2[:, e, f, :] if isinstance(e, int) else w2[:, bass.ds(e, 1), f, :].rearrange("p o h -> p (o h)")
                        ins = nc.tensor.matmul(ps_y[i][:], gT[:, f, :], w, start=(f == 0), stop=(f == FT - 1))
                    ins.then_inc(y_filled, 1)

                def expert_of(u):
                    at = tile_expert_int[0:1, u:u + 1] if isinstance(u, int) else tile_expert_int[0:1, bass.ds(u, 1)]
                    return pe.value_load(at, min_val=0, max_val=E - 1)

                def tile(u, t, i):
                    first = isinstance(u, int) and u == 0
                    e = expert_of(u)
                    e_before = None if first else expert_of(u - 1)
                    pe.wait_ge(x_low, u + 1)
                    m = 0
                    for j in range(KT):
                        for a, c in PASSES:
                            if m == 9 and not first:
                                g_transposes(u - 1)
                            ins = nc.tensor.matmul(ps_h[i][:], xT[a][:, j, :],
                                                   w13[c][:, bass.ds(e, 1), j, :].rearrange("p o f -> p (o f)"),
                                                   start=(m == 0), stop=(m == 3 * KT - 1))
                            m += 1
                    ins.then_inc(h_filled, 1)
                    if not isinstance(u, int) or u < TILES - 1:
                        transposes(u + 1, t + i, 1 - i)
                    if not first:
                        down(u - 1, 1 - i, e_before)

                transposes(0, 0, 0)
                in_steps(pe, TILES, tile, last=3)
                g_transposes(TILES - 1)
                down(TILES - 1, (TILES - 1) % 2, expert_of(TILES - 1))


def decoder_layer(nc, x, context, mask, mask_cols, a_wq, a_wkv, a_wd, x_wq, x_bq, x_wk, x_bk, x_wv, x_bv,
                  f_wg, f_w13, f_w2, f_bias, out):
    B, S, H = x.shape
    GROUPS = 4
    HEADS = a_wq.shape[1] // P
    x1 = nc.dram_tensor("x1", [B, S, H], F32, kind="Internal").ap()
    x2 = out[0:B * S].rearrange("(b s) h -> b s h", s=S)
    aux = nc.dram_tensor("mask_rows_split", [B, 6, 2, H], F32, kind="Internal").ap()
    rinv = nc.dram_tensor("row_sum_inverses", [4, 4 * H], F32, kind="Internal").ap()

    def by_512(t):
        return t.rearrange("(g b) s h -> g (b s) h", b=BANK // S)

    attention_phase(nc, by_512(x), a_wq, a_wkv, a_wd, by_512(x1), B * S, H, S, HEADS, GROUPS)
    cross_attention_phase(nc, x1, context, mask, mask_cols, x_wq, x_bq, x_wk, x_bk, x_wv, x_bv, aux, rinv, x2)
    experts_phase(nc, out, f_wg, f_w13, f_w2, f_bias, *experts_scratch(nc))


def kernel(**inputs):
    import numpy as np
    import concourse.bacc as bacc
    from concourse.bass_utils import run_bass_kernel_spmd

    a = {name: np.asarray(value) for name, value in inputs.items()}
    B, S, H = a["x"].shape
    C = a["L0_xattn_Wq"].shape[0]
    mask = a["mask_Bx1x2048_fk1"].reshape(B, H)

    def by_quads(w):
        return w.reshape(4, 4, 16, -1).transpose(0, 2, 1, 3).reshape(C, -1)

    laid = {
        "x": a["x"],
        "context": a["ctx_2048"],
        "mask": mask,
        "mask_cols": mask.reshape(B, H // 128, 128).transpose(0, 2, 1),
        "a_wq": a["L0_attn_w_q"],
        "a_wkv": a["L0_attn_w_kv"],
        "a_wd": a["L0_attn_w_dense"],
        "x_wq": by_quads(a["L0_xattn_Wq"]).T,
        "x_bq": by_quads(a["L0_xattn_bq"]).reshape(C // 128, 128).T,
        "x_wk": by_quads(a["L0_xattn_Wk"]).T,
        "x_bk": by_quads(a["L0_xattn_bk"]).reshape(C // 128, 128).T,
        "x_wv": a["L0_xattn_Wv"].T,
        "x_bv": a["L0_xattn_bv"].reshape(1, C),
        "f_wg": a["L0_ffn_Wg"].T,
        "f_w13": np.concatenate([a["L0_ffn_W1"], a["L0_ffn_W3"]], axis=1).transpose(0, 2, 1),
        "f_w2": a["L0_ffn_W2"].transpose(0, 2, 1),
        "f_bias": a["L0_ffn_bias"].reshape(1, -1),
    }
    nc = bacc.Bacc("TRN2", target_bir_lowering=False, num_devices=1)
    arrays = {f"in_{name}": np.ascontiguousarray(value) for name, value in laid.items()}
    args = [nc.dram_tensor(f"in_{name}", list(arrays[f"in_{name}"].shape), F32, kind="ExternalInput").ap() for name in laid]
    out = nc.dram_tensor("out", [B * S + P, H], F32, kind="ExternalOutput").ap()
    decoder_layer(nc, *args, out)
    r = run_bass_kernel_spmd(nc, [arrays], core_ids=[0])
    return r.results[0]["out"][0:B * S].reshape(B, S, H)
```
